# Optimizing a Trainium2 kernel written in Bass

```python
import numpy as np
import jax
import jax.numpy as jnp

def _softmax(x, axis=-1):
    return jax.nn.softmax(x, axis=axis)

def _gelu(x):
    return jax.nn.gelu(x, approximate=True)

def _silu(x):
    return jax.nn.silu(x)

def _sigmoid(x):
    return jax.nn.sigmoid(x)

def _layernorm(x, axis=-1, eps=1e-05):
    m = jnp.mean(x, axis=axis, keepdims=True)
    v = jnp.var(x, axis=axis, keepdims=True)
    return (x - m) / jnp.sqrt(v + eps)

def _scatter_add(tgt, idx, src, axis=0):
    return tgt.at[idx].add(src)

def _segment_sum(src, seg, n):
    return jax.ops.segment_sum(src, seg, n)
kernel_name = 'mk_xattn_ffn_d2_seqx_r4_0c3b82'

def setup_inputs(seed: int=0):
    np.random.seed(seed)
    _w = jnp.asarray

    def _rec_inputs():
        import jax
        import jax.numpy as jnp
        _rk = jax.random.key(seed)
        x = 7.22e-05 + 1 * jax.random.normal(jax.random.fold_in(_rk, 1), (1, 2048, 256), jnp.float32)
        _lenS = 2048 - jax.random.randint(jax.random.fold_in(_rk, 7), (1,), 0, max(1, 2048 // 4) + 1, jnp.int32)
        _lenS2 = 1601 - jax.random.randint(jax.random.fold_in(_rk, 8), (1,), 0, max(1, 1601 // 4) + 1, jnp.int32)
        _ctx_1024P = jax.random.normal(jax.random.fold_in(_rk, 11), (1, 16, 256), jnp.float32)
        _ctx_1024c = jax.random.dirichlet(jax.random.fold_in(_rk, 511), 0.3 * jnp.ones((16,), jnp.float32), (1, 1601))
        _ctx_1024t = jnp.einsum('bsk,bkd->bsd', _ctx_1024c, _ctx_1024P)
        _ctx_1024t = _ctx_1024t * jax.lax.rsqrt(jnp.mean(jnp.square(_ctx_1024t)) + 1e-12) * 0.953939
        ctx_1024 = 4.13588e-05 + 0.999923 * (_ctx_1024t + 0.3 * jax.random.normal(jax.random.fold_in(_rk, 611), (1, 1601, 256), jnp.float32))
        _validS = jnp.arange(2048)[None, :] < _lenS[:, None]
        _validS2 = jnp.arange(1601)[None, :] < _lenS2[:, None]
        _causal = jnp.tril(jnp.ones((2048, 2048), dtype=bool))
        mask_BxS2_bf1 = jnp.ones((1, 1601), dtype=bool)
        return (x, ctx_1024, mask_BxS2_bf1)
    x, ctx_1024, mask_BxS2_bf1 = _rec_inputs()

    def _L0_xattn_setup():
        import jax, jax.numpy as jnp
        import numpy as np
        B, SQ, SKV, E, H = (4, 512, 512, 256, 16)
        HD = E // H

        def stablemax(x):
            s = jnp.where(x >= 0, x + 1.0, 1.0 / (1.0 - x))
            return s / jnp.sum(s, axis=-1, keepdims=True)
        key = jax.random.key(seed)
        ks = jax.random.split(key, 6)
        scale = 1.0 / np.sqrt(E)
        return {'query': jax.random.normal(ks[0], (B, SQ, E), jnp.float32), 'key_value': jax.random.normal(ks[1], (B, SKV, E), jnp.float32), 'Wq': jax.random.normal(ks[2], (E, E), jnp.float32) * scale, 'bq': jnp.zeros((E,), jnp.float32), 'Wk': jax.random.normal(ks[3], (E, E), jnp.float32) * scale, 'bk': jnp.zeros((E,), jnp.float32), 'Wv': jax.random.normal(ks[4], (E, E), jnp.float32) * scale, 'bv': jnp.zeros((E,), jnp.float32), 'Wo': jax.random.normal(ks[5], (E, E), jnp.float32) * scale, 'bo': jnp.zeros((E,), jnp.float32)}
    _L0_xattn_all = _L0_xattn_setup()
    _L0_xattn_in = {k: v for k, v in _L0_xattn_all.items() if k in ('Wq', 'bq', 'Wk', 'bk', 'Wv', 'bv', 'Wo', 'bo')}
    del _L0_xattn_all

    def _L0_ffn_setup():
        import jax, jax.numpy as jnp
        import numpy as np
        B, S, DIM, FFN, E = (4, 512, 256, 1024, 8)
        key = jax.random.key(seed)
        k0, k1, k2, k3 = jax.random.split(key, 4)
        scale = 0.02
        return {'hidden_states': jax.random.normal(k0, (B, S, DIM), jnp.float32), 'router_w': jax.random.normal(k1, (DIM, E), jnp.float32) * scale, 'router_b': jnp.zeros((E,), jnp.float32), 'w1': jax.random.normal(k2, (E, DIM, 2 * FFN), jnp.float32) * scale, 'w2': jax.random.normal(k3, (E, FFN, DIM), jnp.float32) * scale}
    _L0_ffn_all = _L0_ffn_setup()
    _L0_ffn_in = {k: v for k, v in _L0_ffn_all.items() if k in ('router_w', 'router_b', 'w1', 'w2')}
    del _L0_ffn_all

    def _L1_xattn_setup():
        import jax, jax.numpy as jnp
        import numpy as np
        N_HEADS = 16
        D_MODEL = 256
        HEAD_DIM = D_MODEL // N_HEADS
        MASK_FILL = -100000000.0

        def _split_heads(x):
            B, S, _ = x.shape
            return x.reshape(B, S, N_HEADS, HEAD_DIM).transpose(0, 2, 1, 3)
        key = jax.random.key(seed)
        ks = jax.random.split(key, 12)
        B, L, P = (2, 512, 512)
        s = 1.0 / np.sqrt(D_MODEL).astype(np.float32)
        inp = {'q': jax.random.normal(ks[0], (B, L, D_MODEL), dtype=jnp.float32), 'k': jax.random.normal(ks[1], (B, P, D_MODEL), dtype=jnp.float32), 'v': jax.random.normal(ks[2], (B, P, D_MODEL), dtype=jnp.float32), 'attention_mask': jnp.ones((B, P), dtype=bool), 'Wq': jax.random.normal(ks[3], (D_MODEL, D_MODEL), dtype=jnp.float32) * s, 'bq': jnp.zeros((D_MODEL,), dtype=jnp.float32), 'Wk': jax.random.normal(ks[4], (D_MODEL, D_MODEL), dtype=jnp.float32) * s, 'bk': jnp.zeros((D_MODEL,), dtype=jnp.float32), 'Wv': jax.random.normal(ks[5], (D_MODEL, D_MODEL), dtype=jnp.float32) * s, 'bv': jnp.zeros((D_MODEL,), dtype=jnp.float32), 'Wo': jax.random.normal(ks[6], (D_MODEL, D_MODEL), dtype=jnp.float32) * s, 'bo': jnp.zeros((D_MODEL,), dtype=jnp.float32)}
        return inp
    _L1_xattn_all = _L1_xattn_setup()
    _L1_xattn_in = {k: v for k, v in _L1_xattn_all.items() if k in ('Wq', 'bq', 'Wk', 'bk', 'Wv', 'bv', 'Wo', 'bo')}
    del _L1_xattn_all

    def _L1_ffn_setup():
        import jax, jax.numpy as jnp
        import numpy as np
        B, S, D, E, H, DO = (4, 512, 256, 8, 1024, 256)
        TOP_K = 2
        LN_EPS = 1e-05
        key = jax.random.key(seed)
        ks = jax.random.split(key, 9)
        s = 0.02
        return {'x': jax.random.normal(ks[0], (B, S, D), dtype=jnp.float32), 'W1': jax.random.normal(ks[1], (E, D, H), dtype=jnp.float32) * s, 'b1': jnp.zeros((E, H), dtype=jnp.float32), 'W2': jax.random.normal(ks[2], (E, H, DO), dtype=jnp.float32) * s, 'b2': jnp.zeros((E, DO), dtype=jnp.float32), 'gate_W': jax.random.normal(ks[3], (D, E), dtype=jnp.float32) * s, 'shared_W': jax.random.normal(ks[4], (D, DO), dtype=jnp.float32) * s, 'shared_b': jnp.zeros((DO,), dtype=jnp.float32), 'gamma': jnp.ones((DO,), dtype=jnp.float32), 'beta': jnp.zeros((DO,), dtype=jnp.float32)}
    _L1_ffn_all = _L1_ffn_setup()
    _L1_ffn_in = {k: v for k, v in _L1_ffn_all.items() if k in ('W1', 'b1', 'W2', 'b2', 'gate_W', 'shared_W', 'shared_b', 'gamma', 'beta')}
    del _L1_ffn_all
    return {'x': x, 'ctx_1024': ctx_1024, 'mask_BxS2_bf1': mask_BxS2_bf1, 'L0_xattn_Wq': _L0_xattn_in['Wq'], 'L0_xattn_bq': _L0_xattn_in['bq'], 'L0_xattn_Wk': _L0_xattn_in['Wk'], 'L0_xattn_bk': _L0_xattn_in['bk'], 'L0_xattn_Wv': _L0_xattn_in['Wv'], 'L0_xattn_bv': _L0_xattn_in['bv'], 'L0_xattn_Wo': _L0_xattn_in['Wo'], 'L0_xattn_bo': _L0_xattn_in['bo'], 'L0_ffn_router_w': _L0_ffn_in['router_w'], 'L0_ffn_router_b': _L0_ffn_in['router_b'], 'L0_ffn_w1': _L0_ffn_in['w1'], 'L0_ffn_w2': _L0_ffn_in['w2'], 'L1_xattn_Wq': _L1_xattn_in['Wq'], 'L1_xattn_bq': _L1_xattn_in['bq'], 'L1_xattn_Wk': _L1_xattn_in['Wk'], 'L1_xattn_bk': _L1_xattn_in['bk'], 'L1_xattn_Wv': _L1_xattn_in['Wv'], 'L1_xattn_bv': _L1_xattn_in['bv'], 'L1_xattn_Wo': _L1_xattn_in['Wo'], 'L1_xattn_bo': _L1_xattn_in['bo'], 'L1_ffn_W1': _L1_ffn_in['W1'], 'L1_ffn_b1': _L1_ffn_in['b1'], 'L1_ffn_W2': _L1_ffn_in['W2'], 'L1_ffn_b2': _L1_ffn_in['b2'], 'L1_ffn_gate_W': _L1_ffn_in['gate_W'], 'L1_ffn_shared_W': _L1_ffn_in['shared_W'], 'L1_ffn_shared_b': _L1_ffn_in['shared_b'], 'L1_ffn_gamma': _L1_ffn_in['gamma'], 'L1_ffn_beta': _L1_ffn_in['beta']}

def reference(x, ctx_1024, mask_BxS2_bf1, L0_xattn_Wq, L0_xattn_bq, L0_xattn_Wk, L0_xattn_bk, L0_xattn_Wv, L0_xattn_bv, L0_xattn_Wo, L0_xattn_bo, L0_ffn_router_w, L0_ffn_router_b, L0_ffn_w1, L0_ffn_w2, L1_xattn_Wq, L1_xattn_bq, L1_xattn_Wk, L1_xattn_bk, L1_xattn_Wv, L1_xattn_bv, L1_xattn_Wo, L1_xattn_bo, L1_ffn_W1, L1_ffn_b1, L1_ffn_W2, L1_ffn_b2, L1_ffn_gate_W, L1_ffn_shared_W, L1_ffn_shared_b, L1_ffn_gamma, L1_ffn_beta):
    import jax
    import jax.numpy as jnp

    def _L0_xattn_ref(query, key_value, Wq, bq, Wk, bk, Wv, bv, Wo, bo):
        import jax, jax.numpy as jnp
        import numpy as np
        B, SQ, SKV, E, H = (4, 512, 512, 256, 16)
        HD = E // H

        def stablemax(x):
            s = jnp.where(x >= 0, x + 1.0, 1.0 / (1.0 - x))
            return s / jnp.sum(s, axis=-1, keepdims=True)
        b = query.shape[0]
        q = query @ Wq.T + bq
        k = key_value @ Wk.T + bk
        v = key_value @ Wv.T + bv
        q = q.reshape(b, -1, H, HD).transpose(0, 2, 1, 3)
        k = k.reshape(b, -1, H, HD).transpose(0, 2, 1, 3)
        v = v.reshape(b, -1, H, HD).transpose(0, 2, 1, 3)
        scores = jnp.einsum('bhqd,bhkd->bhqk', q, k) / np.sqrt(HD).astype(np.float32)
        attn = stablemax(scores)
        context = jnp.einsum('bhqk,bhkd->bhqd', attn, v)
        context = context.transpose(0, 2, 1, 3).reshape(b, -1, E)
        return context @ Wo.T + bo

    def _L0_ffn_ref(hidden_states, router_w, router_b, w1, w2):
        import jax, jax.numpy as jnp
        import numpy as np
        B, S, DIM, FFN, E = (4, 512, 256, 1024, 8)
        b, s, d = hidden_states.shape
        x = hidden_states.reshape(-1, d)
        logits = x @ router_w + router_b
        route = jax.nn.softmax(logits, axis=1)
        max_prob = jnp.max(route, axis=1, keepdims=True)
        max_ind = jnp.argmax(route, axis=1)
        out = jnp.zeros_like(x)
        num_experts = w1.shape[0]
        for e in range(num_experts):
            h = x @ w1[e]
            a, g = jnp.split(h, 2, axis=1)
            y = jax.nn.silu(a) * g @ w2[e]
            out = jnp.where((max_ind == e)[:, None], y, out)
        out = out * max_prob
        return out.reshape(b, s, d)

    def _L1_xattn_ref(q, k, v, attention_mask, Wq, bq, Wk, bk, Wv, bv, Wo, bo):
        import jax, jax.numpy as jnp
        import numpy as np
        N_HEADS = 16
        D_MODEL = 256
        HEAD_DIM = D_MODEL // N_HEADS
        MASK_FILL = -100000000.0

        def _split_heads(x):
            B, S, _ = x.shape
            return x.reshape(B, S, N_HEADS, HEAD_DIM).transpose(0, 2, 1, 3)
        qm = _split_heads(q @ Wq.T + bq)
        km = _split_heads(k @ Wk.T + bk)
        vm = _split_heads(v @ Wv.T + bv)
        scores = jnp.einsum('bnlh,bnph->bnlp', qm, km) / np.sqrt(HEAD_DIM).astype(np.float32)
        mask = attention_mask[:, None, None, :]
        scores = jnp.where(mask, scores, MASK_FILL)
        attn = jax.nn.softmax(scores, axis=-1)
        out = jnp.einsum('bnlp,bnph->bnlh', attn, vm)
        B, _, L, _ = out.shape
        out = out.transpose(0, 2, 1, 3).reshape(B, L, D_MODEL)
        return out @ Wo.T + bo

    def _L1_ffn_ref(x, W1, b1, W2, b2, gate_W, shared_W, shared_b, gamma, beta):
        import jax, jax.numpy as jnp
        import numpy as np
        B, S, D, E, H, DO = (4, 512, 256, 8, 1024, 256)
        TOP_K = 2
        LN_EPS = 1e-05
        d = x.shape[-1]
        flat = x.reshape(-1, d)
        n_exp = gate_W.shape[-1]
        probs = jax.nn.softmax(flat @ gate_W, axis=-1)
        topk_w, topk_idx = jax.lax.top_k(probs, TOP_K)
        topk_w = topk_w / topk_w.sum(axis=-1, keepdims=True)
        combine = (jax.nn.one_hot(topk_idx, n_exp, dtype=flat.dtype) * topk_w[..., None]).sum(axis=1)
        out = 0.5 * jax.nn.gelu(flat @ shared_W + shared_b, approximate=False)
        for e in range(n_exp):
            h = jax.nn.gelu(flat @ W1[e] + b1[e], approximate=False)
            out = out + combine[:, e:e + 1] * (h @ W2[e] + b2[e])
        mean = out.mean(axis=-1, keepdims=True)
        var = ((out - mean) ** 2).mean(axis=-1, keepdims=True)
        out = (out - mean) * jax.lax.rsqrt(var + LN_EPS) * gamma + beta
        return out.reshape(*x.shape[:-1], out.shape[-1])
    x = x + _L0_xattn_ref(_layernorm(x, axis=-1), ctx_1024, L0_xattn_Wq, L0_xattn_bq, L0_xattn_Wk, L0_xattn_bk, L0_xattn_Wv, L0_xattn_bv, L0_xattn_Wo, L0_xattn_bo)
    x = x + _L0_ffn_ref(_layernorm(x, axis=-1), L0_ffn_router_w, L0_ffn_router_b, L0_ffn_w1, L0_ffn_w2)
    x = x + _L1_xattn_ref(_layernorm(x, axis=-1), ctx_1024, ctx_1024, mask_BxS2_bf1, L1_xattn_Wq, L1_xattn_bq, L1_xattn_Wk, L1_xattn_bk, L1_xattn_Wv, L1_xattn_bv, L1_xattn_Wo, L1_xattn_bo)
    x = x + _L1_ffn_ref(_layernorm(x, axis=-1), L1_ffn_W1, L1_ffn_b1, L1_ffn_W2, L1_ffn_b2, L1_ffn_gate_W, L1_ffn_shared_W, L1_ffn_shared_b, L1_ffn_gamma, L1_ffn_beta)
    return x

_drawn_inputs = setup_inputs


def setup_inputs(seed=0):
    import zlib

    import numpy as np

    out = dict(_drawn_inputs(seed))
    spreads = {'L0_xattn_bq': (0.0, 0.1),
     'L0_xattn_bk': (0.0, 0.436),
     'L0_xattn_bv': (0.0, 0.1),
     'L0_xattn_bo': (0.0, 0.1),
     'L0_ffn_router_b': (0.0, 1.692),
     'L1_xattn_bq': (0.0, 0.1),
     'L1_xattn_bk': (0.0, 2.0),
     'L1_xattn_bv': (0.0, 0.1),
     'L1_xattn_bo': (0.0, 0.1),
     'L1_ffn_b1': (0.0, 0.1),
     'L1_ffn_b2': (0.0, 0.1),
     'L1_ffn_shared_b': (0.0, 0.1),
     'L1_ffn_gamma': (1.0, 0.2),
     'L1_ffn_beta': (0.0, 0.1)}
    factors = {'L0_ffn_router_w': 3.048}
    for name, (base, spread) in spreads.items():
        noise = np.random.default_rng([zlib.crc32(name.encode()), seed]).standard_normal(out[name].shape)
        drawn = base * np.exp(spread * noise) if base else spread * noise
        out[name] = jnp.asarray(drawn.astype(out[name].dtype))
    for name, factor in factors.items():
        out[name] = (out[name] * factor).astype(out[name].dtype)
    return out
```

```python
import concourse.bass as bass
from concourse import mybir
from contextlib import ExitStack

fp32 = mybir.dt.float32
bf16 = mybir.dt.bfloat16
i32 = mybir.dt.int32
u32 = mybir.dt.uint32
u8 = mybir.dt.uint8
ALU = mybir.AluOpType
ACT = mybir.ActivationFunctionType
AX = mybir.AxisListType

LN_EXP = "natural_log_exp_and_others"
P = 128
S = 2048
SK = 1601
D = 256
DC = D // P
H = 16
HD = D // H
E = 8
HID = 1024
MC = HID // P
EPS = 1e-5
FILL = -1e8

QC = 512
NCH = S // QC
TC = QC // P
NT = S // P
G = 4
HG = H // G
KT = (SK + P - 1) // P
KROWS = [min(P, SK - P * k) for k in range(KT)]
SKP = KT * P
KCOLS = [(n, min(512, SK - n)) for n in range(0, SK, 512)]

QPART = [0, 0, 0, 1, 1, 2]
KPART = [0, 1, 2, 0, 1, 0]
NB = len(QPART)
ROW_MASK = NB * HD
ROW_MAX = ROW_MASK + 3
ROWS_ALL = ROW_MAX + 3

U = HG * KT
UC = G * U
NW = 12
NS0 = 3
NS1 = 3
PC2 = UC // 2
CLIP = 200


def routing(top):
    na = NT * top
    nt = na + E - 1
    return na, nt + nt % 2


STATS = TC + 6


class Buffers:
    pass


def build(nc, io, stop=99):
    b = Buffers()
    ctx = ExitStack()
    with ctx:
        def sb(name, shape, dt=fp32):
            return ctx.enter_context(nc.sbuf_tensor(name, shape, dt))

        layer_sems = []

        def sem(name):
            layer_sems.append(nc.alloc_semaphore(name=name))
            return layer_sems[-1]

        b.sem = sem
        b.x = sb("x_res", [P, NT, D])
        b.ident = sb("ident", [P, P])
        b.identb = sb("identb", [P, P], bf16)
        b.tri = sb("tri", [P, P])
        b.ones = sb("ones", [P, P])
        b.kconst = sb("kconst", [P, 2])
        b.wq = sb("wq", [P, 2, DC, D])
        b.wk = sb("wk", [P, 2, DC, D])
        b.wv = sb("wv", [P, 2, DC, D])
        b.wo = sb("wo", [P, 2, DC, D])
        b.bq = sb("bq", [P, 2, DC])
        b.bk = sb("bk", [P, 2, DC])
        b.bv = sb("bv", [P, 2, D])
        b.bo = sb("bo", [P, 2, D])
        b.stats = sb("stats", [P, TC, 6])
        b.mv = sb("mv", [P, TC, 2])
        b.var = sb("var", [P, TC])
        b.rstd = sb("rstd", [P, TC])
        b.newt = sb("newt", [P, TC])
        b.xnT = sb("xnT", [P, DC, QC])
        arena = sb("arena", [P, 36000])
        b.used = 0

        def carve(shape, dt=fp32, at=None):
            n = 1
            for s in shape[1:]:
                n *= s
            words = n if dt in (fp32, i32, u32) else (n + 1) // 2 if dt == bf16 else (n + 3) // 4
            start = b.used if at is None else at
            b.used = start + words
            assert b.used <= 36000, b.used
            v = arena[:shape[0], start:start + words]
            if dt != fp32:
                v = v.bitcast(dt)
            v = v[:, 0:n]
            if len(shape) == 3:
                v = v.rearrange("p (a b) -> p a b", a=shape[1])
            if len(shape) == 4:
                v = v.rearrange("p (a b c) -> p a b c", a=shape[1], b=shape[2])
            return v

        b.carve = carve
        psum = ctx.enter_context(nc.psum_tensor("psum", [P, 8 * 512], fp32))
        b.psum = psum
        b.bank = [psum[:, 512 * i:512 * (i + 1)] for i in range(8)]
        b.banks34 = psum[:, 3 * 512:5 * 512]
        b.banks56 = psum[:, 5 * 512:7 * 512]
        b.slot = sb("slot", [P, 2 * NT], u32)
        b.gate = sb("gate", [P, 2, NT])
        b.texp = sb("texp", [P, 40], u32)

        b.qd = [nc.dram_tensor(f"q_parts{l}", (3, D, S), bf16, kind="Internal").ap() for l in range(2)]
        b.kd = [nc.dram_tensor(f"k_parts{l}", (3, D, SK), bf16, kind="Internal").ap() for l in range(2)]
        b.xs = [nc.dram_tensor(f"sorted_in{l}", (routing(l + 1)[1] * P, D), fp32, kind="Internal").ap()
                for l in range(2)]
        b.ys = [nc.dram_tensor(f"sorted_out{l}", (routing(l + 1)[1] * P, D), fp32, kind="Internal").ap()
                for l in range(2)]

        phases = [lambda: setup(nc, b, io)]
        for l in range(2):
            phases += [lambda l=l: keys_values(nc, b, io, l), lambda l=l: queries(nc, b, io, l),
                       lambda l=l: (attention0 if l == 0 else attention1)(nc, b, io),
                       lambda l=l: route(nc, b, io, l), lambda l=l: experts(nc, b, io, l),
                       lambda l=l: combine(nc, b, io, l)]
        for n, ph in enumerate(phases):
            if n <= stop:
                ph()
            if n == len(phases) // 2:
                nc.clear_and_free_semaphores(layer_sems)
                layer_sems.clear()
                nc.all_engine_barrier()
        if stop < len(phases) - 1:
            dump(nc, b, io)


def dump(nc, b, io):
    s = b.sem("dump")
    with nc.Block() as block:
        @block.sync
        def _(sp):
            sp.dma_start(io["out"].rearrange("(t p) d -> p t d", p=P), b.x[:, :, :]).then_inc(s, 16)
            sp.wait_ge(s, 16)


def setup(nc, b, io):
    zeros = b.carve([P, 1024], at=0)
    loaded, cleared, zero, made = (b.sem(n) for n in ("su_loaded", "su_cleared", "su_zero", "su_made"))
    with nc.Block() as block:
        @block.sync
        def _(sp):
            loads = [(b.x[:, :, :], io["x"].rearrange("(t p) d -> p t d", p=P)),
                     (b.kconst[:, :], io["kconst"]), (b.tri[:, :], io["tri"])]
            for l in range(2):
                for w, n in ((b.wq, "wqT"), (b.wk, "wkT"), (b.wv, "wvT"), (b.wo, "woT")):
                    loads.append((w[:, l], io[f"{n}{l}"].rearrange("(c p) n -> p c n", p=P)))
                for w, n in ((b.bv, "bv"), (b.bo, "bo")):
                    loads.append((w[:, l], io[f"{n}{l}"].rearrange("(a n) -> a n", a=1).to_broadcast([P, D])))
                for w, n in ((b.bq, "bq"), (b.bk, "bk")):
                    loads.append((w[:, l], io[f"{n}{l}"]))
            for dst, src in loads:
                sp.dma_start(dst, src).then_inc(loaded, 16)
            sp.wait_ge(zero, 1)
            n = 0
            for l in range(2):
                rows = b.xs[l].shape[0] // P
                flat = b.xs[l].rearrange("(p a) d -> p (a d)", p=P)
                for at in range(0, rows * D, 1024):
                    sp.dma_start(flat[:, at:at + 1024], zeros[:, :]).then_inc(cleared, 16)
                    n += 1
            sp.wait_ge(loaded, 16 * len(loads))
            sp.wait_ge(cleared, 16 * n)

        @block.gpsimd
        def _(pool):
            pool.memset(b.ident[:, :], 0.0).then_inc(made, 1)
            pool.memset(b.identb[:, :], 0.0).then_inc(made, 1)
            pool.memset(b.ones[:, :], 1.0).then_inc(made, 1)
            pool.wait_ge(made, 3)
            for m in (b.ident, b.identb):
                pool.affine_select(out=m[:, :], in_=m[:, :], compare_op=ALU.not_equal, fill=1.0, base=0,
                                   pattern=[[-1, P]], channel_multiplier=1).then_inc(made, 1)
            pool.wait_ge(made, 5)

        @block.vector
        def _(dve):
            dve.memset(zeros[:, :], 0.0).then_inc(zero, 1)


def keys_values(nc, b, io, l):
    b.used = 0
    b.ks = b.carve([P, H, SKP], bf16)
    b.v = b.carve([P, KT, H * 32])
    b.attn_at = b.used
    ctxT = b.carve([P, DC, SK])
    kf = b.carve([P, SK])
    rest = b.carve([P, SK])
    parts = b.carve([P, 3, SKP], bf16)
    mask = b.carve([P, SKP])
    mask8 = b.carve([P, SK], u8)
    n = f"kv{l}_"
    loaded, prod, evac, chain, ready, stored, placed, vprod, vevac, vzero = (b.sem(n + x) for x in (
        "loaded", "prod", "evac", "chain", "ready", "stored", "placed", "vprod", "vevac", "vzero"))
    with nc.Block() as block:
        @block.sync
        def _(sp):
            sp.dma_start(ctxT, io["ctxT"].rearrange("(c p) n -> p c n", p=P)).then_inc(loaded, 16)
            sp.dma_start(mask8, io["mask"].to_broadcast([P, SK])).then_inc(loaded, 16)
            for m in range(DC):
                sp.wait_ge(ready, m + 1)
                sp.dma_start(b.kd[l][:, m * P:(m + 1) * P, :].rearrange("r p n -> p r n"),
                             parts[:, :, 0:SK]).then_inc(stored, 16)
                sp.wait_ge(stored, 16 * (m + 1))
            sp.wait_ge(vzero, 5)
            for r in range(NB):
                sp.dma_start(b.ks[r * HD:(r + 1) * HD, :, 0:SK],
                             b.kd[l][KPART[r]].rearrange("(h d) n -> d h n", d=HD)).then_inc(placed, 16)
            sp.wait_ge(placed, 16 * NB)

        @block.tensor
        def _(pe):
            pe.wait_ge(loaded, 32)
            u = 0
            for m in range(DC):
                for at, width in KCOLS:
                    if u >= 4:
                        pe.wait_ge(evac, u - 3)
                    for kk in range(DC):
                        mm = pe.matmul(b.bank[u % 4][:, 0:width], b.wk[:, l, kk, m * P:(m + 1) * P],
                                       ctxT[:, kk, at:at + width], start=(kk == 0), stop=(kk == DC - 1))
                    mm.then_inc(prod, 1)
                    u += 1
            for k in range(KT):
                if k >= 4:
                    pe.wait_ge(vevac, k - 3)
                for kk in range(DC):
                    mm = pe.matmul(b.bank[4 + k % 4][0:KROWS[k], 0:D], ctxT[:, kk, k * P:k * P + KROWS[k]],
                                   b.wv[:, l, kk, :], start=(kk == 0), stop=(kk == DC - 1))
                mm.then_inc(vprod, 1)

        @block.gpsimd
        def _(pool):
            v4 = b.v.rearrange("p k (h c) -> p (k h) c", c=32)
            full = (KT - 1) * H
            pool.memset(v4[:, 0:full, 16:32], 0.0).then_inc(vzero, 1)
            pool.wait_ge(vzero, 1)
            pool.memset(v4[:, full:KT * H, :], 0.0).then_inc(vzero, 1)
            pool.wait_ge(vzero, 2)
            pool.memset(v4[:, 0:full, 16:17], 1.0).then_inc(vzero, 1)
            pool.wait_ge(vzero, 3)
            pool.memset(v4[0:KROWS[-1], full:KT * H, 16:17], 1.0).then_inc(vzero, 1)
            pool.wait_ge(vzero, 4)
            pool.memset(b.ks[0:ROW_MASK, :, SK - 1:SKP], 0.0).then_inc(vzero, 1)
            pool.wait_ge(vzero, 5)

        @block.vector
        def _(dve):
            count = [0]

            def link(ins):
                count[0] += 1
                ins.then_inc(chain, 1)
                dve.wait_ge(chain, count[0])

            dve.wait_ge(loaded, 32)
            link(dve.memset(mask[:, SK:SKP], 0.0))
            link(dve.tensor_copy(mask[:, 0:SK], mask8[:, :]))
            if l == 1:
                rows = slice(ROW_MASK, P)
                for h in range(H):
                    dve.tensor_scalar(b.ks[rows, h, :], mask[rows, :], b.kconst[rows, 0:1],
                                      b.kconst[rows, 1:2], ALU.mult, ALU.add).then_inc(chain, 1)
                count[0] += H
                dve.wait_ge(chain, count[0])
            u = 0
            for m in range(DC):
                for at, width in KCOLS:
                    dve.wait_ge(prod, u + 1)
                    if l == 0:
                        ins = dve.tensor_scalar(kf[:, at:at + width], b.bank[u % 4][:, 0:width],
                                                b.bk[:, l, m:m + 1], None, ALU.add)
                    else:
                        ins = dve.scalar_tensor_tensor(out=kf[:, at:at + width], in0=b.bank[u % 4][:, 0:width],
                                                       scalar=b.bk[:, l, m:m + 1], in1=mask[:, at:at + width],
                                                       op0=ALU.add, op1=ALU.mult)
                    ins.then_inc(evac, 1)
                    u += 1
                dve.wait_ge(evac, u)
                if m >= 1:
                    dve.wait_ge(stored, 16 * m)
                src = kf
                for r in range(3):
                    ins = dve.tensor_copy(parts[:, r, 0:SK], src[:, :])
                    if r == 2:
                        ins.then_inc(ready, 1)
                    else:
                        link(ins)
                        link(dve.tensor_tensor(rest[:, :], src[:, :], parts[:, r, 0:SK], ALU.subtract))
                        src = rest
            dve.wait_ge(vzero, 2)
            for k in range(KT):
                dve.wait_ge(vprod, k + 1)
                n = KROWS[k]
                dve.tensor_tensor(b.v[0:n, k, :].rearrange("p (h c) -> p h c", c=32)[:, :, 0:HD],
                                  b.bank[4 + k % 4][0:n, 0:D].rearrange("p (h c) -> p h c", c=HD),
                                  b.bv[0:n, l, :].rearrange("p (h c) -> p h c", c=HD),
                                  ALU.add).then_inc(vevac, 1)
            dve.wait_ge(vevac, KT)


def norm_vector(dve, b, c, s, xn, src=None):
    src = b.x if src is None else src
    for j in range(TC):
        dve.bn_stats(b.stats[:, j, :], src[:, bass.ds(c * TC + j, 1), :].rearrange("p a d -> p (a d)")
                     ).then_inc(s.stat, 1)
    dve.wait_ge(s.stat, c * STATS + TC)
    even, odd = b.stats[:, :, 0:3], b.stats[:, :, 3:6]
    dve.tensor_tensor(b.mv[:, :, 0], even[:, :, 1], odd[:, :, 1], ALU.add).then_inc(s.stat, 1)
    dve.tensor_tensor(b.mv[:, :, 1], even[:, :, 1], odd[:, :, 1], ALU.subtract).then_inc(s.stat, 1)
    dve.tensor_tensor(b.var[:, :], even[:, :, 2], odd[:, :, 2], ALU.add).then_inc(s.stat, 1)
    dve.wait_ge(s.stat, c * STATS + TC + 3)
    dve.tensor_scalar(b.mv[:, :, 0], b.mv[:, :, 0], 0.5, None, ALU.mult).then_inc(s.stat, 1)
    dve.scalar_tensor_tensor(out=b.mv[:, :, 1], in0=b.mv[:, :, 1], scalar=0.25, in1=b.mv[:, :, 1],
                             op0=ALU.mult, op1=ALU.mult).then_inc(s.stat, 1)
    dve.tensor_scalar(b.var[:, :], b.var[:, :], 1.0 / D, EPS, ALU.mult, ALU.add).then_inc(s.stat, 1)
    dve.wait_ge(s.stat, c * STATS + STATS)
    dve.tensor_tensor(b.var[:, :], b.var[:, :], b.mv[:, :, 1], ALU.add).then_inc(s.vare, 1)
    dve.wait_ge(s.root, 2 * c + 2)
    dve.tensor_tensor(b.newt[:, :], b.rstd[:, :], b.rstd[:, :], ALU.mult).then_inc(s.newton, 1)
    dve.wait_ge(s.newton, c * 4 + 1)
    dve.tensor_tensor(b.newt[:, :], b.newt[:, :], b.var[:, :], ALU.mult).then_inc(s.newton, 1)
    dve.wait_ge(s.newton, c * 4 + 2)
    dve.tensor_scalar(b.newt[:, :], b.newt[:, :], -0.5, 1.5, ALU.mult, ALU.add).then_inc(s.newton, 1)
    dve.wait_ge(s.newton, c * 4 + 3)
    dve.tensor_tensor(b.rstd[:, :], b.rstd[:, :], b.newt[:, :], ALU.mult).then_inc(s.newton, 1)
    dve.wait_ge(s.newton, c * 4 + 4)
    for j in range(TC):
        dve.tensor_scalar(xn(j), src[:, bass.ds(c * TC + j, 1), :].rearrange("p a d -> p (a d)"),
                          b.mv[:, j, 0:1], b.rstd[:, j:j + 1], ALU.subtract, ALU.mult).then_inc(s.normed, 1)


def norm_scalar(act, b, c, s):
    act.wait_ge(s.vare, c + 1)
    act.activation(b.rstd[:, :], b.var[:, :], ACT.Ln).then_inc(s.root, 1)
    act.wait_ge(s.root, 2 * c + 1)
    act.activation(b.rstd[:, :], b.rstd[:, :], ACT.Exp, scale=-0.5).then_inc(s.root, 1)


def norm_sems(b, n):
    s = Buffers()
    s.stat, s.vare, s.root, s.newton, s.normed = (b.sem(n + x) for x in (
        "stat", "vare", "root", "newton", "normed"))
    return s


def queries(nc, b, io, l):
    b.used = b.attn_at
    xn = b.carve([P, TC, D])
    qf = b.carve([P, DC, QC])
    rest = b.carve([P, QC])
    parts = b.carve([P, 3, DC, QC], bf16)
    n = f"q{l}_"
    s = norm_sems(b, n)
    turned, copied, prod, evac, chain, ready, stored = (b.sem(n + x) for x in (
        "turned", "copied", "prod", "evac", "chain", "ready", "stored"))
    with nc.Block() as block:
        @block.sync
        def _(sp):
            with sp.Fori(0, NCH) as c:
                sp.wait_ge(ready, 2 * c + 2)
                for r in range(3):
                    sp.dma_start(b.qd[l][r, :, bass.ds(c * QC, QC)].rearrange("(m p) q -> p m q", p=P),
                                 parts[:, r]).then_inc(stored, 16)
            sp.wait_ge(stored, 48 * NCH)

        @block.scalar
        def _(act):
            act.preload_act_table_set(LN_EXP)
            with act.Fori(0, NCH) as c:
                norm_scalar(act, b, c, s)
                for kk in range(DC):
                    act.wait_ge(turned, DC * c + kk + 1)
                    act.activation(b.xnT[:, kk, :], b.bank[kk][:, :], ACT.Copy).then_inc(copied, 1)

        @block.tensor
        def _(pe):
            with pe.Fori(0, NCH) as c:
                pe.wait_ge(s.normed, TC * c + TC)
                for kk in range(DC):
                    for j in range(TC):
                        mm = pe.transpose(b.bank[kk][:, j * P:(j + 1) * P], xn[:, j, kk * P:(kk + 1) * P],
                                          b.ident[:, :])
                    mm.then_inc(turned, 1)
                pe.wait_ge(copied, DC * c + DC)
                for m in range(DC):
                    for kk in range(DC):
                        mm = pe.matmul(b.bank[2 + m][:, :], b.wq[:, l, kk, m * P:(m + 1) * P],
                                       b.xnT[:, kk, :], start=(kk == 0), stop=(kk == DC - 1))
                    mm.then_inc(prod, 1)
                pe.wait_ge(evac, DC * c + DC)

        @block.vector
        def _(dve):
            with dve.Fori(0, NCH) as c:
                norm_vector(dve, b, c, s, lambda j: xn[:, j, :])
                k = 0
                for m in range(DC):
                    dve.wait_ge(prod, DC * c + m + 1)
                    dve.tensor_scalar(qf[:, m, :], b.bank[2 + m][:, :], b.bq[:, l, m:m + 1], HD ** -0.5,
                                      ALU.add, ALU.mult).then_inc(evac, 1)
                    dve.wait_ge(evac, DC * c + m + 1)
                    src = qf[:, m, :]
                    for r in range(3):
                        ins = dve.tensor_copy(parts[:, r, m, :], src)
                        if r == 2:
                            ins.then_inc(ready, 1)
                        else:
                            ins.then_inc(chain, 1)
                            k += 1
                            dve.wait_ge(chain, 8 * c + k)
                            dve.tensor_tensor(rest[:, :], src, parts[:, r, m, :],
                                              ALU.subtract).then_inc(chain, 1)
                            k += 1
                            dve.wait_ge(chain, 8 * c + k)
                            src = rest[:, :]
                    dve.wait_ge(ready, 2 * c + m + 1)
                assert k == 8
                dve.wait_ge(turned, DC * c + DC)
                dve.wait_ge(stored, 48 * c + 48)


def load_queries(sp, b, l, q, c, loaded):
    for r in range(NB):
        sp.dma_start(q[r * HD:(r + 1) * HD, :, :],
                     b.qd[l][QPART[r], :, bass.ds(c * QC, QC)].rearrange("(h d) q -> d h q", d=HD)
                     ).then_inc(loaded, 16)


def key_tile(i):
    g, r = divmod(i, U)
    k, j = divmod(r, HG)
    return g, k, j


def value_product(pe, b, ring, g, k, acc, done):
    for j in range(HG):
        h = g * HG + j
        i = (g * KT + k) * HG + j
        mm = pe.matmul(acc[32 * j:32 * j + 32, :], b.v[:, k, 32 * h:32 * h + 32],
                       ring[:, i % NW, :], start=(k == 0), stop=(k == KT - 1))
    mm.then_inc(done, 1)


def finish_sems(b, n):
    f = Buffers()
    f.acc_out, f.turned, f.recip, f.scaled, f.turned2, f.copied2, f.proj, f.added, f.resid = (
        b.sem(n + x) for x in ("acc_out", "turned", "recip", "scaled", "turned2", "copied2", "proj",
                               "added", "resid"))
    return f


def finish_tensor(pe, b, l, c, f, accs, att, attT):
    for t in range(TC):
        if t == 0:
            pe.wait_ge(f.acc_out, G * c + G)
        for g in range(G):
            mm = pe.transpose(b.bank[t][:, g * P:(g + 1) * P], accs[:, g, t * P:(t + 1) * P], b.ident[:, :])
        mm.then_inc(f.turned, 1)
    for t in range(TC):
        pe.wait_ge(f.scaled, TC * c + t + 1)
        o = b.bank[4 + t % 2]
        if t >= 2:
            pe.wait_ge(f.added, TC * c + t - 1)
        for kk in range(DC):
            mm = pe.transpose(o[:, kk * P:(kk + 1) * P], att[:, t % 2, kk * P:(kk + 1) * P], b.ident[:, :])
        mm.then_inc(f.turned2, 1)
        pe.wait_ge(f.copied2, TC * c + t + 1)
        for kk in range(DC):
            mm = pe.matmul(o[:, D:2 * D], attT[:, t % 2, kk, :], b.wo[:, l, kk, :],
                           start=(kk == 0), stop=(kk == DC - 1))
        mm.then_inc(f.proj, 1)


def finish_vector(dve, b, l, c, f, rsum, att, attT, out):
    for t in range(TC):
        dve.wait_ge(f.turned, TC * c + t + 1)
        rows = b.bank[t][:, :].rearrange("p (h c) -> p h c", c=32)
        dve.reciprocal(rsum[:, t, :], rows[:, :, HD]).then_inc(f.recip, 1)
        dve.wait_ge(f.recip, TC * c + t + 1)
        if t >= 2:
            dve.wait_ge(f.turned2, TC * c + t - 1)
        dve.tensor_tensor(att[:, t % 2, :].rearrange("p (h c) -> p h c", c=HD), rows[:, :, 0:HD],
                          rsum[:, t, :].rearrange("p (h a) -> p h a", a=1).to_broadcast([P, H, HD]),
                          ALU.mult).then_inc(f.scaled, 1)
        if t >= 1:
            finish_tile(dve, b, l, c, f, t - 1, att, attT, out)
    finish_tile(dve, b, l, c, f, TC - 1, att, attT, out)


def end_vector(dve, c, f, valued):
    dve.wait_ge(f.resid, TC * c + TC)
    dve.wait_ge(valued, (c + 1) * G * KT)


def finish_tile(dve, b, l, c, f, t, att, attT, out):
    o = b.bank[4 + t % 2]
    dve.wait_ge(f.turned2, TC * c + t + 1)
    if t >= 2:
        dve.wait_ge(f.proj, TC * c + t - 1)
    dve.tensor_copy(attT[:, t % 2].rearrange("p a q -> p (a q)"), o[:, 0:D]).then_inc(f.copied2, 1)
    dve.wait_ge(f.proj, TC * c + t + 1)
    if t >= 1:
        dve.wait_ge(f.resid, TC * c + t)
    dve.tensor_tensor(out[:, :], o[:, D:2 * D], b.bo[:, l, :], ALU.add).then_inc(f.added, 1)
    dve.wait_ge(f.added, TC * c + t + 1)
    row = b.x[:, bass.ds(c * TC + t, 1), :].rearrange("p a d -> p (a d)")
    dve.tensor_tensor(row, row, out[:, :], ALU.add).then_inc(f.resid, 1)


def attention0(nc, b, io):
    b.used = b.attn_at
    q = b.carve([P, H, QC], bf16)
    ring = b.carve([P, NW, QC])
    accs = b.carve([P, G, QC])
    rsum = b.carve([P, TC, H])
    att = b.carve([P, 2, D])
    attT = b.carve([P, 2, DC, P])
    out = b.carve([P, D])
    n = "a0_"
    loaded, scored, clipped, clipped_act, logged, exped, weighted, valued = (b.sem(n + x) for x in (
        "loaded", "scored", "clipped", "clipped_act", "logged", "exped", "weighted", "valued"))
    f = finish_sems(b, n)
    NPV = G * KT
    with nc.Block() as block:
        @block.sync
        def _(sp):
            load_queries(sp, b, 0, q, 0, loaded)
            with sp.Fori(1, NCH) as c:
                sp.wait_ge(scored, c * PC2)
                load_queries(sp, b, 0, q, c, loaded)
            sp.wait_ge(loaded, 16 * NB * NCH)

        @block.tensor
        def _(pe):
            with pe.Fori(0, NCH) as c:
                pe.wait_ge(loaded, 16 * NB * (c + 1))

                def values(v):
                    g, k = divmod(v, KT)
                    pe.wait_ge(weighted, c * PC2 + 2 * (v + 1))
                    if k == 0 and g >= 2:
                        pe.wait_ge(f.acc_out, G * c + g - 1)
                    value_product(pe, b, ring, g, k, b.bank[6 + g % 2], valued)

                for i in range(PC2):
                    if i >= NS0:
                        pe.wait_ge(weighted, c * PC2 + i - NS0 + 1)
                    for u in (2 * i, 2 * i + 1):
                        g, k, j = key_tile(u)
                        mm = pe.matmul(b.bank[u % (2 * NS0)][:, :],
                                       b.ks[0:ROW_MASK, g * HG + j, k * P:(k + 1) * P],
                                       q[0:ROW_MASK, g * HG + j, :], start=True, stop=True)
                    mm.then_inc(scored, 1)
                    if i % 2 == 0 and i >= 4:
                        values(i // 2 - 2)
                for v in range(NPV - 2, NPV):
                    values(v)
                finish_tensor(pe, b, 0, c, f, accs, att, attT)
                pe.wait_ge(f.resid, TC * c + TC)

        def pair(x, i, n):
            return x[:, 1024 * (i % n):1024 * (i % n) + 1024]

        rings = ring.rearrange("p a q -> p (a q)")
        by_act = [i % CLIP == CLIP - 1 for i in range(PC2)]

        @block.vector
        def _(dve):
            with dve.Fori(0, NCH) as c:
                for i in range(PC2 + 1):
                    if i < PC2 and not by_act[i]:
                        dve.wait_ge(scored, c * PC2 + i + 1)
                        if i >= NW // 2:
                            dve.wait_ge(valued, c * NPV + (i - NW // 2) // 2 + 1)
                        dve.tensor_scalar(pair(rings, i, NW // 2), pair(b.psum, i, NS0), 0.0, None,
                                          ALU.min).then_inc(clipped, 1)
                    if i >= 1:
                        o = i - 1
                        dve.wait_ge(exped, c * PC2 + o + 1)
                        dve.scalar_tensor_tensor(out=pair(rings, o, NW // 2), in0=pair(b.psum, o, NS0),
                                                 scalar=1.0, in1=pair(rings, o, NW // 2), op0=ALU.add,
                                                 op1=ALU.max).then_inc(weighted, 1)
                finish_vector(dve, b, 0, c, f, rsum, att, attT, out)
                end_vector(dve, c, f, valued)

        @block.scalar
        def _(act):
            act.preload_act_table_set(LN_EXP)
            with act.Fori(0, NCH) as c:
                def sums_out(g):
                    act.wait_ge(valued, c * NPV + (g + 1) * KT)
                    act.activation(accs[:, g, :], b.bank[6 + g % 2][:, :], ACT.Copy).then_inc(f.acc_out, 1)

                for i in range(PC2):
                    tile = pair(rings, i, NW // 2)
                    if by_act[i]:
                        act.wait_ge(scored, c * PC2 + i + 1)
                        if i >= NW // 2:
                            act.wait_ge(valued, c * NPV + (i - NW // 2) // 2 + 1)
                        act.activation(tile, pair(b.psum, i, NS0), ACT.Relu, scale=-1.0).then_inc(clipped_act, 1)
                        act.wait_ge(clipped_act, c * sum(by_act) + sum(by_act[:i + 1]))
                    else:
                        act.wait_ge(clipped, c * (PC2 - sum(by_act)) + i + 1 - sum(by_act[:i]))
                    act.activation(tile, tile, ACT.Ln, bias=1.0,
                                   scale=1.0 if by_act[i] else -1.0).then_inc(logged, 1)
                    act.wait_ge(logged, c * PC2 + i + 1)
                    act.activation(tile, tile, ACT.Exp, scale=-1.0).then_inc(exped, 1)
                    if i > U // 2 and i % (U // 2) == 2 * HG:
                        sums_out(i // (U // 2) - 1)
                sums_out(G - 1)
                act.wait_ge(f.turned, TC * c + TC)
                act.wait_ge(valued, (c + 1) * NPV)


def attention1(nc, b, io):
    b.used = b.attn_at
    q = b.carve([P, H, QC], bf16)
    ring = b.carve([P, NW, QC])
    accs = b.carve([P, G, QC])
    rsum = b.carve([P, TC, H])
    att = b.carve([P, 2, D])
    attT = b.carve([P, 2, DC, P])
    out = b.carve([P, D])
    mx2 = b.carve([P, HG * TC, 2])
    mx = b.carve([P, HG * TC])
    mparts = b.carve([P, P], bf16)
    mrows = b.carve([3 * HG * TC, P], bf16)
    n = "a1_"
    loaded, ones, zeroed, scored, exped, valued, mscored, mread, mchain, mcut, mturned, mcopied, placed = (
        b.sem(n + x) for x in ("loaded", "ones", "zeroed", "scored", "exped", "valued", "mscored", "mread", "mchain",
                               "mcut", "mturned", "mcopied", "placed"))
    f = finish_sems(b, n)
    NPV = G * KT
    MU = HG * TC
    MH = 2 * MU
    bT = b.bank[3][:, 0:P // 2].bitcast(bf16)
    with nc.Block() as block:
        @block.gpsimd
        def _(pool):
            pool.memset(mparts[:, :], 0.0).then_inc(zeroed, 1)
            pool.wait_ge(zeroed, 1)
            pool.memset(q[ROW_MASK:P, :, :], 1.0).then_inc(ones, 1)

        @block.sync
        def _(sp):
            def place_maxima(before):
                for g in range(G):
                    sp.wait_ge(mcopied, before * G + g + 1)
                    for r in range(3):
                        sp.dma_start(q[ROW_MAX + r:ROW_MAX + r + 1, g * HG:(g + 1) * HG, :]
                                     .rearrange("a h (t q) -> a (h t) q", q=P),
                                     mrows[r * MU:(r + 1) * MU, :]).then_inc(placed, 16)

            sp.wait_ge(ones, 1)
            load_queries(sp, b, 1, q, 0, loaded)
            with sp.Fori(1, NCH) as c:
                place_maxima(c - 1)
                sp.wait_ge(scored, c * UC)
                load_queries(sp, b, 1, q, c, loaded)
            place_maxima(NCH - 1)
            sp.wait_ge(placed, 48 * G * NCH)
            sp.wait_ge(loaded, 16 * NB * NCH)

        @block.tensor
        def _(pe):
            pe.wait_ge(ones, 1)
            with pe.Fori(0, NCH) as c:
                pe.wait_ge(loaded, 16 * NB * (c + 1))
                def max_half(g, m):
                    j, t = divmod(m // 2, TC)
                    h = g * HG + j
                    if m >= 2:
                        pe.wait_ge(mread, (c * G + g) * MH + m - 1)
                    elif m == 0 and g >= 1:
                        pe.wait_ge(mread, (c * G + g) * MH)
                        pe.wait_ge(mcopied, c * G + g)
                    lo = 3 + 2 * (m % 2)
                    for n, (at, width) in enumerate(KCOLS[2 * (m % 2):2 * (m % 2) + 2]):
                        mm = pe.matmul(b.bank[lo + n][:, 0:width], q[0:ROW_MAX, h, t * P:(t + 1) * P],
                                       b.ks[0:ROW_MAX, h, at:at + width], start=True, stop=True)
                    mm.then_inc(mscored, 1)

                def max_rows(g):
                    pe.wait_ge(mcut, c * G + g + 1)
                    pe.transpose(bT, mparts, b.identb[:, :]).then_inc(mturned, 1)

                def scores(i):
                    g, k, j = key_tile(i)
                    h = g * HG + j
                    if i % U == 0:
                        pe.wait_ge(placed, 48 * (c * G + g + 1))
                    if i >= NS1:
                        pe.wait_ge(exped, c * UC + i - NS1 + 1)
                    pe.matmul(b.bank[i % NS1][:, :], b.ks[0:ROWS_ALL, h, k * P:(k + 1) * P],
                              q[0:ROWS_ALL, h, :], start=True, stop=True).then_inc(scored, 1)

                def values(v):
                    g, k = divmod(v, KT)
                    pe.wait_ge(exped, c * UC + HG * (v + 1))
                    if k == 0 and g >= 1:
                        pe.wait_ge(f.acc_out, G * c + g)
                    value_product(pe, b, ring, g, k, b.bank[7], valued)

                for m in range(MH):
                    max_half(0, m)
                max_rows(0)
                for g in range(G):
                    made = 0
                    for r in range(U):
                        i = g * U + r
                        scores(i)
                        if r % HG == 0 and i >= HG:
                            values(i // HG - 1)
                        if g < G - 1:
                            while made < MH * (r + 1) // (U - 4) and made < MH:
                                max_half(g + 1, made)
                                made += 1
                    if g < G - 1:
                        max_rows(g + 1)
                values(NPV - 1)
                finish_tensor(pe, b, 1, c, f, accs, att, attT)
                pe.wait_ge(f.resid, TC * c + TC)
                pe.wait_ge(mcopied, (c + 1) * G)

        @block.vector
        def _(dve):
            dve.wait_ge(zeroed, 1)
            with dve.Fori(0, NCH) as c:
                for g in range(G):
                    for m in range(MH):
                        lo = 3 + 2 * (m % 2)
                        dve.wait_ge(mscored, (c * G + g) * MH + m + 1)
                        if m % 2 == 0:
                            src = b.banks34[:, :]
                        else:
                            src = b.banks56[:, 0:SK - 1024]
                        dve.tensor_reduce(mx2[:, m // 2, m % 2:m % 2 + 1], src, AX.X, ALU.max
                                          ).then_inc(mread, 1)
                    dve.wait_ge(mread, (c * G + g + 1) * MH)
                    base = (c * G + g) * 5
                    dve.tensor_tensor(mx[:, :], mx2[:, :, 0], mx2[:, :, 1], ALU.max).then_inc(mchain, 1)
                    dve.wait_ge(mchain, base + 1)
                    if g >= 1:
                        dve.wait_ge(mturned, c * G + g)
                    for r in range(3):
                        ins = dve.tensor_copy(mparts[:, r * MU:(r + 1) * MU], mx[:, :])
                        if r == 2:
                            ins.then_inc(mcut, 1)
                        else:
                            ins.then_inc(mchain, 1)
                            dve.wait_ge(mchain, base + 2 * r + 2)
                            dve.tensor_tensor(mx[:, :], mx[:, :], mparts[:, r * MU:(r + 1) * MU], ALU.subtract
                                              ).then_inc(mchain, 1)
                            dve.wait_ge(mchain, base + 2 * r + 3)
                    dve.wait_ge(mcut, c * G + g + 1)
                    dve.wait_ge(mturned, c * G + g + 1)
                    if g >= 1:
                        dve.wait_ge(placed, 48 * (c * G + g))
                    dve.tensor_copy(mrows[:, :], bT[0:3 * MU, :]).then_inc(mcopied, 1)
                finish_vector(dve, b, 1, c, f, rsum, att, attT, out)
                end_vector(dve, c, f, valued)
                dve.wait_ge(placed, 48 * G * (c + 1))

        @block.scalar
        def _(act):
            act.preload_act_table_set(LN_EXP)
            with act.Fori(0, NCH) as c:
                def sums_out(g):
                    act.wait_ge(valued, c * NPV + (g + 1) * KT)
                    act.activation(accs[:, g, :], b.bank[7][:, :], ACT.Copy).then_inc(f.acc_out, 1)

                for i in range(UC):
                    act.wait_ge(scored, c * UC + i + 1)
                    if i >= NW:
                        act.wait_ge(valued, c * NPV + (i - NW) // HG + 1)
                    act.activation(ring[:, i % NW, :], b.bank[i % NS1][:, :], ACT.Exp
                                   ).then_inc(exped, 1)
                    if i > U and i % U == 3:
                        sums_out(i // U - 1)
                sums_out(G - 1)
                act.wait_ge(f.turned, TC * c + TC)
                act.wait_ge(valued, (c + 1) * NPV)


def tile_of(x, c, j):
    return x[:, bass.ds(c * TC + j, 1), :].rearrange("p a d -> p (a d)")


def route(nc, b, io, l):
    top = l + 1
    NA, T = routing(top)
    b.used = 0
    b.shared = b.carve([P, NT, D])
    b.expert_at = b.used
    xn = b.carve([P, TC, D])
    xall = b.carve([P, NT, D])
    logits = b.carve([P, NT, E])
    logit_bias = b.carve([P, TC * E])
    gate_w = b.carve([P, DC, E])
    shared_w = b.carve([P, DC, D])
    shared_b = b.carve([P, D])
    best = b.carve([P, NT, E])
    best_at = b.carve([P, NT, E], u32)
    at_f = b.carve([P, top, NT])
    onehot = b.carve([P, NA, E])
    iota_e = b.carve([P, E])
    iota_rows = b.carve([P, NA])
    iota_t = b.carve([P, T])
    totals = b.carve([P, NA, E])
    upto = b.carve([P, E, NA])
    fills = b.carve([P, E, NA])
    tiles = b.carve([P, E])
    ends = b.carve([P, E])
    base = b.carve([P, E])
    place = b.carve([P, NA, E])
    place_f = b.carve([P, NA])
    owner = b.carve([P, T, E])
    owner_f = b.carve([P, T])
    expd = b.carve([P, NT, E])
    n = f"r{l}_"
    s = norm_sems(b, n)
    loaded, turned, copied, kept, prod, evac, chain, onehots, counted, shifted, exped, placed, sent, act_done = (
        b.sem(n + x) for x in ("loaded", "turned", "copied", "kept", "prod", "evac", "chain", "onehots",
                               "counted", "shifted", "exped", "placed", "sent", "act_done"))
    NL = 7 if l else 5
    with nc.Block() as block:
        @block.sync
        def _(sp):
            sp.dma_start(gate_w, io[f"gate{l}"].rearrange("(c p) e -> p c e", p=P)).then_inc(loaded, 16)
            sp.dma_start(iota_e, io["iota"][0:1, 0:E].to_broadcast([P, E])).then_inc(loaded, 16)
            sp.dma_start(iota_rows, io["iota"][1:2, 0:NA].to_broadcast([P, NA])).then_inc(loaded, 16)
            sp.dma_start(iota_t, io["iota"][0:1, 0:T].to_broadcast([P, T])).then_inc(loaded, 16)
            if l == 0:
                src = io["gate_bias"].rearrange("(a n) -> a n", a=1)
                for j in range(TC):
                    sp.dma_start(logit_bias[:, j * E:(j + 1) * E], src.to_broadcast([P, E])).then_inc(loaded, 16)
            else:
                sp.dma_start(shared_w, io["shared_w"].rearrange("(c p) n -> p c n", p=P)).then_inc(loaded, 16)
                sp.dma_start(shared_b, io["shared_b"].rearrange("(a n) -> a n", a=1).to_broadcast([P, D])
                             ).then_inc(loaded, 16)
            sp.wait_ge(loaded, 16 * (4 + (TC if l == 0 else 2)))

        NLOAD = 16 * (4 + (TC if l == 0 else 2))

        @block.scalar
        def _(act):
            act.preload_act_table_set(LN_EXP)
            with act.Fori(0, NCH) as c:
                norm_scalar(act, b, c, s)
                for kk in range(DC):
                    act.wait_ge(turned, DC * c + kk + 1)
                    act.activation(b.xnT[:, kk, :], b.bank[kk][:, :], ACT.Copy).then_inc(copied, 1)
            act.wait_ge(shifted, 1)
            if l == 0:
                act.activation(expd[:, :, :], expd[:, :, :], ACT.Exp).then_inc(exped, 1)
            else:
                act.activation(expd[:, :, 0], expd[:, :, 0], ACT.Exp).then_inc(exped, 1)
                act.wait_ge(evac, NCH * (1 + TC))
                act.activation(b.shared[:, :, :], b.shared[:, :, :], ACT.Gelu).then_inc(act_done, 1)

        @block.tensor
        def _(pe):
            pe.wait_ge(loaded, NLOAD)
            with pe.Fori(0, NCH) as c:
                pe.wait_ge(s.normed, TC * c + TC)
                for kk in range(DC):
                    for j in range(TC):
                        mm = pe.transpose(b.bank[kk][:, j * P:(j + 1) * P], xn[:, j, kk * P:(kk + 1) * P],
                                          b.ident[:, :])
                    mm.then_inc(turned, 1)
                pe.wait_ge(copied, DC * c + DC)
                for j in range(TC):
                    for kk in range(DC):
                        mm = pe.matmul(b.bank[2][:, j * E:(j + 1) * E], b.xnT[:, kk, j * P:(j + 1) * P],
                                       gate_w[:, kk, :], start=(kk == 0), stop=(kk == DC - 1))
                mm.then_inc(prod, 1)
                if l == 1:
                    for j in range(TC):
                        for kk in range(DC):
                            mm = pe.matmul(b.bank[3 + j][:, 0:D], b.xnT[:, kk, j * P:(j + 1) * P],
                                           shared_w[:, kk, :], start=(kk == 0), stop=(kk == DC - 1))
                        mm.then_inc(prod, 1)
                pe.wait_ge(evac, (1 + TC * l) * (c + 1))
            pe.wait_ge(onehots, 1)
            flat = onehot.rearrange("p a e -> p (a e)")
            pe.matmul(b.bank[0][:, 0:NA * E], b.tri[:, :], flat, start=True, stop=True)
            pe.matmul(b.bank[1][:, 0:NA * E], b.ones[:, :], flat, start=True, stop=True).then_inc(counted, 1)

        @block.gpsimd
        def _(pool):
            with pool.Fori(0, NCH) as c:
                pool.wait_ge(s.normed, TC * c + TC)
                pool.tensor_copy(xall[:, bass.ds(c * TC, TC), :], xn[:, :, :]).then_inc(kept, 1)
            pool.wait_ge(kept, NCH)
            pool.wait_ge(placed, 1)
            for a in range(NA):
                pool.indirect_dma_start(b.xs[l][:, :], bass.IndirectOffsetOnAxis(ap=b.slot[:, a:a + 1], axis=0),
                                        xall[:, a % NT, :], None).then_inc(sent, 16)
            pool.wait_ge(sent, 16 * NA)

        @block.vector
        def _(dve):
            dve.wait_ge(loaded, NLOAD)
            flat = logits.rearrange("p t e -> p (t e)")
            with dve.Fori(0, NCH) as c:
                norm_vector(dve, b, c, s, lambda j: xn[:, j, :])
                per = 1 + TC * l
                dve.wait_ge(prod, per * c + 1)
                out = flat[:, bass.ds(c * TC * E, TC * E)]
                if l == 0:
                    dve.tensor_tensor(out, b.bank[2][:, 0:TC * E], logit_bias[:, :], ALU.add).then_inc(evac, 1)
                else:
                    dve.tensor_copy(out, b.bank[2][:, 0:TC * E]).then_inc(evac, 1)
                    for j in range(TC):
                        dve.wait_ge(prod, per * c + 2 + j)
                        dve.tensor_tensor(tile_of(b.shared, c, j), b.bank[3 + j][:, 0:D], shared_b[:, :],
                                          ALU.add).then_inc(evac, 1)
                dve.wait_ge(turned, DC * c + DC)
                dve.wait_ge(kept, c + 1)
            dve.wait_ge(evac, NCH * (1 + TC * l))
            count = [0]

            def link(ins):
                count[0] += 1
                ins.then_inc(chain, 1)
                dve.wait_ge(chain, count[0])

            for t in range(NT):
                ins = dve.max(best[:, t, :], logits[:, t, :])
                ins.then_inc(chain, 1)
            count[0] += NT
            dve.wait_ge(chain, count[0])
            for t in range(NT):
                dve.max_index(best_at[:, t, :], best[:, t, :], logits[:, t, :]).then_inc(chain, 1)
            count[0] += NT
            dve.wait_ge(chain, count[0])
            if l == 0:
                dve.tensor_tensor(expd[:, :, :], logits[:, :, :], best[:, :, 0:1].to_broadcast([P, NT, E]),
                                  ALU.subtract).then_inc(shifted, 1)
            else:
                dve.tensor_tensor(expd[:, :, 0], best[:, :, 1], best[:, :, 0], ALU.subtract).then_inc(shifted, 1)
            link(dve.tensor_copy(at_f[:, :, :], best_at[:, :, 0:top].rearrange("p t r -> p r t")))
            dve.tensor_tensor(onehot[:, :, :],
                              at_f.rearrange("p r (t a) -> p (r t) a", a=1).to_broadcast([P, NA, E]),
                              iota_e.rearrange("p (a e) -> p a e", a=1).to_broadcast([P, NA, E]),
                              ALU.is_equal).then_inc(onehots, 1)
            dve.wait_ge(exped, 1)
            if l == 0:
                link(dve.tensor_reduce(b.gate[:, 1, :], expd[:, :, :], AX.X, ALU.add))
                link(dve.reciprocal(b.gate[:, 0, :], b.gate[:, 1, :]))
            else:
                link(dve.tensor_scalar(b.gate[:, 1, :], expd[:, :, 0], 1.0, None, ALU.add))
                link(dve.reciprocal(b.gate[:, 0, :], b.gate[:, 1, :]))
                link(dve.tensor_tensor(b.gate[:, 1, :], expd[:, :, 0], b.gate[:, 0, :], ALU.mult))
            dve.wait_ge(counted, 1)
            link(dve.tensor_copy(totals.rearrange("p a e -> p (a e)"), b.bank[1][:, 0:NA * E]))
            for e in range(E):
                dve.tensor_tensor_scan(upto[:, e, :], b.ones[:, 0:NA], totals[:, :, e], 0.0,
                                       ALU.mult, ALU.add).then_inc(chain, 1)
            count[0] += E
            dve.wait_ge(chain, count[0])
            link(dve.tensor_tensor(fills[:, :, :], upto[:, :, NA - 1:NA].to_broadcast([P, E, NA]),
                                   iota_rows.rearrange("p (a n) -> p a n", a=1).to_broadcast([P, E, NA]),
                                   ALU.is_gt))
            link(dve.tensor_reduce(tiles[:, :], fills[:, :, :], AX.X, ALU.add))
            link(dve.tensor_tensor_scan(ends[:, :], b.ones[:, 0:E], tiles[:, :], 0.0, ALU.mult, ALU.add))
            link(dve.tensor_tensor(base[:, :], ends[:, :], tiles[:, :], ALU.subtract))
            link(dve.tensor_scalar(base[:, :], base[:, :], float(P), None, ALU.mult))
            link(dve.tensor_tensor(place.rearrange("p a e -> p (a e)"), b.bank[0][:, 0:NA * E],
                                   totals.rearrange("p a e -> p (a e)"), ALU.subtract))
            link(dve.tensor_tensor(place[:, :, :], place[:, :, :], upto.rearrange("p e a -> p a e"), ALU.add))
            link(dve.tensor_tensor(place[:, :, :], place[:, :, :],
                                   base.rearrange("p (a e) -> p a e", a=1).to_broadcast([P, NA, E]), ALU.add))
            link(dve.tensor_tensor(place[:, :, :], place[:, :, :], onehot[:, :, :], ALU.mult))
            link(dve.tensor_reduce(place_f[:, :], place[:, :, :], AX.X, ALU.add))
            dve.tensor_copy(b.slot[:, 0:NA], place_f[:, :]).then_inc(placed, 1)
            link(dve.tensor_tensor(owner[:, :, :],
                                   ends.rearrange("p (a e) -> p a e", a=1).to_broadcast([P, T, E]),
                                   iota_t.rearrange("p (t a) -> p t a", a=1).to_broadcast([P, T, E]),
                                   ALU.is_le))
            link(dve.tensor_reduce(owner_f[:, :], owner[:, :, :], AX.X, ALU.add))
            link(dve.tensor_scalar(b.texp[:, 0:T], owner_f[:, :], float(E - 1), None, ALU.min))
            dve.wait_ge(placed, 1)
            if l == 1:
                dve.wait_ge(act_done, 1)


def experts(nc, b, io, l):
    _, T = routing(l + 1)
    W = HID * (2 - l)
    b.used = b.expert_at
    w1 = [b.carve([P, DC, W]) for _ in range(2)]
    w2 = [b.carve([P, MC, D]) for _ in range(2)]
    b1 = [b.carve([P, MC]) for _ in range(2)]
    b2 = [b.carve([1, D]) for _ in range(2)]
    xt = [b.carve([P, D]) for _ in range(2)]
    xT = [b.carve([P, DC, P]) for _ in range(2)]
    gated = [b.carve([P, HID]) for _ in range(2)]
    h = [b.carve([P, MC, P]) for _ in range(2)]
    y = [b.carve([P, D]) for _ in range(2)]
    now = b.carve([1, 2], u32)
    n = f"e{l}_"
    named, turned, turned_out, up, active, hidden, down, y_out = (
        b.sem(n + x) for x in ("named", "turned", "turned_out", "up", "active", "hidden", "down", "y_out"))
    rows_in, up_in, down_in, stored = (
        [b.sem(f"{n}{x}{k}") for k in range(2)] for x in ("rows_in", "up_in", "down_in", "stored"))
    ND = 1 + 2 * l
    NH = 2
    TURN = b.bank[7]

    with nc.Block() as block:
        @block.gpsimd
        def _(pool):
            def name(t, k):
                pool.tensor_copy(now[0:1, k:k + 1], b.texp[0:1, bass.ds(t, 1)]).then_inc(named, 1)

            for k in range(2):
                name(k, k)
            with pool.Fori(0, T // 2 - 1) as p:
                for k in range(2):
                    pool.wait_ge(up, NH * (2 * p + k + 1))
                    name(2 * p + k + 2, k)

        @block.sync
        def _(sp):
            def load_up(t, k):
                sp.wait_ge(named, t + 1)
                sp.dma_start(xt[k], b.xs[l][bass.ds(t * P, P), :]).then_inc(rows_in[k], 16)
                e = sp.value_load(now[0:1, k:k + 1], min_val=0, max_val=E - 1)
                sp.dma_start(w1[k], io[f"w1_{l}"][bass.ds(e, 1)].rearrange("a (c p) n -> p (a c) n", p=P)
                             ).then_inc(up_in[k], 16)
                return e

            def load_down(e, k):
                if l == 1:
                    sp.dma_start(b1[k], io["b1"][bass.ds(e, 1)].rearrange("a p c -> p (a c)")
                                 ).then_inc(down_in[k], 16)
                    sp.dma_start(b2[k], io["b2"][bass.ds(e, 1), :]).then_inc(down_in[k], 16)
                sp.dma_start(w2[k], io[f"w2_{l}"][bass.ds(e, 1)].rearrange("a (c p) n -> p (a c) n", p=P)
                             ).then_inc(down_in[k], 16)

            def store(t, k):
                sp.wait_ge(y_out, t + 1)
                sp.dma_start(b.ys[l][bass.ds(t * P, P), :], y[k]).then_inc(stored[k], 16)

            for k in range(2):
                load_down(load_up(k, k), k)
            with sp.Fori(0, T // 2 - 1) as p:
                for k in range(2):
                    t = 2 * p + k
                    e = load_up(t + 2, k)
                    store(t, k)
                    load_down(e, k)
            for k in range(2):
                store(T - 2 + k, k)
            for k in range(2):
                sp.wait_ge(stored[k], 16 * (T // 2))

        @block.tensor
        def _(pe):
            def turn(t, k, p):
                pe.wait_ge(rows_in[k], 16 * (p + 1))
                if not (isinstance(t, int) and t < 1):
                    pe.wait_ge(turned_out, t)
                for kk in range(DC):
                    mm = pe.transpose(TURN[:, kk * P:(kk + 1) * P], xt[k][:, kk * P:(kk + 1) * P], b.ident[:, :])
                mm.then_inc(turned, 1)

            def up_half(t, k, half):
                for part in range(2 - l):
                    bank = b.bank[half + 2 * part] if l == 0 else b.bank[2 * k + half]
                    for m in range(MC // 2):
                        for kk in range(DC):
                            at = part * HID + (half * MC // 2 + m) * P
                            mm = pe.matmul(bank[:, m * P:(m + 1) * P], w1[k][:, kk, at:at + P], xT[k][:, kk, :],
                                           start=(kk == 0), stop=(kk == DC - 1))
                mm.then_inc(up, 1)

            def rise(t, k, p):
                turn(t, k, p)
                pe.wait_ge(up_in[k], 16 * (p + 1))
                pe.wait_ge(turned_out, t + 1)
                for half in range(NH):
                    before = 1 if l == 0 else 2
                    if not (isinstance(t, int) and t < before):
                        pe.wait_ge(hidden, NH * (t - before + 1))
                    up_half(t, k, half)

            def fall(t, k, p):
                pe.wait_ge(down_in[k], 16 * ND * (p + 1))
                pe.wait_ge(hidden, NH * (t + 1))
                if not (isinstance(t, int) and t < 2):
                    pe.wait_ge(y_out, t - 1)
                out = b.bank[4 + k]
                for m in range(MC):
                    mm = pe.matmul(out[:, 0:D], h[k][:, m, :], w2[k][:, m, :], start=(m == 0),
                                   stop=(l == 0 and m == MC - 1))
                if l == 1:
                    mm = pe.matmul(out[:, 0:D], b.ones[0:1, :], b2[k], start=False, stop=True)
                mm.then_inc(down, 1)

            def pair(p):
                rise(2 * p + 1, 1, p)
                fall(2 * p, 0, p)
                rise(2 * p + 2, 0, p + 1)
                fall(2 * p + 1, 1, p)

            rise(0, 0, 0)
            pair(0)
            with pe.Fori(1, T // 2 - 1) as p:
                pair(p)
            rise(T - 1, 1, T // 2 - 1)
            fall(T - 2, 0, T // 2 - 1)
            fall(T - 1, 1, T // 2 - 1)

        @block.scalar
        def _(act):
            def tile(p, k):
                t = 2 * p + k
                first = isinstance(p, int) and p == 0
                for half in range(NH):
                    act.wait_ge(up, NH * t + half + 1)
                    if l == 0:
                        if not first:
                            act.wait_ge(hidden, NH * (t - 1))
                        act.activation(gated[k][:, half * 512:(half + 1) * 512], b.bank[half][:, :],
                                       ACT.Silu).then_inc(active, 1)
                    else:
                        if not first:
                            act.wait_ge(down, t - 1)
                        act.wait_ge(down_in[k], 16 * ND * (p + 1))
                        for m in range(MC // 2):
                            at = half * MC // 2 + m
                            ins = act.activation(h[k][:, at, :], b.bank[2 * k + half][:, m * P:(m + 1) * P],
                                                 ACT.Gelu, bias=b1[k][:, at:at + 1])
                        ins.then_inc(hidden, 1)

            for k in range(2):
                tile(0, k)
            with act.Fori(1, T // 2) as p:
                for k in range(2):
                    tile(p, k)

        @block.vector
        def _(dve):
            def turn_out(t, k):
                dve.wait_ge(turned, t + 1)
                dve.tensor_copy(xT[k].rearrange("p a q -> p (a q)"), TURN[:, 0:D]).then_inc(turned_out, 1)

            def gate(t, k):
                for half in range(NH):
                    dve.wait_ge(active, NH * t + half + 1)
                    dve.tensor_tensor(h[k].rearrange("p a q -> p (a q)")[:, half * 512:(half + 1) * 512],
                                      gated[k][:, half * 512:(half + 1) * 512], b.bank[2 + half][:, :],
                                      ALU.mult).then_inc(hidden, 1)

            def out(t, k, p):
                dve.wait_ge(down, t + 1)
                dve.wait_ge(stored[k], 16 * p)
                dve.tensor_copy(y[k], b.bank[4 + k][:, 0:D]).then_inc(y_out, 1)

            def step(t, k, first=False):
                turn_out(t, k)
                if l == 0:
                    gate(t, k)

            step(0, 0)
            step(1, 1)
            out(0, 0, 0)
            step(2, 0)
            out(1, 1, 0)
            with dve.Fori(1, T // 2 - 1) as p:
                step(2 * p + 1, 1)
                out(2 * p, 0, p)
                step(2 * p + 2, 0)
                out(2 * p + 1, 1, p)
            step(T - 1, 1)
            out(T - 2, 0, T // 2 - 1)
            out(T - 1, 1, T // 2 - 1)


def combine(nc, b, io, l):
    top = l + 1
    NA, _ = routing(top)
    b.used = b.expert_at
    got = b.carve([P, NA, D])
    mixed = b.carve([P, NT, D])
    gamma = b.carve([P, D])
    beta = b.carve([P, D])
    xn = b.carve([P, TC, D])
    n = f"c{l}_"
    s = norm_sems(b, n)
    gathered, halved, mixes, loaded, scaled, summed, final, written = (b.sem(n + x) for x in (
        "gathered", "halved", "mixes", "loaded", "scaled", "summed", "final", "written"))
    with nc.Block() as block:
        @block.gpsimd
        def _(pool):
            for a in range(NA):
                pool.indirect_dma_start(got[:, a, :], None, b.ys[l][:, :],
                                        bass.IndirectOffsetOnAxis(ap=b.slot[:, a:a + 1], axis=0)
                                        ).then_inc(gathered, 16)

        if l == 0:
            @block.vector
            def _(dve):
                dve.wait_ge(gathered, 16 * NA)
                for t in range(NT):
                    dve.scalar_tensor_tensor(out=b.x[:, t, :], in0=got[:, t, :], scalar=b.gate[:, 0, t:t + 1],
                                             in1=b.x[:, t, :], op0=ALU.mult, op1=ALU.add).then_inc(mixes, 1)
                dve.wait_ge(mixes, NT)
            return

        @block.sync
        def _(sp):
            sp.dma_start(gamma, io["gamma"].rearrange("(a n) -> a n", a=1).to_broadcast([P, D])).then_inc(loaded, 16)
            sp.dma_start(beta, io["beta"].rearrange("(a n) -> a n", a=1).to_broadcast([P, D])).then_inc(loaded, 16)
            sp.wait_ge(final, NCH * TC)
            sp.dma_start(io["out"].rearrange("(t p) d -> p t d", p=P), b.x[:, :, :]).then_inc(written, 16)
            sp.wait_ge(written, 16)

        @block.scalar
        def _(act):
            act.preload_act_table_set(LN_EXP)
            with act.Fori(0, NCH) as c:
                norm_scalar(act, b, c, s)

        @block.vector
        def _(dve):
            dve.tensor_scalar(b.shared[:, :, :], b.shared[:, :, :], 0.5, None, ALU.mult).then_inc(halved, 1)
            dve.wait_ge(halved, 1)
            dve.wait_ge(gathered, 16 * NA)
            for t in range(NT):
                dve.scalar_tensor_tensor(out=mixed[:, t, :], in0=got[:, t, :], scalar=b.gate[:, 0, t:t + 1],
                                         in1=b.shared[:, t, :], op0=ALU.mult, op1=ALU.add).then_inc(mixes, 1)
            for t in range(NT):
                dve.wait_ge(mixes, NT + t)
                dve.scalar_tensor_tensor(out=mixed[:, t, :], in0=got[:, NT + t, :],
                                         scalar=b.gate[:, 1, t:t + 1], in1=mixed[:, t, :], op0=ALU.mult,
                                         op1=ALU.add).then_inc(mixes, 1)
            dve.wait_ge(mixes, 2 * NT)
            dve.wait_ge(loaded, 32)
            with dve.Fori(0, NCH) as c:
                norm_vector(dve, b, c, s, lambda j: xn[:, j, :], src=mixed)
                for j in range(TC):
                    dve.wait_ge(s.normed, TC * c + j + 1)
                    dve.tensor_tensor(xn[:, j, :], xn[:, j, :], gamma[:, :], ALU.mult).then_inc(scaled, 1)
                for j in range(TC):
                    dve.wait_ge(scaled, TC * c + j + 1)
                    dve.tensor_tensor(xn[:, j, :], xn[:, j, :], beta[:, :], ALU.add).then_inc(summed, 1)
                for j in range(TC):
                    dve.wait_ge(summed, TC * c + j + 1)
                    dve.tensor_tensor(tile_of(b.x, c, j), tile_of(b.x, c, j), xn[:, j, :],
                                      ALU.add).then_inc(final, 1)


def kernel(**inputs):
    import numpy as _np
    import concourse.bacc as _bacc
    from concourse import mybir as _mybir
    from concourse.bass_utils import run_bass_kernel_spmd as _run

    a = {k: _np.asarray(v) for k, v in inputs.items()}
    arrays = {"x": a["x"][0], "ctxT": a["ctx_1024"][0].T, "mask": a["mask_BxS2_bf1"].view(_np.uint8)}
    for l in range(2):
        for n in "qkvo":
            arrays[f"w{n}T{l}"] = a[f"L{l}_xattn_W{n}"].T
        for n in "qk":
            arrays[f"b{n}{l}"] = a[f"L{l}_xattn_b{n}"].reshape(DC, P).T
        for n in "vo":
            arrays[f"b{n}{l}"] = a[f"L{l}_xattn_b{n}"]
    arrays |= {"gate0": a["L0_ffn_router_w"], "gate_bias": a["L0_ffn_router_b"], "w1_0": a["L0_ffn_w1"],
               "w2_0": a["L0_ffn_w2"], "gate1": a["L1_ffn_gate_W"], "w1_1": a["L1_ffn_W1"],
               "w2_1": a["L1_ffn_W2"], "b1": a["L1_ffn_b1"].reshape(E, MC, P).transpose(0, 2, 1),
               "b2": a["L1_ffn_b2"], "shared_w": a["L1_ffn_shared_W"], "shared_b": a["L1_ffn_shared_b"],
               "gamma": a["L1_ffn_gamma"], "beta": a["L1_ffn_beta"]}
    arrays["iota"] = _np.stack([_np.arange(64), P * _np.arange(64)]).astype(_np.float32)
    arrays["tri"] = _np.triu(_np.ones((P, P), _np.float32), 1)
    kconst = _np.zeros((P, 2), _np.float32)
    rest = _np.float32(FILL)
    for r in range(3):
        part = (_np.array([rest]).view(_np.uint32) & _np.uint32(0xFFFF0000)).view(_np.float32)[0]
        rest = rest - part
        kconst[ROW_MASK + r] = (-part, part)
        kconst[ROW_MAX + r] = (0.0, -1.0)
    arrays["kconst"] = kconst
    arrays = {k: _np.ascontiguousarray(v) for k, v in arrays.items()}

    nc = _bacc.Bacc("TRN2", target_bir_lowering=False, num_devices=1)
    io = {k: nc.dram_tensor(f"in_{k}", v.shape, _mybir.dt.from_np(v.dtype), kind="ExternalInput").ap()
          for k, v in arrays.items()}
    io["out"] = nc.dram_tensor("out_x", (S, D), fp32, kind="ExternalOutput").ap()
    build(nc, io)
    r = _run(nc, [{f"in_{k}": v for k, v in arrays.items()}], core_ids=[0])
    return r.results[0]["out_x"].reshape(1, S, D)
```

```python
import concourse.bass as bass
from concourse import mybir
from contextlib import ExitStack

fp32 = mybir.dt.float32
bf16 = mybir.dt.bfloat16
i32 = mybir.dt.int32
u32 = mybir.dt.uint32
u8 = mybir.dt.uint8
ALU = mybir.AluOpType
ACT = mybir.ActivationFunctionType
AX = mybir.AxisListType

LN_EXP = "natural_log_exp_and_others"
P = 128
S = 2048
SK = 1601
D = 256
DC = D // P
H = 16
HD = D // H
E = 8
HID = 1024
MC = HID // P
EPS = 1e-5
FILL = -1e8

QC = 512
NCH = S // QC
TC = QC // P
NT = S // P
G = 4
HG = H // G
KT = (SK + P - 1) // P
KROWS = [min(P, SK - P * k) for k in range(KT)]
SKP = KT * P
KCOLS = [(n, min(512, SK - n)) for n in range(0, SK, 512)]

QPART = [0, 0, 0, 1, 1, 2]
KPART = [0, 1, 2, 0, 1, 0]
NB = len(QPART)
ROW_MASK = NB * HD
ROW_MAX = ROW_MASK + 3
ROWS_ALL = ROW_MAX + 3

U = HG * KT
UC = G * U
NW = 16
OUT1 = 3
NS1 = 3
PC2 = UC // 2


def routing(top):
    na = NT * top
    nt = na + E - 1
    return na, nt + nt % 2


STATS = TC + 6


class Buffers:
    pass


def build(nc, io, stop=99):
    b = Buffers()
    ctx = ExitStack()
    with ctx:
        def sb(name, shape, dt=fp32):
            return ctx.enter_context(nc.sbuf_tensor(name, shape, dt))

        layer_sems = []

        def sem(name):
            layer_sems.append(nc.alloc_semaphore(name=name))
            return layer_sems[-1]

        b.sem = sem
        b.x = sb("x_res", [P, NT, D])
        b.ident = sb("ident", [P, P])
        b.identb = sb("identb", [P, P], bf16)
        b.tri = sb("tri", [P, P])
        b.ones = sb("ones", [P, P])
        b.kconst = sb("kconst", [P, 2])
        b.wq = sb("wq", [P, 2, DC, D])
        b.wk = sb("wk", [P, 2, DC, D])
        b.wv = sb("wv", [P, 2, DC, D])
        b.wo = sb("wo", [P, 2, DC, D])
        b.bq = sb("bq", [P, 2, DC])
        b.bk = sb("bk", [P, 2, DC])
        b.bv = sb("bv", [P, 2, D])
        b.bo = sb("bo", [P, 2, D])
        b.stats = sb("stats", [P, TC, 6])
        b.mv = sb("mv", [P, TC, 2])
        b.var = sb("var", [P, TC])
        b.rstd = sb("rstd", [P, TC])
        b.newt = sb("newt", [P, TC])
        b.xnT = sb("xnT", [P, DC, QC])
        arena = sb("arena", [P, 41000])
        b.used = 0

        def carve(shape, dt=fp32, at=None):
            n = 1
            for s in shape[1:]:
                n *= s
            words = n if dt in (fp32, i32, u32) else (n + 1) // 2 if dt == bf16 else (n + 3) // 4
            start = b.used if at is None else at
            b.used = start + words
            assert b.used <= 41000, b.used
            v = arena[:shape[0], start:start + words]
            if dt != fp32:
                v = v.bitcast(dt)
            v = v[:, 0:n]
            if len(shape) == 3:
                v = v.rearrange("p (a b) -> p a b", a=shape[1])
            if len(shape) == 4:
                v = v.rearrange("p (a b c) -> p a b c", a=shape[1], b=shape[2])
            return v

        b.carve = carve
        psum = ctx.enter_context(nc.psum_tensor("psum", [P, 8 * 512], fp32))
        b.psum = psum
        b.bank = [psum[:, 512 * i:512 * (i + 1)] for i in range(8)]
        b.slot = sb("slot", [P, 2 * NT], u32)
        b.gate = sb("gate", [P, 2, NT])
        b.texp = sb("texp", [P, 40], u32)

        b.qd = [nc.dram_tensor(f"q_parts{l}", (3, D, S), bf16, kind="Internal").ap() for l in range(2)]
        b.kd = [nc.dram_tensor(f"k_parts{l}", (3, D, SK), bf16, kind="Internal").ap() for l in range(2)]
        b.q32 = nc.dram_tensor("q32", (D, S), fp32, kind="Internal").ap()
        b.xs = [nc.dram_tensor(f"sorted_in{l}", (routing(l + 1)[1] * P, D), fp32, kind="Internal").ap()
                for l in range(2)]
        b.ys = [nc.dram_tensor(f"sorted_out{l}", (routing(l + 1)[1] * P, D), fp32, kind="Internal").ap()
                for l in range(2)]

        phases = [lambda: setup(nc, b, io)]
        for l in range(2):
            phases += [lambda l=l: keys_values(nc, b, io, l), lambda l=l: queries(nc, b, io, l),
                       lambda l=l: (attention0 if l == 0 else attention1)(nc, b, io),
                       lambda l=l: route(nc, b, io, l), lambda l=l: experts(nc, b, io, l),
                       lambda l=l: combine(nc, b, io, l)]
        for n, ph in enumerate(phases):
            if n <= stop:
                ph()
            if n == len(phases) // 2:
                nc.clear_and_free_semaphores(layer_sems)
                layer_sems.clear()
                nc.all_engine_barrier()
        if stop < len(phases) - 1:
            dump(nc, b, io)


def dump(nc, b, io):
    s = b.sem("dump")
    with nc.Block() as block:
        @block.sync
        def _(sp):
            sp.dma_start(io["out"].rearrange("(t p) d -> p t d", p=P), b.x[:, :, :]).then_inc(s, 16)
            sp.wait_ge(s, 16)


def setup(nc, b, io):
    zeros = b.carve([P, 1024], at=0)
    loaded, cleared, zero, made = (b.sem(n) for n in ("su_loaded", "su_cleared", "su_zero", "su_made"))
    with nc.Block() as block:
        @block.sync
        def _(sp):
            loads = [(b.x[:, :, :], io["x"].rearrange("(t p) d -> p t d", p=P)),
                     (b.kconst[:, :], io["kconst"]), (b.tri[:, :], io["tri"])]
            for l in range(2):
                for w, n in ((b.wq, "wqT"), (b.wk, "wkT"), (b.wv, "wvT"), (b.wo, "woT")):
                    loads.append((w[:, l], io[f"{n}{l}"].rearrange("(c p) n -> p c n", p=P)))
                for w, n in ((b.bv, "bv"), (b.bo, "bo")):
                    loads.append((w[:, l], io[f"{n}{l}"].rearrange("(a n) -> a n", a=1).to_broadcast([P, D])))
                for w, n in ((b.bq, "bq"), (b.bk, "bk")):
                    loads.append((w[:, l], io[f"{n}{l}"]))
            for dst, src in loads:
                sp.dma_start(dst, src).then_inc(loaded, 16)
            sp.wait_ge(zero, 1)
            n = 0
            for l in range(2):
                rows = b.xs[l].shape[0] // P
                flat = b.xs[l].rearrange("(p a) d -> p (a d)", p=P)
                for at in range(0, rows * D, 1024):
                    sp.dma_start(flat[:, at:at + 1024], zeros[:, :]).then_inc(cleared, 16)
                    n += 1
            sp.wait_ge(loaded, 16 * len(loads))
            sp.wait_ge(cleared, 16 * n)

        @block.gpsimd
        def _(pool):
            pool.memset(b.ident[:, :], 0.0).then_inc(made, 1)
            pool.memset(b.identb[:, :], 0.0).then_inc(made, 1)
            pool.memset(b.ones[:, :], 1.0).then_inc(made, 1)
            pool.wait_ge(made, 3)
            for m in (b.ident, b.identb):
                pool.affine_select(out=m[:, :], in_=m[:, :], compare_op=ALU.not_equal, fill=1.0, base=0,
                                   pattern=[[-1, P]], channel_multiplier=1).then_inc(made, 1)
            pool.wait_ge(made, 5)

        @block.vector
        def _(dve):
            dve.memset(zeros[:, :], 0.0).then_inc(zero, 1)


def keys_values(nc, b, io, l):
    b.used = 0
    b.ks = b.carve([P, H, SKP], bf16)
    b.v = b.carve([P, KT, H * 32])
    b.lin = b.carve([P, H * 32])
    b.attn_at = b.used
    if l == 0:
        ktok = b.carve([P, KT, D])
        bk_row = b.carve([P, D])
        own = b.carve([P, H // DC])
    ctxT = b.carve([P, DC, SK])
    kf = b.carve([P, SK])
    rest = b.carve([P, SK])
    parts = b.carve([P, 3, SKP], bf16)
    mask = b.carve([P, SKP])
    mask8 = b.carve([P, SK], u8)
    n = f"kv{l}_"
    loaded, prod, evac, chain, ready, stored, placed, vprod, vevac, vzero = (b.sem(n + x) for x in (
        "loaded", "prod", "evac", "chain", "ready", "stored", "placed", "vprod", "vevac", "vzero"))
    lin_made, lin_out = b.sem(n + "lin_made"), b.sem(n + "lin_out")
    NVE = 2 - l
    NLOAD = 32 if l else 64
    with nc.Block() as block:
        @block.sync
        def _(sp):
            sp.dma_start(ctxT, io["ctxT"].rearrange("(c p) n -> p c n", p=P)).then_inc(loaded, 16)
            sp.dma_start(mask8, io["mask"].to_broadcast([P, SK])).then_inc(loaded, 16)
            if l == 0:
                sp.dma_start(bk_row, io["bk_row"].to_broadcast([P, D])).then_inc(loaded, 16)
                sp.dma_start(own, io["own"]).then_inc(loaded, 16)
            for m in range(DC):
                sp.wait_ge(ready, m + 1)
                sp.dma_start(b.kd[l][:, m * P:(m + 1) * P, :].rearrange("r p n -> p r n"),
                             parts[:, :, 0:SK]).then_inc(stored, 16)
                sp.wait_ge(stored, 16 * (m + 1))
            sp.wait_ge(vzero, 5)
            for r in range(NB):
                sp.dma_start(b.ks[r * HD:(r + 1) * HD, :, 0:SK],
                             b.kd[l][KPART[r]].rearrange("(h d) n -> d h n", d=HD)).then_inc(placed, 16)
            sp.wait_ge(placed, 16 * NB)

        @block.tensor
        def _(pe):
            pe.wait_ge(loaded, NLOAD)
            u = 0
            for m in range(DC):
                for at, width in KCOLS:
                    if u >= 4:
                        pe.wait_ge(evac, u - 3)
                    for kk in range(DC):
                        mm = pe.matmul(b.bank[u % 4][:, 0:width], b.wk[:, l, kk, m * P:(m + 1) * P],
                                       ctxT[:, kk, at:at + width], start=(kk == 0), stop=(kk == DC - 1))
                    mm.then_inc(prod, 1)
                    u += 1
            for k in range(KT):
                if k >= 4:
                    pe.wait_ge(vevac, NVE * (k - 3))
                for side, w in enumerate((b.wv, b.wk)[:NVE]):
                    for kk in range(DC):
                        mm = pe.matmul(b.bank[4 + k % 4][0:KROWS[k], side * D:(side + 1) * D],
                                       ctxT[:, kk, k * P:k * P + KROWS[k]], w[:, l, kk, :],
                                       start=(kk == 0), stop=(kk == DC - 1))
                mm.then_inc(vprod, 1)
            if l == 0:
                pe.wait_ge(vzero, 5)
                pe.wait_ge(vevac, NVE * KT)
                for m in range(DC):
                    for k in range(KT):
                        mm = pe.matmul(b.bank[m][:, 0:H * 32 // DC], ktok[0:KROWS[k], k, m * P:(m + 1) * P],
                                       b.v[0:KROWS[k], k, m * H * 32 // DC:(m + 1) * H * 32 // DC],
                                       start=(k == 0), stop=(k == KT - 1))
                    mm.then_inc(lin_made, 1)

        @block.gpsimd
        def _(pool):
            v4 = b.v.rearrange("p k (h c) -> p (k h) c", c=32)
            full = (KT - 1) * H
            pool.memset(v4[:, 0:full, 16:32], 0.0).then_inc(vzero, 1)
            pool.wait_ge(vzero, 1)
            pool.memset(v4[:, full:KT * H, :], 0.0).then_inc(vzero, 1)
            pool.wait_ge(vzero, 2)
            pool.memset(v4[:, 0:full, 16:17], 1.0).then_inc(vzero, 1)
            pool.wait_ge(vzero, 3)
            pool.memset(v4[0:KROWS[-1], full:KT * H, 16:17], 1.0).then_inc(vzero, 1)
            pool.wait_ge(vzero, 4)
            pool.memset(b.ks[0:ROW_MASK, :, SK - 1:SKP], 0.0).then_inc(vzero, 1)
            pool.wait_ge(vzero, 5)

        @block.vector
        def _(dve):
            count = [0]

            def link(ins):
                count[0] += 1
                ins.then_inc(chain, 1)
                dve.wait_ge(chain, count[0])

            dve.wait_ge(loaded, NLOAD)
            link(dve.memset(mask[:, SK:SKP], 0.0))
            link(dve.tensor_copy(mask[:, 0:SK], mask8[:, :]))
            if l == 1:
                rows = slice(ROW_MASK, P)
                for h in range(H):
                    dve.tensor_scalar(b.ks[rows, h, :], mask[rows, :], b.kconst[rows, 0:1],
                                      b.kconst[rows, 1:2], ALU.mult, ALU.add).then_inc(chain, 1)
                count[0] += H
                dve.wait_ge(chain, count[0])
            u = 0
            for m in range(DC):
                for at, width in KCOLS:
                    dve.wait_ge(prod, u + 1)
                    if l == 0:
                        ins = dve.tensor_scalar(kf[:, at:at + width], b.bank[u % 4][:, 0:width],
                                                b.bk[:, l, m:m + 1], None, ALU.add)
                    else:
                        ins = dve.scalar_tensor_tensor(out=kf[:, at:at + width], in0=b.bank[u % 4][:, 0:width],
                                                       scalar=b.bk[:, l, m:m + 1], in1=mask[:, at:at + width],
                                                       op0=ALU.add, op1=ALU.mult)
                    ins.then_inc(evac, 1)
                    u += 1
                dve.wait_ge(evac, u)
                if m >= 1:
                    dve.wait_ge(stored, 16 * m)
                src = kf
                for r in range(3):
                    ins = dve.tensor_copy(parts[:, r, 0:SK], src[:, :])
                    if r == 2:
                        ins.then_inc(ready, 1)
                    else:
                        link(ins)
                        link(dve.tensor_tensor(rest[:, :], src[:, :], parts[:, r, 0:SK], ALU.subtract))
                        src = rest
            dve.wait_ge(vzero, 2)
            for k in range(KT):
                dve.wait_ge(vprod, k + 1)
                n = KROWS[k]
                dve.tensor_tensor(b.v[0:n, k, :].rearrange("p (h c) -> p h c", c=32)[:, :, 0:HD],
                                  b.bank[4 + k % 4][0:n, 0:D].rearrange("p (h c) -> p h c", c=HD),
                                  b.bv[0:n, l, :].rearrange("p (h c) -> p h c", c=HD),
                                  ALU.add).then_inc(vevac, 1)
                if l == 0:
                    dve.tensor_tensor(ktok[0:n, k, :], b.bank[4 + k % 4][0:n, D:2 * D], bk_row[0:n, :],
                                      ALU.add).then_inc(vevac, 1)
            dve.wait_ge(vevac, NVE * KT)
            if l == 0:
                for m in range(DC):
                    dve.wait_ge(lin_made, m + 1)
                    w = H * 32 // DC
                    dve.tensor_tensor(b.lin[:, m * w:(m + 1) * w].rearrange("p (h c) -> p h c", c=32),
                                      b.bank[m][:, 0:w].rearrange("p (h c) -> p h c", c=32),
                                      own.rearrange("p (h a) -> p h a", a=1).to_broadcast([P, H // DC, 32]),
                                      ALU.mult).then_inc(lin_out, 1)
                dve.wait_ge(lin_out, DC)


def norm_vector(dve, b, c, s, xn, src=None):
    src = b.x if src is None else src
    for j in range(TC):
        dve.bn_stats(b.stats[:, j, :], src[:, bass.ds(c * TC + j, 1), :].rearrange("p a d -> p (a d)")
                     ).then_inc(s.stat, 1)
    dve.wait_ge(s.stat, c * STATS + TC)
    even, odd = b.stats[:, :, 0:3], b.stats[:, :, 3:6]
    dve.tensor_tensor(b.mv[:, :, 0], even[:, :, 1], odd[:, :, 1], ALU.add).then_inc(s.stat, 1)
    dve.tensor_tensor(b.mv[:, :, 1], even[:, :, 1], odd[:, :, 1], ALU.subtract).then_inc(s.stat, 1)
    dve.tensor_tensor(b.var[:, :], even[:, :, 2], odd[:, :, 2], ALU.add).then_inc(s.stat, 1)
    dve.wait_ge(s.stat, c * STATS + TC + 3)
    dve.tensor_scalar(b.mv[:, :, 0], b.mv[:, :, 0], 0.5, None, ALU.mult).then_inc(s.stat, 1)
    dve.scalar_tensor_tensor(out=b.mv[:, :, 1], in0=b.mv[:, :, 1], scalar=0.25, in1=b.mv[:, :, 1],
                             op0=ALU.mult, op1=ALU.mult).then_inc(s.stat, 1)
    dve.tensor_scalar(b.var[:, :], b.var[:, :], 1.0 / D, EPS, ALU.mult, ALU.add).then_inc(s.stat, 1)
    dve.wait_ge(s.stat, c * STATS + STATS)
    dve.tensor_tensor(b.var[:, :], b.var[:, :], b.mv[:, :, 1], ALU.add).then_inc(s.vare, 1)
    dve.wait_ge(s.root, 2 * c + 2)
    dve.tensor_tensor(b.newt[:, :], b.rstd[:, :], b.rstd[:, :], ALU.mult).then_inc(s.newton, 1)
    dve.wait_ge(s.newton, c * 4 + 1)
    dve.tensor_tensor(b.newt[:, :], b.newt[:, :], b.var[:, :], ALU.mult).then_inc(s.newton, 1)
    dve.wait_ge(s.newton, c * 4 + 2)
    dve.tensor_scalar(b.newt[:, :], b.newt[:, :], -0.5, 1.5, ALU.mult, ALU.add).then_inc(s.newton, 1)
    dve.wait_ge(s.newton, c * 4 + 3)
    dve.tensor_tensor(b.rstd[:, :], b.rstd[:, :], b.newt[:, :], ALU.mult).then_inc(s.newton, 1)
    dve.wait_ge(s.newton, c * 4 + 4)
    for j in range(TC):
        dve.tensor_scalar(xn(j), src[:, bass.ds(c * TC + j, 1), :].rearrange("p a d -> p (a d)"),
                          b.mv[:, j, 0:1], b.rstd[:, j:j + 1], ALU.subtract, ALU.mult).then_inc(s.normed, 1)


def norm_scalar(act, b, c, s):
    act.wait_ge(s.vare, c + 1)
    act.activation(b.rstd[:, :], b.var[:, :], ACT.Ln).then_inc(s.root, 1)
    act.wait_ge(s.root, 2 * c + 1)
    act.activation(b.rstd[:, :], b.rstd[:, :], ACT.Exp, scale=-0.5).then_inc(s.root, 1)


def norm_sems(b, n):
    s = Buffers()
    s.stat, s.vare, s.root, s.newton, s.normed = (b.sem(n + x) for x in (
        "stat", "vare", "root", "newton", "normed"))
    return s


def queries(nc, b, io, l):
    b.used = b.attn_at
    xn = b.carve([P, TC, D])
    qf = b.carve([P, DC, QC])
    rest = b.carve([P, QC])
    parts = b.carve([P, 3, DC, QC], bf16)
    n = f"q{l}_"
    s = norm_sems(b, n)
    turned, copied, prod, evac, chain, ready, stored = (b.sem(n + x) for x in (
        "turned", "copied", "prod", "evac", "chain", "ready", "stored"))
    NST = 16 * (4 - l)
    with nc.Block() as block:
        @block.sync
        def _(sp):
            with sp.Fori(0, NCH) as c:
                sp.wait_ge(ready, 2 * c + 2)
                for r in range(3):
                    sp.dma_start(b.qd[l][r, :, bass.ds(c * QC, QC)].rearrange("(m p) q -> p m q", p=P),
                                 parts[:, r]).then_inc(stored, 16)
                if l == 0:
                    sp.dma_start(b.q32[:, bass.ds(c * QC, QC)].rearrange("(m p) q -> p m q", p=P), qf
                                 ).then_inc(stored, 16)
            sp.wait_ge(stored, NST * NCH)

        @block.scalar
        def _(act):
            act.preload_act_table_set(LN_EXP)
            with act.Fori(0, NCH) as c:
                norm_scalar(act, b, c, s)
                for kk in range(DC):
                    act.wait_ge(turned, DC * c + kk + 1)
                    act.activation(b.xnT[:, kk, :], b.bank[kk][:, :], ACT.Copy).then_inc(copied, 1)

        @block.tensor
        def _(pe):
            with pe.Fori(0, NCH) as c:
                pe.wait_ge(s.normed, TC * c + TC)
                for kk in range(DC):
                    for j in range(TC):
                        mm = pe.transpose(b.bank[kk][:, j * P:(j + 1) * P], xn[:, j, kk * P:(kk + 1) * P],
                                          b.ident[:, :])
                    mm.then_inc(turned, 1)
                pe.wait_ge(copied, DC * c + DC)
                for m in range(DC):
                    for kk in range(DC):
                        mm = pe.matmul(b.bank[2 + m][:, :], b.wq[:, l, kk, m * P:(m + 1) * P],
                                       b.xnT[:, kk, :], start=(kk == 0), stop=(kk == DC - 1))
                    mm.then_inc(prod, 1)
                pe.wait_ge(evac, DC * c + DC)

        @block.vector
        def _(dve):
            with dve.Fori(0, NCH) as c:
                norm_vector(dve, b, c, s, lambda j: xn[:, j, :])
                k = 0
                for m in range(DC):
                    dve.wait_ge(prod, DC * c + m + 1)
                    dve.tensor_scalar(qf[:, m, :], b.bank[2 + m][:, :], b.bq[:, l, m:m + 1], HD ** -0.5,
                                      ALU.add, ALU.mult).then_inc(evac, 1)
                    dve.wait_ge(evac, DC * c + m + 1)
                    src = qf[:, m, :]
                    for r in range(3):
                        ins = dve.tensor_copy(parts[:, r, m, :], src)
                        if r == 2:
                            ins.then_inc(ready, 1)
                        else:
                            ins.then_inc(chain, 1)
                            k += 1
                            dve.wait_ge(chain, 8 * c + k)
                            dve.tensor_tensor(rest[:, :], src, parts[:, r, m, :],
                                              ALU.subtract).then_inc(chain, 1)
                            k += 1
                            dve.wait_ge(chain, 8 * c + k)
                            src = rest[:, :]
                    dve.wait_ge(ready, 2 * c + m + 1)
                assert k == 8
                dve.wait_ge(turned, DC * c + DC)
                dve.wait_ge(stored, NST * c + NST)


def load_queries(sp, b, l, q, c, g, loaded):
    for r in range(NB):
        sp.dma_start(q[r * HD:(r + 1) * HD, g * HG:(g + 1) * HG, :],
                     b.qd[l][QPART[r], g * HG * HD:(g + 1) * HG * HD, bass.ds(c * QC, QC)]
                     .rearrange("(h d) q -> d h q", d=HD)).then_inc(loaded[g], 16)


def key_tile(i):
    g, r = divmod(i, U)
    k, j = divmod(r, HG)
    return g, k, j


def value_product(pe, b, ring, nw, g, k, acc, done):
    for j in range(HG):
        h = g * HG + j
        i = (g * KT + k) * HG + j
        mm = pe.matmul(acc[32 * j:32 * j + 32, :], b.v[:, k, 32 * h:32 * h + 32],
                       ring[:, i % nw, :], start=(k == 0), stop=(k == KT - 1))
    mm.then_inc(done, 1)


def finish_sems(b, n):
    f = Buffers()
    f.acc_out, f.turned, f.recip, f.scaled, f.turned2, f.copied2, f.proj, f.added, f.resid = (
        b.sem(n + x) for x in ("acc_out", "turned", "recip", "scaled", "turned2", "copied2", "proj",
                               "added", "resid"))
    return f


class Finish:

    def __init__(self, b, l, f, accs):
        self.b, self.l, self.f, self.accs = b, l, f, accs
        self.rsum = b.carve([P, H])
        self.att = b.carve([P, D])
        self.attT = b.carve([P, DC, P])
        self.out = b.carve([P, D])

    def tensor(self, pe, step, c, t, o):
        b, f = self.b, self.f
        if step == 1:
            pe.wait_ge(f.acc_out, G * c + G)
            for g in range(G):
                mm = pe.transpose(o[:, g * P:(g + 1) * P], self.accs[:, g, t * P:(t + 1) * P], b.ident[:, :])
            mm.then_inc(f.turned, 1)
        elif step == 2:
            pe.wait_ge(f.scaled, TC * c + t + 1)
            for kk in range(DC):
                mm = pe.transpose(o[:, kk * P:(kk + 1) * P], self.att[:, kk * P:(kk + 1) * P], b.ident[:, :])
            mm.then_inc(f.turned2, 1)
        else:
            pe.wait_ge(f.copied2, TC * c + t + 1)
            for kk in range(DC):
                mm = pe.matmul(o[:, 0:D], self.attT[:, kk, :], b.wo[:, self.l, kk, :],
                               start=(kk == 0), stop=(kk == DC - 1))
            mm.then_inc(f.proj, 1)

    def vector(self, dve, step, c, t, o):
        b, f = self.b, self.f
        if step == 1:
            dve.wait_ge(f.turned, TC * c + t + 1)
            rows = o[:, 0:32 * H].rearrange("p (h c) -> p h c", c=32)
            dve.reciprocal(self.rsum[:, :], rows[:, :, HD]).then_inc(f.recip, 1)
            dve.wait_ge(f.recip, TC * c + t + 1)
            dve.tensor_tensor(self.att.rearrange("p (h c) -> p h c", c=HD), rows[:, :, 0:HD],
                              self.rsum.rearrange("p (h a) -> p h a", a=1).to_broadcast([P, H, HD]),
                              ALU.mult).then_inc(f.scaled, 1)
        elif step == 3:
            dve.wait_ge(f.proj, TC * c + t + 1)
            dve.tensor_tensor(self.out[:, :], o[:, 0:D], b.bo[:, self.l, :], ALU.add).then_inc(f.added, 1)
            dve.wait_ge(f.added, TC * c + t + 1)
            row = tile_of(b.x, c, t)
            dve.tensor_tensor(row, row, self.out[:, :], ALU.add).then_inc(f.resid, 1)

    def scalar(self, act, step, c, t, o):
        if step == 2:
            act.wait_ge(self.f.turned2, TC * c + t + 1)
            act.activation(self.attT.rearrange("p a q -> p (a q)"), o[:, 0:D], ACT.Copy
                           ).then_inc(self.f.copied2, 1)

    def turned_back(self, dve, step, c, t, o):
        if step == 2:
            dve.wait_ge(self.f.turned2, TC * c + t + 1)
            dve.tensor_copy(self.attT.rearrange("p a q -> p (a q)"), o[:, 0:D]).then_inc(self.f.copied2, 1)

    def freed(self, step, c, t):
        return ((self.f.scaled, self.f.copied2, self.f.added)[step - 1], TC * c + t + 1)


FSTEPS = [(t, step) for t in range(TC) for step in (1, 2, 3)]


def attention0(nc, b, io):
    b.used = b.attn_at
    q = b.carve([P, H, QC], bf16)
    q32 = b.carve([P, DC, QC])
    NN, NE = 2, 4
    nring = b.carve([P, NN * HG, QC])
    ering = b.carve([P, NE * HG, QC])
    accs = b.carve([P, G, QC])
    n = "a0_"
    scored, clipped, logged, exped, valued_n, valued_e = (b.sem(n + x) for x in (
        "scored", "clipped", "logged", "exped", "valued_n", "valued_e"))
    loaded = [b.sem(f"{n}loaded{g}") for g in range(G)]
    loaded32 = [b.sem(f"{n}loaded32_{m}") for m in range(DC)]
    f = finish_sems(b, n)
    fin = Finish(b, 0, f, accs)
    NV = G * KT
    PG = U // 2
    NS = 2
    ACC, FIN = [b.bank[4], b.bank[5]], b.bank[6]
    LAG_N, LAG_E = 1, 4
    OUT = 2 * LAG_E + 1
    AT = [OUT + 1 + 2 * n for n in range(len(FSTEPS))]
    assert AT[-1] < PG + OUT and PC2 % NS == 0 and NV % NN == 0 and NV % NE == 0

    def unit(x, v):
        return x.rearrange("p a q -> p (a q)")[:, v % (x.shape[1] // HG) * HG * QC:][:, 0:HG * QC]

    def pair(i):
        return b.psum[:, 2 * QC * (i % NS):2 * QC * (i % NS + 1)]

    with nc.Block() as block:
        @block.sync
        def _(sp):
            def load32(c, m):
                sp.dma_start(q32[:, m, :], b.q32[m * P:(m + 1) * P, bass.ds(c * QC, QC)]
                             ).then_inc(loaded32[m], 16)

            for g in range(G):
                load_queries(sp, b, 0, q, 0, g, loaded)
                if g % 2 == 0:
                    load32(0, g // 2)
            with sp.Fori(1, NCH) as c:
                for g in range(G):
                    sp.wait_ge(scored, (c - 1) * PC2 + (g + 1) * PG)
                    load_queries(sp, b, 0, q, c, g, loaded)
                    if g % 2 == 1:
                        load32(c, g // 2)

        @block.tensor
        def _(pe):
            def times_values(ring, v, stop=False):
                g, k = divmod(v % NV, KT)
                for j in range(HG):
                    h = g * HG + j
                    mm = pe.matmul(ACC[g % 2][32 * j:32 * j + 32, :], b.v[:, k, 32 * h:32 * h + 32],
                                   unit(ring, v)[:, j * QC:(j + 1) * QC], start=False, stop=stop)
                return mm

            def values_n(c, v):
                first = isinstance(c, int) and c == 0
                g, k = divmod(v % NV, KT)
                if k == 0:
                    if not (first and g < 2):
                        pe.wait_ge(f.acc_out, G * (c + v // NV) + g - 1)
                    pe.wait_ge(loaded32[g // 2], 16 * (c + v // NV + 1))
                    for j in range(HG):
                        h = g * HG + j
                        pe.matmul(ACC[g % 2][32 * j:32 * j + 32, :], b.lin[:, 32 * h:32 * h + 32],
                                  q32[:, g // 2, :], start=True, stop=False)
                pe.wait_ge(clipped, c * PC2 + 2 * (v + 1))
                times_values(nring, v).then_inc(valued_n, 1)

            def values_e(c, v):
                pe.wait_ge(exped, c * NV + v + 1)
                times_values(ering, v, stop=v % KT == KT - 1).then_inc(valued_e, 1)

            def finish(c, t, step):
                n = FSTEPS.index((t, step))
                if n >= 1:
                    s, v = fin.freed(FSTEPS[n - 1][1], c, FSTEPS[n - 1][0])
                    pe.wait_ge(s, v)
                fin.tensor(pe, step, c, t, FIN)

            def chunk(c, first):
                for i in range(PC2):
                    if i % PG == 0:
                        pe.wait_ge(loaded[i // PG], 16 * NB * (c + 1))
                    if i >= NS or not first:
                        pe.wait_ge(clipped, c * PC2 + i - NS + 1)
                    for u in (2 * i, 2 * i + 1):
                        g, k, j = key_tile(u)
                        mm = pe.matmul(pair(i)[:, QC * (u % 2):QC * (u % 2 + 1)],
                                       b.ks[0:ROW_MASK, g * HG + j, k * P:(k + 1) * P],
                                       q[0:ROW_MASK, g * HG + j, :], start=True, stop=True)
                    mm.then_inc(scored, 1)
                    if i % 2 == 1:
                        v = i // 2
                        if v >= LAG_N or not first:
                            values_n(c, v - LAG_N)
                        if v >= LAG_E or not first:
                            values_e(c, v - LAG_E)
                    if not first and i in AT:
                        t, step = FSTEPS[AT.index(i)]
                        finish(c - 1, t, step)

            chunk(0, True)
            with pe.Fori(1, NCH) as c:
                chunk(c, False)
            for v in range(NV - LAG_N, NV):
                values_n(NCH - 1, v)
            for v in range(NV - LAG_E, NV):
                values_e(NCH - 1, v)
            for t, step in FSTEPS:
                finish(NCH - 1, t, step)

        @block.vector
        def _(dve):
            def sums_out(c, g):
                dve.wait_ge(valued_e, c * NV + (g + 1) * KT)
                dve.tensor_copy(accs[:, g % G, :], ACC[g % 2]).then_inc(f.acc_out, 1)

            def chunk(c, first):
                for i in range(PC2):
                    v = i // 2
                    dve.wait_ge(scored, c * PC2 + i + 1)
                    if i % 2 == 0 and (v >= NN or not first):
                        dve.wait_ge(valued_n, c * NV + v - NN + 1)
                        dve.wait_ge(logged, c * NV + v - NN + 1)
                    dve.tensor_scalar(unit(nring, v)[:, 2 * QC * (i % 2):2 * QC * (i % 2 + 1)], pair(i), -1.0, 0.0,
                                      ALU.mult, ALU.max).then_inc(clipped, 1)
                    if i % PG == OUT and (i >= PG or not first):
                        if i // PG == 1 and not first:
                            dve.wait_ge(f.turned, TC * c)
                        sums_out(c, i // PG - 1)
                    if not first and i in AT:
                        t, step = FSTEPS[AT.index(i)]
                        fin.vector(dve, step, c - 1, t, FIN)
                        fin.turned_back(dve, step, c - 1, t, FIN)

            chunk(0, True)
            with dve.Fori(1, NCH) as c:
                chunk(c, False)
            sums_out(NCH - 1, G - 1)
            for t, step in FSTEPS:
                fin.vector(dve, step, NCH - 1, t, FIN)
                fin.turned_back(dve, step, NCH - 1, t, FIN)
            dve.wait_ge(f.resid, TC * NCH)

        @block.scalar
        def _(act):
            act.preload_act_table_set(LN_EXP)

            def log(c, v, first):
                act.wait_ge(clipped, c * PC2 + 2 * (v + 1))
                if v >= NE or not first:
                    act.wait_ge(valued_e, c * NV + v - NE + 1)
                act.activation(unit(ering, v), unit(nring, v), ACT.Ln, bias=1.0).then_inc(logged, 1)

            def exp(c, v):
                act.wait_ge(logged, c * NV + v + 1)
                act.activation(unit(ering, v), unit(ering, v), ACT.Exp, scale=-1.0).then_inc(exped, 1)

            def chunk(c, first):
                for v in range(NV):
                    log(c, v, first)
                    if v >= 1 or not first:
                        exp(c, v - 1)

            chunk(0, True)
            with act.Fori(1, NCH) as c:
                chunk(c, False)
            exp(NCH - 1, NV - 1)


AHEAD = 8
LAG_TURN = 3


def maximum_items(g, groups):
    items = [("half", g + 1, m) for m in range(AHEAD, 2 * HG * TC)]
    items += [("half", g + 2, m) for m in range(LAG_TURN)]
    items += [("turn", g + 1)]
    items += [("half", g + 2, m) for m in range(LAG_TURN, AHEAD)]
    return [x for x in items if x[1] < groups]


def slot_items(first, last):
    items, after = [], []
    for g in range(G):
        mine = maximum_items(g, G if last else 2 * G)
        if g == 0 and not first:
            for n, (t, s) in enumerate(FSTEPS):
                mine.insert(6 + 3 * n, ("finish", -1, t, s))
        span = U if mine and mine[-1][0] == "half" else U - 6
        items += mine
        after += [g * U + (span * (n + 1)) // len(mine) for n in range(len(mine))]
    if last:
        items += [("finish", 0, t, s) for t, s in FSTEPS]
        after += [UC] * len(FSTEPS)
    assert last or len(items) % 2 == 0
    return list(zip(items, after))


def attention1(nc, b, io):
    b.used = b.attn_at
    q = b.carve([P, H, QC], bf16)
    ring = b.carve([P, NW, QC])
    accs = b.carve([P, G, QC])
    mx2 = b.carve([P, HG * TC, 2])
    mx = b.carve([P, HG * TC])
    mparts = b.carve([P, P], bf16)
    mrows = b.carve([3 * HG * TC, P], bf16)
    n = "a1_"
    ones, zeroed, scored, exped, valued, mscored, mread, mchain, mcut, mturned, mcopied, placed = (
        b.sem(n + x) for x in ("ones", "zeroed", "scored", "exped", "valued", "mscored", "mread", "mchain",
                               "mcut", "mturned", "mcopied", "placed"))
    loaded = [b.sem(f"{n}loaded{g}") for g in range(G)]
    f = finish_sems(b, n)
    fin = Finish(b, 1, f, accs)
    NPV = G * KT
    MU = HG * TC
    MH = 2 * MU
    HALVES = [(0, SK // 2 + SK % 2 + 1), (SK // 2 + SK % 2 + 1, SK)]
    ACC = b.bank[7]
    slot = [b.psum[:, 512 * (NS1 + 2 * k):512 * (NS1 + 2 * k + 2)] for k in range(2)]
    slot_rows = [x[:, 0:P // 2].bitcast(bf16) for x in slot]
    BEFORE = maximum_items(-1, 2 * G)
    BEFORE = [("half", 0, m) for m in range(AHEAD)] + BEFORE
    assert len(BEFORE) % 2 == 1 and UC % NW == 0

    def chunks(engine, chunk):
        chunk(0, slot_items(True, False))
        with engine.Fori(1, NCH - 1) as c:
            chunk(c, slot_items(False, False))
        chunk(NCH - 1, slot_items(False, True))

    with nc.Block() as block:
        @block.gpsimd
        def _(pool):
            pool.memset(mparts[:, :], 0.0).then_inc(zeroed, 1)
            pool.wait_ge(zeroed, 1)
            pool.memset(q[ROW_MASK:P, :, :], 1.0).then_inc(ones, 1)

        @block.sync
        def _(sp):
            def place(c, d):
                sp.wait_ge(mcopied, c * G + d + 1)
                g = d % G
                for r in range(3):
                    sp.dma_start(q[ROW_MAX + r:ROW_MAX + r + 1, g * HG:(g + 1) * HG, :]
                                 .rearrange("a h (t q) -> a (h t) q", q=P),
                                 mrows[r * MU:(r + 1) * MU, :]).then_inc(placed, 16)

            sp.wait_ge(ones, 1)
            for g in range(G):
                load_queries(sp, b, 1, q, 0, g, loaded)
            place(0, 0)
            with sp.Fori(0, NCH - 1) as c:
                for g in range(G):
                    place(c, g + 1)
                    sp.wait_ge(scored, c * UC + (g + 1) * U)
                    load_queries(sp, b, 1, q, c + 1, g, loaded)
            for g in range(G - 1):
                place(NCH - 1, g + 1)

        @block.tensor
        def _(pe):
            pe.wait_ge(ones, 1)

            def slot_free(c, item):
                if item[0] == "half":
                    pe.wait_ge(mread, (c * G + item[1]) * MH + item[2] + 1)
                elif item[0] == "turn":
                    pe.wait_ge(mcopied, c * G + item[1] + 1)
                else:
                    s, v = fin.freed(item[3], c + item[1], item[2])
                    pe.wait_ge(s, v)

            def make(c, item, k):
                if item[0] == "half":
                    _, d, m = item
                    j, t = divmod(m // 2, TC)
                    h = d % G * HG + j
                    if m == 0:
                        pe.wait_ge(loaded[d % G], 16 * NB * (c + d // G + 1))
                    lo, hi = HALVES[m % 2]
                    for at in (lo, lo + 512):
                        to = min(at + 512, hi)
                        mm = pe.matmul(slot[k][:, at - lo:to - lo], q[0:ROW_MAX, h, t * P:(t + 1) * P],
                                       b.ks[0:ROW_MAX, h, at:to], start=True, stop=True)
                    mm.then_inc(mscored, 1)
                elif item[0] == "turn":
                    pe.wait_ge(mcut, c * G + item[1] + 1)
                    pe.transpose(slot_rows[k], mparts, b.identb[:, :]).then_inc(mturned, 1)
                else:
                    fin.tensor(pe, item[3], c + item[1], item[2], slot[k])

            def values(c, v):
                g, k = divmod(v % NPV, KT)
                pe.wait_ge(exped, c * UC + HG * (v + 1))
                if k == 0 and not (isinstance(c, int) and c == 0 and g == 0):
                    pe.wait_ge(f.acc_out, G * c + g)
                value_product(pe, b, ring, NW, g, k, ACC, valued)

            def chunk(c, items):
                todo = 0
                for i in range(UC):
                    g, k, j = key_tile(i)
                    h = g * HG + j
                    if i % U == 0:
                        pe.wait_ge(placed, 48 * (c * G + g + 1))
                    if i >= NS1:
                        pe.wait_ge(exped, c * UC + i - NS1 + 1)
                    elif not (isinstance(c, int) and c == 0):
                        pe.wait_ge(exped, c * UC)
                    pe.matmul(b.bank[i % NS1][:, :], b.ks[0:ROWS_ALL, h, k * P:(k + 1) * P],
                              q[0:ROWS_ALL, h, :], start=True, stop=True).then_inc(scored, 1)
                    while todo < len(items) and items[todo][1] <= i + 1:
                        slot_free(c, items[todo - 2][0] if todo >= 2 else ("half", 1, AHEAD - 2 + todo))
                        make(c, items[todo][0], todo % 2)
                        todo += 1
                    if i % HG == 2 and (i >= HG or not (isinstance(c, int) and c == 0)):
                        values(c, i // HG - 1)
                return todo

            for k, item in enumerate(BEFORE):
                if k >= 2:
                    slot_free(0, BEFORE[k - 2])
                make(0, item, (k + 1) % 2)
            chunk(0, slot_items(True, False))
            with pe.Fori(1, NCH - 1) as c:
                chunk(c, slot_items(False, False))
            items = slot_items(False, True)
            c = NCH - 1
            todo = chunk(c, [x for x in items if x[1] < UC])
            values(c, NPV - 1)
            for k in range(todo, len(items)):
                slot_free(c, items[k - 2][0])
                make(c, items[k][0], k % 2)

        @block.vector
        def _(dve):
            def use(c, item, k):
                if item[0] == "half":
                    _, d, m = item
                    group = c * G + d
                    dve.wait_ge(mscored, group * MH + m + 1)
                    lo, hi = HALVES[m % 2]
                    dve.tensor_reduce(mx2[:, m // 2, m % 2:m % 2 + 1], slot[k][:, 0:hi - lo], AX.X,
                                      ALU.max).then_inc(mread, 1)
                    if m == MH - 1:
                        cut(group)
                elif item[0] == "turn":
                    _, d = item
                    dve.wait_ge(mturned, c * G + d + 1)
                    if not (isinstance(c, int) and c * G + d == 0):
                        dve.wait_ge(placed, 48 * (c * G + d))
                    dve.tensor_copy(mrows[:, :], slot_rows[k][0:3 * MU, :]).then_inc(mcopied, 1)
                else:
                    fin.vector(dve, item[3], c + item[1], item[2], slot[k])

            def cut(group):
                dve.wait_ge(mread, (group + 1) * MH)
                dve.tensor_tensor(mx[:, :], mx2[:, :, 0], mx2[:, :, 1], ALU.max).then_inc(mchain, 1)
                dve.wait_ge(mchain, group * 5 + 1)
                for r in range(3):
                    ins = dve.tensor_copy(mparts[:, r * MU:(r + 1) * MU], mx[:, :])
                    if r == 2:
                        ins.then_inc(mcut, 1)
                        dve.wait_ge(mcut, group + 1)
                    else:
                        ins.then_inc(mchain, 1)
                        dve.wait_ge(mchain, group * 5 + 2 * r + 2)
                        dve.tensor_tensor(mx[:, :], mx[:, :], mparts[:, r * MU:(r + 1) * MU], ALU.subtract
                                          ).then_inc(mchain, 1)
                        dve.wait_ge(mchain, group * 5 + 2 * r + 3)

            dve.wait_ge(zeroed, 1)
            for k, item in enumerate(BEFORE):
                use(0, item, (k + 1) % 2)
            chunks(dve, lambda c, items: [use(c, item, k % 2) for k, (item, _) in enumerate(items)])
            dve.wait_ge(f.resid, TC * NCH)

        @block.scalar
        def _(act):
            act.preload_act_table_set(LN_EXP)

            def sums_out(c, g):
                act.wait_ge(valued, c * NPV + (g + 1) * KT)
                act.activation(accs[:, g % G, :], ACC, ACT.Copy).then_inc(f.acc_out, 1)

            def chunk(c, items):
                first = isinstance(c, int) and c == 0
                for i in range(UC):
                    act.wait_ge(scored, c * UC + i + 1)
                    if i >= NW or not first:
                        act.wait_ge(valued, c * NPV + (i - NW) // HG + 1)
                    act.activation(ring[:, i % NW, :], b.bank[i % NS1][:, :], ACT.Exp
                                   ).then_inc(exped, 1)
                    if i % U == OUT1 and (i >= U or not first):
                        if i // U == 1 and not first:
                            act.wait_ge(f.turned, TC * c)
                        sums_out(c, i // U - 1)
                    for k, (item, after) in enumerate(items):
                        if item[0] == "finish" and item[1] == -1 and after == i - 1:
                            fin.scalar(act, item[3], c - 1, item[2], slot[k % 2])

            chunks(act, chunk)
            c = NCH - 1
            sums_out(c, G - 1)
            for k, (item, after) in enumerate(slot_items(False, True)):
                if item[0] == "finish" and item[1] == 0:
                    fin.scalar(act, item[3], c, item[2], slot[k % 2])


def tile_of(x, c, j):
    return x[:, bass.ds(c * TC + j, 1), :].rearrange("p a d -> p (a d)")


def route(nc, b, io, l):
    top = l + 1
    NA, T = routing(top)
    b.used = 0
    b.shared = b.carve([P, NT, D])
    b.expert_at = b.used
    xn = b.carve([P, TC, D])
    xall = b.carve([P, NT, D])
    logits = b.carve([P, NT, E])
    logit_bias = b.carve([P, TC * E])
    gate_w = b.carve([P, DC, E])
    shared_w = b.carve([P, DC, D])
    shared_b = b.carve([P, D])
    best = b.carve([P, NT, E])
    best_at = b.carve([P, NT, E], u32)
    at_f = b.carve([P, top, NT])
    onehot = b.carve([P, NA, E])
    iota_e = b.carve([P, E])
    iota_rows = b.carve([P, NA])
    iota_t = b.carve([P, T])
    totals = b.carve([P, NA, E])
    upto = b.carve([P, E, NA])
    fills = b.carve([P, E, NA])
    tiles = b.carve([P, E])
    ends = b.carve([P, E])
    base = b.carve([P, E])
    place = b.carve([P, NA, E])
    place_f = b.carve([P, NA])
    owner = b.carve([P, T, E])
    owner_f = b.carve([P, T])
    expd = b.carve([P, NT, E])
    n = f"r{l}_"
    s = norm_sems(b, n)
    loaded, turned, copied, kept, prod, evac, chain, onehots, counted, shifted, exped, placed, sent, act_done = (
        b.sem(n + x) for x in ("loaded", "turned", "copied", "kept", "prod", "evac", "chain", "onehots",
                               "counted", "shifted", "exped", "placed", "sent", "act_done"))
    NL = 7 if l else 5
    with nc.Block() as block:
        @block.sync
        def _(sp):
            sp.dma_start(gate_w, io[f"gate{l}"].rearrange("(c p) e -> p c e", p=P)).then_inc(loaded, 16)
            sp.dma_start(iota_e, io["iota"][0:1, 0:E].to_broadcast([P, E])).then_inc(loaded, 16)
            sp.dma_start(iota_rows, io["iota"][1:2, 0:NA].to_broadcast([P, NA])).then_inc(loaded, 16)
            sp.dma_start(iota_t, io["iota"][0:1, 0:T].to_broadcast([P, T])).then_inc(loaded, 16)
            if l == 0:
                src = io["gate_bias"].rearrange("(a n) -> a n", a=1)
                for j in range(TC):
                    sp.dma_start(logit_bias[:, j * E:(j + 1) * E], src.to_broadcast([P, E])).then_inc(loaded, 16)
            else:
                sp.dma_start(shared_w, io["shared_w"].rearrange("(c p) n -> p c n", p=P)).then_inc(loaded, 16)
                sp.dma_start(shared_b, io["shared_b"].rearrange("(a n) -> a n", a=1).to_broadcast([P, D])
                             ).then_inc(loaded, 16)
            sp.wait_ge(loaded, 16 * (4 + (TC if l == 0 else 2)))

        NLOAD = 16 * (4 + (TC if l == 0 else 2))

        @block.scalar
        def _(act):
            act.preload_act_table_set(LN_EXP)
            with act.Fori(0, NCH) as c:
                norm_scalar(act, b, c, s)
                for kk in range(DC):
                    act.wait_ge(turned, DC * c + kk + 1)
                    act.activation(b.xnT[:, kk, :], b.bank[kk][:, :], ACT.Copy).then_inc(copied, 1)
            act.wait_ge(shifted, 1)
            if l == 0:
                act.activation(expd[:, :, :], expd[:, :, :], ACT.Exp).then_inc(exped, 1)
            else:
                act.activation(expd[:, :, 0], expd[:, :, 0], ACT.Exp).then_inc(exped, 1)
                act.wait_ge(evac, NCH * (1 + TC))
                act.activation(b.shared[:, :, :], b.shared[:, :, :], ACT.Gelu).then_inc(act_done, 1)

        @block.tensor
        def _(pe):
            pe.wait_ge(loaded, NLOAD)
            with pe.Fori(0, NCH) as c:
                pe.wait_ge(s.normed, TC * c + TC)
                for kk in range(DC):
                    for j in range(TC):
                        mm = pe.transpose(b.bank[kk][:, j * P:(j + 1) * P], xn[:, j, kk * P:(kk + 1) * P],
                                          b.ident[:, :])
                    mm.then_inc(turned, 1)
                pe.wait_ge(copied, DC * c + DC)
                for j in range(TC):
                    for kk in range(DC):
                        mm = pe.matmul(b.bank[2][:, j * E:(j + 1) * E], b.xnT[:, kk, j * P:(j + 1) * P],
                                       gate_w[:, kk, :], start=(kk == 0), stop=(kk == DC - 1))
                mm.then_inc(prod, 1)
                if l == 1:
                    for j in range(TC):
                        for kk in range(DC):
                            mm = pe.matmul(b.bank[3 + j][:, 0:D], b.xnT[:, kk, j * P:(j + 1) * P],
                                           shared_w[:, kk, :], start=(kk == 0), stop=(kk == DC - 1))
                        mm.then_inc(prod, 1)
                pe.wait_ge(evac, (1 + TC * l) * (c + 1))
            pe.wait_ge(onehots, 1)
            flat = onehot.rearrange("p a e -> p (a e)")
            pe.matmul(b.bank[0][:, 0:NA * E], b.tri[:, :], flat, start=True, stop=True)
            pe.matmul(b.bank[1][:, 0:NA * E], b.ones[:, :], flat, start=True, stop=True).then_inc(counted, 1)

        @block.gpsimd
        def _(pool):
            with pool.Fori(0, NCH) as c:
                pool.wait_ge(s.normed, TC * c + TC)
                pool.tensor_copy(xall[:, bass.ds(c * TC, TC), :], xn[:, :, :]).then_inc(kept, 1)
            pool.wait_ge(kept, NCH)
            pool.wait_ge(placed, 1)
            for a in range(NA):
                pool.indirect_dma_start(b.xs[l][:, :], bass.IndirectOffsetOnAxis(ap=b.slot[:, a:a + 1], axis=0),
                                        xall[:, a % NT, :], None).then_inc(sent, 16)
            pool.wait_ge(sent, 16 * NA)

        @block.vector
        def _(dve):
            dve.wait_ge(loaded, NLOAD)
            flat = logits.rearrange("p t e -> p (t e)")
            with dve.Fori(0, NCH) as c:
                norm_vector(dve, b, c, s, lambda j: xn[:, j, :])
                per = 1 + TC * l
                dve.wait_ge(prod, per * c + 1)
                out = flat[:, bass.ds(c * TC * E, TC * E)]
                if l == 0:
                    dve.tensor_tensor(out, b.bank[2][:, 0:TC * E], logit_bias[:, :], ALU.add).then_inc(evac, 1)
                else:
                    dve.tensor_copy(out, b.bank[2][:, 0:TC * E]).then_inc(evac, 1)
                    for j in range(TC):
                        dve.wait_ge(prod, per * c + 2 + j)
                        dve.tensor_tensor(tile_of(b.shared, c, j), b.bank[3 + j][:, 0:D], shared_b[:, :],
                                          ALU.add).then_inc(evac, 1)
                dve.wait_ge(turned, DC * c + DC)
                dve.wait_ge(kept, c + 1)
            dve.wait_ge(evac, NCH * (1 + TC * l))
            count = [0]

            def link(ins):
                count[0] += 1
                ins.then_inc(chain, 1)
                dve.wait_ge(chain, count[0])

            for t in range(NT):
                ins = dve.max(best[:, t, :], logits[:, t, :])
                ins.then_inc(chain, 1)
            count[0] += NT
            dve.wait_ge(chain, count[0])
            for t in range(NT):
                dve.max_index(best_at[:, t, :], best[:, t, :], logits[:, t, :]).then_inc(chain, 1)
            count[0] += NT
            dve.wait_ge(chain, count[0])
            if l == 0:
                dve.tensor_tensor(expd[:, :, :], logits[:, :, :], best[:, :, 0:1].to_broadcast([P, NT, E]),
                                  ALU.subtract).then_inc(shifted, 1)
            else:
                dve.tensor_tensor(expd[:, :, 0], best[:, :, 1], best[:, :, 0], ALU.subtract).then_inc(shifted, 1)
            link(dve.tensor_copy(at_f[:, :, :], best_at[:, :, 0:top].rearrange("p t r -> p r t")))
            dve.tensor_tensor(onehot[:, :, :],
                              at_f.rearrange("p r (t a) -> p (r t) a", a=1).to_broadcast([P, NA, E]),
                              iota_e.rearrange("p (a e) -> p a e", a=1).to_broadcast([P, NA, E]),
                              ALU.is_equal).then_inc(onehots, 1)
            dve.wait_ge(exped, 1)
            if l == 0:
                link(dve.tensor_reduce(b.gate[:, 1, :], expd[:, :, :], AX.X, ALU.add))
                link(dve.reciprocal(b.gate[:, 0, :], b.gate[:, 1, :]))
            else:
                link(dve.tensor_scalar(b.gate[:, 1, :], expd[:, :, 0], 1.0, None, ALU.add))
                link(dve.reciprocal(b.gate[:, 0, :], b.gate[:, 1, :]))
                link(dve.tensor_tensor(b.gate[:, 1, :], expd[:, :, 0], b.gate[:, 0, :], ALU.mult))
            dve.wait_ge(counted, 1)
            link(dve.tensor_copy(totals.rearrange("p a e -> p (a e)"), b.bank[1][:, 0:NA * E]))
            for e in range(E):
                dve.tensor_tensor_scan(upto[:, e, :], b.ones[:, 0:NA], totals[:, :, e], 0.0,
                                       ALU.mult, ALU.add).then_inc(chain, 1)
            count[0] += E
            dve.wait_ge(chain, count[0])
            link(dve.tensor_tensor(fills[:, :, :], upto[:, :, NA - 1:NA].to_broadcast([P, E, NA]),
                                   iota_rows.rearrange("p (a n) -> p a n", a=1).to_broadcast([P, E, NA]),
                                   ALU.is_gt))
            link(dve.tensor_reduce(tiles[:, :], fills[:, :, :], AX.X, ALU.add))
            link(dve.tensor_tensor_scan(ends[:, :], b.ones[:, 0:E], tiles[:, :], 0.0, ALU.mult, ALU.add))
            link(dve.tensor_tensor(base[:, :], ends[:, :], tiles[:, :], ALU.subtract))
            link(dve.tensor_scalar(base[:, :], base[:, :], float(P), None, ALU.mult))
            link(dve.tensor_tensor(place.rearrange("p a e -> p (a e)"), b.bank[0][:, 0:NA * E],
                                   totals.rearrange("p a e -> p (a e)"), ALU.subtract))
            link(dve.tensor_tensor(place[:, :, :], place[:, :, :], upto.rearrange("p e a -> p a e"), ALU.add))
            link(dve.tensor_tensor(place[:, :, :], place[:, :, :],
                                   base.rearrange("p (a e) -> p a e", a=1).to_broadcast([P, NA, E]), ALU.add))
            link(dve.tensor_tensor(place[:, :, :], place[:, :, :], onehot[:, :, :], ALU.mult))
            link(dve.tensor_reduce(place_f[:, :], place[:, :, :], AX.X, ALU.add))
            dve.tensor_copy(b.slot[:, 0:NA], place_f[:, :]).then_inc(placed, 1)
            link(dve.tensor_tensor(owner[:, :, :],
                                   ends.rearrange("p (a e) -> p a e", a=1).to_broadcast([P, T, E]),
                                   iota_t.rearrange("p (t a) -> p t a", a=1).to_broadcast([P, T, E]),
                                   ALU.is_le))
            link(dve.tensor_reduce(owner_f[:, :], owner[:, :, :], AX.X, ALU.add))
            link(dve.tensor_scalar(b.texp[:, 0:T], owner_f[:, :], float(E - 1), None, ALU.min))
            dve.wait_ge(placed, 1)
            if l == 1:
                dve.wait_ge(act_done, 1)


def experts(nc, b, io, l):
    _, T = routing(l + 1)
    W = HID * (2 - l)
    NOW = 4
    assert T % NOW == 0
    b.used = b.expert_at
    w1 = [b.carve([P, DC, W]) for _ in range(2)]
    w2 = [b.carve([P, MC, D]) for _ in range(2)]
    b1 = [b.carve([P, MC]) for _ in range(2)]
    b2 = [b.carve([1, D]) for _ in range(2)]
    xt = [b.carve([P, D]) for _ in range(2)]
    xT = [b.carve([P, DC, P]) for _ in range(2)]
    gated = [b.carve([P, HID]) for _ in range(2)]
    h = [b.carve([P, MC, P]) for _ in range(2)]
    y = [b.carve([P, D]) for _ in range(2)]
    now = b.carve([1, NOW], u32)
    n = f"e{l}_"
    named, turned, turned_out, up, active, hidden, down, y_out = (
        b.sem(n + x) for x in ("named", "turned", "turned_out", "up", "active", "hidden", "down", "y_out"))
    rows_in, up_in, down_in, stored = (
        [b.sem(f"{n}{x}{k}") for k in range(2)] for x in ("rows_in", "up_in", "down_in", "stored"))
    ND = 1 + 2 * l
    NH = 2
    TURN = b.bank[7]

    with nc.Block() as block:
        @block.gpsimd
        def _(pool):
            def name(t, k):
                pool.tensor_copy(now[0:1, k:k + 1], b.texp[0:1, bass.ds(t, 1)]).then_inc(named, 1)

            def name_next(t, k):
                pool.wait_ge(up, NH * (t - 1))
                name(t, k)

            for k in range(2):
                name(k, k)
            for k in range(2, NOW):
                name_next(k, k)
            with pool.Fori(1, T // NOW) as p:
                for k in range(NOW):
                    name_next(NOW * p + k, k)

        @block.sync
        def _(sp):
            def expert(k):
                return sp.value_load(now[0:1, k % NOW:k % NOW + 1], min_val=0, max_val=E - 1)

            def load_up(t, k):
                sp.wait_ge(named, t + 1)
                sp.dma_start(xt[k % 2], b.xs[l][bass.ds(t * P, P), :]).then_inc(rows_in[k % 2], 16)
                sp.dma_start(w1[k % 2], io[f"w1_{l}"][bass.ds(expert(k), 1)].rearrange("a (c p) n -> p (a c) n", p=P)
                             ).then_inc(up_in[k % 2], 16)

            def load_down(k):
                e = expert(k)
                if l == 1:
                    sp.dma_start(b1[k % 2], io["b1"][bass.ds(e, 1)].rearrange("a p c -> p (a c)")
                                 ).then_inc(down_in[k % 2], 16)
                    sp.dma_start(b2[k % 2], io["b2"][bass.ds(e, 1), :]).then_inc(down_in[k % 2], 16)
                sp.dma_start(w2[k % 2], io[f"w2_{l}"][bass.ds(e, 1)].rearrange("a (c p) n -> p (a c) n", p=P)
                             ).then_inc(down_in[k % 2], 16)

            def store(t, k):
                sp.wait_ge(y_out, t + 1)
                sp.dma_start(b.ys[l][bass.ds(t * P, P), :], y[k % 2]).then_inc(stored[k % 2], 16)

            def advance(t, k):
                load_up(t, k)
                store(t - 3, k - 3)
                load_down(k - 1)

            for k in range(2):
                load_up(k, k)
                load_down(k)
            load_up(2, 2)
            advance(3, 3)
            with sp.Fori(1, T // NOW) as p:
                for k in range(NOW):
                    advance(NOW * p + k, k)
            store(T - 3, T - 3)
            load_down(T - 1)
            for k in range(2):
                store(T - 2 + k, k)
            for k in range(2):
                sp.wait_ge(stored[k], 16 * (T // 2))

        @block.tensor
        def _(pe):
            def turn(t, k, p):
                pe.wait_ge(rows_in[k], 16 * (p + 1))
                if not (isinstance(t, int) and t < 1):
                    pe.wait_ge(turned_out, t)
                for kk in range(DC):
                    mm = pe.transpose(TURN[:, kk * P:(kk + 1) * P], xt[k][:, kk * P:(kk + 1) * P], b.ident[:, :])
                mm.then_inc(turned, 1)

            def up_half(t, k, half):
                for part in range(2 - l):
                    bank = b.bank[half + 2 * part] if l == 0 else b.bank[2 * k + half]
                    for m in range(MC // 2):
                        for kk in range(DC):
                            at = part * HID + (half * MC // 2 + m) * P
                            mm = pe.matmul(bank[:, m * P:(m + 1) * P], w1[k][:, kk, at:at + P], xT[k][:, kk, :],
                                           start=(kk == 0), stop=(kk == DC - 1))
                mm.then_inc(up, 1)

            def rise(t, k, p):
                pe.wait_ge(up_in[k], 16 * (p + 1))
                pe.wait_ge(turned_out, t + 1)
                for half in range(NH):
                    before = 1 if l == 0 else 2
                    if not (isinstance(t, int) and t < before):
                        pe.wait_ge(hidden, NH * (t - before + 1))
                    up_half(t, k, half)

            def fall(t, k, p):
                pe.wait_ge(down_in[k], 16 * ND * (p + 1))
                pe.wait_ge(hidden, NH * (t + 1))
                if not (isinstance(t, int) and t < 2):
                    pe.wait_ge(y_out, t - 1)
                out = b.bank[4 + k]
                for m in range(MC):
                    mm = pe.matmul(out[:, 0:D], h[k][:, m, :], w2[k][:, m, :], start=(m == 0),
                                   stop=(l == 0 and m == MC - 1))
                if l == 1:
                    mm = pe.matmul(out[:, 0:D], b.ones[0:1, :], b2[k], start=False, stop=True)
                mm.then_inc(down, 1)

            def pair(p):
                rise(2 * p + 1, 1, p)
                turn(2 * p + 2, 0, p + 1)
                fall(2 * p, 0, p)
                rise(2 * p + 2, 0, p + 1)
                turn(2 * p + 3, 1, p + 1)
                fall(2 * p + 1, 1, p)

            turn(0, 0, 0)
            rise(0, 0, 0)
            turn(1, 1, 0)
            pair(0)
            with pe.Fori(1, T // 2 - 1) as p:
                pair(p)
            rise(T - 1, 1, T // 2 - 1)
            fall(T - 2, 0, T // 2 - 1)
            fall(T - 1, 1, T // 2 - 1)

        @block.scalar
        def _(act):
            def tile(p, k):
                t = 2 * p + k
                first = isinstance(p, int) and p == 0
                for half in range(NH):
                    act.wait_ge(up, NH * t + half + 1)
                    if l == 0:
                        if not first:
                            act.wait_ge(hidden, NH * (t - 1))
                        act.activation(gated[k][:, half * 512:(half + 1) * 512], b.bank[half][:, :],
                                       ACT.Silu).then_inc(active, 1)
                    else:
                        if not first:
                            act.wait_ge(down, t - 1)
                        act.wait_ge(down_in[k], 16 * ND * (p + 1))
                        for m in range(MC // 2):
                            at = half * MC // 2 + m
                            ins = act.activation(h[k][:, at, :], b.bank[2 * k + half][:, m * P:(m + 1) * P],
                                                 ACT.Gelu, bias=b1[k][:, at:at + 1])
                        ins.then_inc(hidden, 1)

            for k in range(2):
                tile(0, k)
            with act.Fori(1, T // 2) as p:
                for k in range(2):
                    tile(p, k)

        @block.vector
        def _(dve):
            def turn_out(t, k):
                dve.wait_ge(turned, t + 1)
                dve.tensor_copy(xT[k].rearrange("p a q -> p (a q)"), TURN[:, 0:D]).then_inc(turned_out, 1)

            def gate(t, k):
                for half in range(NH):
                    dve.wait_ge(active, NH * t + half + 1)
                    dve.tensor_tensor(h[k].rearrange("p a q -> p (a q)")[:, half * 512:(half + 1) * 512],
                                      gated[k][:, half * 512:(half + 1) * 512], b.bank[2 + half][:, :],
                                      ALU.mult).then_inc(hidden, 1)

            def out(t, k, p):
                dve.wait_ge(down, t + 1)
                dve.wait_ge(stored[k], 16 * p)
                dve.tensor_copy(y[k], b.bank[4 + k][:, 0:D]).then_inc(y_out, 1)

            def step(t, k, turned_next=True):
                if l == 0:
                    gate(t, k)
                if turned_next:
                    turn_out(t + 1, 1 - k)

            turn_out(0, 0)
            step(0, 0)
            step(1, 1)
            out(0, 0, 0)
            step(2, 0)
            out(1, 1, 0)
            with dve.Fori(1, T // 2 - 1) as p:
                step(2 * p + 1, 1)
                out(2 * p, 0, p)
                step(2 * p + 2, 0)
                out(2 * p + 1, 1, p)
            step(T - 1, 1, turned_next=False)
            out(T - 2, 0, T // 2 - 1)
            out(T - 1, 1, T // 2 - 1)


def combine(nc, b, io, l):
    top = l + 1
    NA, _ = routing(top)
    b.used = b.expert_at
    got = b.carve([P, NA, D])
    mixed = b.carve([P, NT, D])
    gamma = b.carve([P, D])
    beta = b.carve([P, D])
    xn = b.carve([P, TC, D])
    n = f"c{l}_"
    s = norm_sems(b, n)
    gathered, halved, mixes, loaded, scaled, summed, final, written = (b.sem(n + x) for x in (
        "gathered", "halved", "mixes", "loaded", "scaled", "summed", "final", "written"))
    with nc.Block() as block:
        @block.gpsimd
        def _(pool):
            for a in range(NA):
                pool.indirect_dma_start(got[:, a, :], None, b.ys[l][:, :],
                                        bass.IndirectOffsetOnAxis(ap=b.slot[:, a:a + 1], axis=0)
                                        ).then_inc(gathered, 16)

        if l == 0:
            @block.vector
            def _(dve):
                dve.wait_ge(gathered, 16 * NA)
                for t in range(NT):
                    dve.scalar_tensor_tensor(out=b.x[:, t, :], in0=got[:, t, :], scalar=b.gate[:, 0, t:t + 1],
                                             in1=b.x[:, t, :], op0=ALU.mult, op1=ALU.add).then_inc(mixes, 1)
                dve.wait_ge(mixes, NT)
            return

        @block.sync
        def _(sp):
            sp.dma_start(gamma, io["gamma"].rearrange("(a n) -> a n", a=1).to_broadcast([P, D])).then_inc(loaded, 16)
            sp.dma_start(beta, io["beta"].rearrange("(a n) -> a n", a=1).to_broadcast([P, D])).then_inc(loaded, 16)
            sp.wait_ge(final, NCH * TC)
            sp.dma_start(io["out"].rearrange("(t p) d -> p t d", p=P), b.x[:, :, :]).then_inc(written, 16)
            sp.wait_ge(written, 16)

        @block.scalar
        def _(act):
            act.preload_act_table_set(LN_EXP)
            with act.Fori(0, NCH) as c:
                norm_scalar(act, b, c, s)

        @block.vector
        def _(dve):
            dve.tensor_scalar(b.shared[:, :, :], b.shared[:, :, :], 0.5, None, ALU.mult).then_inc(halved, 1)
            dve.wait_ge(halved, 1)
            dve.wait_ge(gathered, 16 * NA)
            for t in range(NT):
                dve.scalar_tensor_tensor(out=mixed[:, t, :], in0=got[:, t, :], scalar=b.gate[:, 0, t:t + 1],
                                         in1=b.shared[:, t, :], op0=ALU.mult, op1=ALU.add).then_inc(mixes, 1)
            for t in range(NT):
                dve.wait_ge(mixes, NT + t)
                dve.scalar_tensor_tensor(out=mixed[:, t, :], in0=got[:, NT + t, :],
                                         scalar=b.gate[:, 1, t:t + 1], in1=mixed[:, t, :], op0=ALU.mult,
                                         op1=ALU.add).then_inc(mixes, 1)
            dve.wait_ge(mixes, 2 * NT)
            dve.wait_ge(loaded, 32)
            with dve.Fori(0, NCH) as c:
                norm_vector(dve, b, c, s, lambda j: xn[:, j, :], src=mixed)
                for j in range(TC):
                    dve.wait_ge(s.normed, TC * c + j + 1)
                    dve.tensor_tensor(xn[:, j, :], xn[:, j, :], gamma[:, :], ALU.mult).then_inc(scaled, 1)
                for j in range(TC):
                    dve.wait_ge(scaled, TC * c + j + 1)
                    dve.tensor_tensor(xn[:, j, :], xn[:, j, :], beta[:, :], ALU.add).then_inc(summed, 1)
                for j in range(TC):
                    dve.wait_ge(summed, TC * c + j + 1)
                    dve.tensor_tensor(tile_of(b.x, c, j), tile_of(b.x, c, j), xn[:, j, :],
                                      ALU.add).then_inc(final, 1)


def kernel(**inputs):
    import numpy as _np
    import concourse.bacc as _bacc
    from concourse import mybir as _mybir
    from concourse.bass_utils import run_bass_kernel_spmd as _run

    a = {k: _np.asarray(v) for k, v in inputs.items()}
    arrays = {"x": a["x"][0], "ctxT": a["ctx_1024"][0].T, "mask": a["mask_BxS2_bf1"].view(_np.uint8)}
    for l in range(2):
        for n in "qkvo":
            arrays[f"w{n}T{l}"] = a[f"L{l}_xattn_W{n}"].T
        for n in "qk":
            arrays[f"b{n}{l}"] = a[f"L{l}_xattn_b{n}"].reshape(DC, P).T
        for n in "vo":
            arrays[f"b{n}{l}"] = a[f"L{l}_xattn_b{n}"]
    arrays |= {"gate0": a["L0_ffn_router_w"], "gate_bias": a["L0_ffn_router_b"], "w1_0": a["L0_ffn_w1"],
               "w2_0": a["L0_ffn_w2"], "gate1": a["L1_ffn_gate_W"], "w1_1": a["L1_ffn_W1"],
               "w2_1": a["L1_ffn_W2"], "b1": a["L1_ffn_b1"].reshape(E, MC, P).transpose(0, 2, 1),
               "b2": a["L1_ffn_b2"], "shared_w": a["L1_ffn_shared_W"], "shared_b": a["L1_ffn_shared_b"],
               "gamma": a["L1_ffn_gamma"], "beta": a["L1_ffn_beta"]}
    arrays["iota"] = _np.stack([_np.arange(64), P * _np.arange(64)]).astype(_np.float32)
    arrays["tri"] = _np.triu(_np.ones((P, P), _np.float32), 1)
    kconst = _np.zeros((P, 2), _np.float32)
    rest = _np.float32(FILL)
    for r in range(3):
        part = (_np.array([rest]).view(_np.uint32) & _np.uint32(0xFFFF0000)).view(_np.float32)[0]
        rest = rest - part
        kconst[ROW_MASK + r] = (-part, part)
        kconst[ROW_MAX + r] = (0.0, -1.0)
    arrays["kconst"] = kconst
    arrays["own"] = _np.kron(_np.eye(P // HD), _np.ones((HD, 1))).astype(_np.float32)
    arrays["bk_row"] = a["L0_xattn_bk"].reshape(1, D)
    arrays = {k: _np.ascontiguousarray(v) for k, v in arrays.items()}

    nc = _bacc.Bacc("TRN2", target_bir_lowering=False, num_devices=1)
    io = {k: nc.dram_tensor(f"in_{k}", v.shape, _mybir.dt.from_np(v.dtype), kind="ExternalInput").ap()
          for k, v in arrays.items()}
    io["out"] = nc.dram_tensor("out_x", (S, D), fp32, kind="ExternalOutput").ap()
    build(nc, io)
    r = _run(nc, [{f"in_{k}": v for k, v in arrays.items()}], core_ids=[0])
    return r.results[0]["out_x"].reshape(1, S, D)
```

```python
import concourse.bass as bass
from concourse import mybir
from contextlib import ExitStack

fp32 = mybir.dt.float32
bf16 = mybir.dt.bfloat16
i32 = mybir.dt.int32
u32 = mybir.dt.uint32
u8 = mybir.dt.uint8
ALU = mybir.AluOpType
ACT = mybir.ActivationFunctionType
AX = mybir.AxisListType

LN_EXP = "natural_log_exp_and_others"
P = 128
S = 2048
SK = 1601
D = 256
DC = D // P
H = 16
HD = D // H
E = 8
HID = 1024
MC = HID // P
EPS = 1e-5
FILL = -1e8

QC = 512
NCH = S // QC
TC = QC // P
NT = S // P
G = 4
HG = H // G
KT = (SK + P - 1) // P
KROWS = [min(P, SK - P * k) for k in range(KT)]
SKP = KT * P
KCOLS = [(n, min(512, SK - n)) for n in range(0, SK, 512)]

QPART = [0, 0, 0, 1, 1, 2]
KPART = [0, 1, 2, 0, 1, 0]
NB = len(QPART)
ROW_MASK = NB * HD
ROW_MAX = ROW_MASK + 3
ROWS_ALL = ROW_MAX + 3

U = HG * KT
UC = G * U
NW = 16
OUT1 = 3
NS1 = 3
PC2 = UC // 2


def routing(top):
    na = NT * top
    nt = na + E - 1
    return na, nt + nt % 2


STATS = TC + 6


class Buffers:
    pass


def build(nc, io):
    b = Buffers()
    ctx = ExitStack()
    with ctx:
        def sb(name, shape, dt=fp32):
            return ctx.enter_context(nc.sbuf_tensor(name, shape, dt))

        layer_sems = []

        def sem(name):
            layer_sems.append(nc.alloc_semaphore(name=name))
            return layer_sems[-1]

        b.sem = sem
        b.x = sb("x_res", [P, NT, D])
        b.ident = sb("ident", [P, P])
        b.identb = sb("identb", [P, P], bf16)
        b.tri = sb("tri", [P, P])
        b.ones = sb("ones", [P, P])
        b.kconst = sb("kconst", [P, 2])
        b.wq = sb("wq", [P, 2, DC, D])
        b.wk = sb("wk", [P, 2, DC, D])
        b.wv = sb("wv", [P, 2, DC, D])
        b.wo = sb("wo", [P, 2, DC, D])
        b.bq = sb("bq", [P, 2, DC])
        b.bk = sb("bk", [P, 2, DC])
        b.bv = sb("bv", [P, 2, D])
        b.bo = sb("bo", [P, 2, D])
        b.stats = sb("stats", [P, TC, 6])
        b.mv = sb("mv", [P, TC, 2])
        b.var = sb("var", [P, TC])
        b.rstd = sb("rstd", [P, TC])
        b.newt = sb("newt", [P, TC])
        b.xnT = sb("xnT", [P, DC, QC])
        arena = sb("arena", [P, 41600])
        b.used = 0

        def carve(shape, dt=fp32, at=None):
            n = 1
            for s in shape[1:]:
                n *= s
            words = n if dt in (fp32, i32, u32) else (n + 1) // 2 if dt == bf16 else (n + 3) // 4
            start = b.used if at is None else at
            b.used = start + words
            assert b.used <= 41600, b.used
            v = arena[:shape[0], start:start + words]
            if dt != fp32:
                v = v.bitcast(dt)
            v = v[:, 0:n]
            if len(shape) == 3:
                v = v.rearrange("p (a b) -> p a b", a=shape[1])
            if len(shape) == 4:
                v = v.rearrange("p (a b c) -> p a b c", a=shape[1], b=shape[2])
            return v

        b.carve = carve
        psum = ctx.enter_context(nc.psum_tensor("psum", [P, 8 * 512], fp32))
        b.psum = psum
        b.bank = [psum[:, 512 * i:512 * (i + 1)] for i in range(8)]
        b.slot = sb("slot", [P, 2 * NT], u32)
        b.gate = sb("gate", [P, 2, NT])
        b.texp = sb("texp", [P, 40], u32)

        b.qd = [nc.dram_tensor(f"q_parts{l}", (3, D, S), bf16, kind="Internal").ap() for l in range(2)]
        b.kd = [nc.dram_tensor(f"k_parts{l}", (3, D, SK), bf16, kind="Internal").ap() for l in range(2)]
        b.q32 = nc.dram_tensor("q32", (D, S), fp32, kind="Internal").ap()
        b.xs = [nc.dram_tensor(f"sorted_in{l}", (routing(l + 1)[1] * P, D), fp32, kind="Internal").ap()
                for l in range(2)]
        b.ys = [nc.dram_tensor(f"sorted_out{l}", (routing(l + 1)[1] * P, D), fp32, kind="Internal").ap()
                for l in range(2)]

        phases = [lambda: setup(nc, b, io)]
        for l in range(2):
            phases += [lambda l=l: keys_values(nc, b, io, l), lambda l=l: queries(nc, b, io, l),
                       lambda l=l: (attention0 if l == 0 else attention1)(nc, b, io),
                       lambda l=l: route(nc, b, io, l), lambda l=l: experts(nc, b, io, l),
                       lambda l=l: combine(nc, b, io, l)]
        for n, phase in enumerate(phases):
            phase()
            if n == len(phases) // 2:
                nc.clear_and_free_semaphores(layer_sems)
                layer_sems.clear()
                nc.all_engine_barrier()


def setup(nc, b, io):
    made = b.sem("su_made")
    b.first_in, b.rest_in, b.cleared = b.sem("su_first_in"), b.sem("su_rest_in"), b.sem("su_cleared")
    with nc.Block() as block:
        @block.sync
        def _(sp):
            b.first_loads = load_weights(sp, b, io, 0, (("wk", b.wk), ("wv", b.wv)), (("bv", b.bv),),
                                         (("bk", b.bk),), b.first_in)

        @block.gpsimd
        def _(pool):
            pool.memset(b.ident[:, :], 0.0).then_inc(made, 1)
            pool.memset(b.identb[:, :], 0.0).then_inc(made, 1)
            pool.memset(b.ones[:, :], 1.0).then_inc(made, 1)
            pool.wait_ge(made, 3)
            for m in (b.ident, b.identb):
                pool.affine_select(out=m[:, :], in_=m[:, :], compare_op=ALU.not_equal, fill=1.0, base=0,
                                   pattern=[[-1, P]], channel_multiplier=1).then_inc(made, 1)
            pool.wait_ge(made, 5)


def load_weights(sp, b, io, l, matrices, rows, columns, done):
    for n, w in matrices:
        sp.dma_start(w[:, l], io[f"{n}T{l}"].rearrange("(c p) n -> p c n", p=P)).then_inc(done, 16)
    for n, w in rows:
        sp.dma_start(w[:, l], io[f"{n}{l}"].rearrange("(a n) -> a n", a=1).to_broadcast([P, D])).then_inc(done, 16)
    for n, w in columns:
        sp.dma_start(w[:, l], io[f"{n}{l}"]).then_inc(done, 16)
    return len(matrices) + len(rows) + len(columns)


def load_rest(sp, b, io):
    for dst, src in ((b.x[:, :, :], io["x"].rearrange("(t p) d -> p t d", p=P)),
                     (b.kconst[:, :], io["kconst"]), (b.tri[:, :], io["tri"])):
        sp.dma_start(dst, src).then_inc(b.rest_in, 16)
    n = load_weights(sp, b, io, 0, (("wq", b.wq), ("wo", b.wo)), (("bo", b.bo),), (("bq", b.bq),), b.rest_in)
    return 3 + n + load_weights(sp, b, io, 1, (("wq", b.wq), ("wk", b.wk), ("wv", b.wv), ("wo", b.wo)),
                                (("bv", b.bv), ("bo", b.bo)), (("bq", b.bq), ("bk", b.bk)), b.rest_in)


def keys_values(nc, b, io, l):
    b.used = 0
    b.ks = b.carve([P, H, SKP], bf16)
    b.v = b.carve([P, KT, H * 32])
    b.lin = b.carve([P, H * 32])
    b.attn_at = b.used
    if l == 0:
        ktok = b.carve([P, KT, D])
        bk_row = b.carve([P, D])
        own = b.carve([P, H // DC])
    ctxT = b.carve([P, DC, SK])
    kf = b.carve([P, SK])
    rest = b.carve([P, SK])
    parts = b.carve([P, 3, SKP], bf16)
    mask = b.carve([P, SKP])
    mask8 = b.carve([P, SK], u8)
    if l == 1:
        const = b.carve([P, SKP], bf16)
    n = f"kv{l}_"
    loaded, prod, evac, chain, ready, stored, placed, vprod, vevac, vzero = (b.sem(n + x) for x in (
        "loaded", "prod", "evac", "chain", "ready", "stored", "placed", "vprod", "vevac", "vzero"))
    lin_made, lin_out, const_made = b.sem(n + "lin_made"), b.sem(n + "lin_out"), b.sem(n + "const_made")
    NVE = 2 - l
    NLOAD = 32 if l else 64
    with nc.Block() as block:
        @block.sync
        def _(sp):
            sp.dma_start(ctxT, io["ctxT"].rearrange("(c p) n -> p c n", p=P)).then_inc(loaded, 16)
            sp.dma_start(mask8, io["mask"].to_broadcast([P, SK])).then_inc(loaded, 16)
            if l == 0:
                sp.dma_start(bk_row, io["bk_row"].to_broadcast([P, D])).then_inc(loaded, 16)
                sp.dma_start(own, io["own"]).then_inc(loaded, 16)
                rest_loads = load_rest(sp, b, io)
            for m in range(DC):
                sp.wait_ge(ready, m + 1)
                sp.dma_start(b.kd[l][:, m * P:(m + 1) * P, :].rearrange("r p n -> p r n"),
                             parts[:, :, 0:SK]).then_inc(stored, 16)
                sp.wait_ge(stored, 16 * (m + 1))
                if m == 0:
                    sp.wait_ge(vzero, 5)
                    if l == 1:
                        sp.wait_ge(const_made, 1)
                        sp.dma_start(b.ks[ROW_MASK:ROWS_ALL, :, :],
                                     const[ROW_MASK:ROWS_ALL, :].rearrange("p (a n) -> p a n", a=1)
                                     .to_broadcast([ROWS_ALL - ROW_MASK, H, SKP])).then_inc(placed, 16)
                hs = slice(m * H // DC, (m + 1) * H // DC)
                for r in range(NB):
                    sp.dma_start(b.ks[r * HD:(r + 1) * HD, hs, 0:SK],
                                 b.kd[l][KPART[r], m * P:(m + 1) * P, :].rearrange("(h d) n -> d h n", d=HD)
                                 ).then_inc(placed, 16)
            sp.wait_ge(placed, 16 * (DC * NB + l))
            if l == 0:
                sp.wait_ge(b.rest_in, 16 * rest_loads)

        @block.tensor
        def _(pe):
            pe.wait_ge(loaded, NLOAD)
            if l == 0:
                pe.wait_ge(b.first_in, 16 * b.first_loads)
            u = 0
            for m in range(DC):
                for at, width in KCOLS:
                    if u >= 4:
                        pe.wait_ge(evac, u - 3)
                    for kk in range(DC):
                        mm = pe.matmul(b.bank[u % 4][:, 0:width], b.wk[:, l, kk, m * P:(m + 1) * P],
                                       ctxT[:, kk, at:at + width], start=(kk == 0), stop=(kk == DC - 1))
                    mm.then_inc(prod, 1)
                    u += 1
            for k in range(KT):
                if k >= 4:
                    pe.wait_ge(vevac, NVE * (k - 3))
                for side, w in enumerate((b.wv, b.wk)[:NVE]):
                    for kk in range(DC):
                        mm = pe.matmul(b.bank[4 + k % 4][0:KROWS[k], side * D:(side + 1) * D],
                                       ctxT[:, kk, k * P:k * P + KROWS[k]], w[:, l, kk, :],
                                       start=(kk == 0), stop=(kk == DC - 1))
                mm.then_inc(vprod, 1)
            if l == 0:
                pe.wait_ge(vzero, 5)
                pe.wait_ge(vevac, NVE * KT)
                for m in range(DC):
                    for k in range(KT):
                        mm = pe.matmul(b.bank[m][:, 0:H * 32 // DC], ktok[0:KROWS[k], k, m * P:(m + 1) * P],
                                       b.v[0:KROWS[k], k, m * H * 32 // DC:(m + 1) * H * 32 // DC],
                                       start=(k == 0), stop=(k == KT - 1))
                    mm.then_inc(lin_made, 1)

        @block.gpsimd
        def _(pool):
            v4 = b.v.rearrange("p k (h c) -> p (k h) c", c=32)
            full = (KT - 1) * H
            pool.memset(v4[:, 0:full, 16:32], 0.0).then_inc(vzero, 1)
            pool.wait_ge(vzero, 1)
            pool.memset(v4[:, full:KT * H, :], 0.0).then_inc(vzero, 1)
            pool.wait_ge(vzero, 2)
            pool.memset(v4[:, 0:full, 16:17], 1.0).then_inc(vzero, 1)
            pool.wait_ge(vzero, 3)
            pool.memset(v4[0:KROWS[-1], full:KT * H, 16:17], 1.0).then_inc(vzero, 1)
            pool.wait_ge(vzero, 4)
            pool.memset(b.ks[0:ROW_MASK, :, SK - 1:SKP], 0.0).then_inc(vzero, 1)
            pool.wait_ge(vzero, 5)

        @block.vector
        def _(dve):
            count = [0]

            def link(ins):
                count[0] += 1
                ins.then_inc(chain, 1)
                dve.wait_ge(chain, count[0])

            dve.wait_ge(loaded, NLOAD)
            if l == 0:
                dve.wait_ge(b.first_in, 16 * b.first_loads)
            link(dve.memset(mask[:, SK:SKP], 0.0))
            link(dve.tensor_copy(mask[:, 0:SK], mask8[:, :]))
            if l == 1:
                rows = slice(ROW_MASK, P)
                dve.tensor_scalar(const[rows, :], mask[rows, :], b.kconst[rows, 0:1], b.kconst[rows, 1:2],
                                  ALU.mult, ALU.add).then_inc(const_made, 1)
            out_of = [0]

            def values_out(tiles):
                for k in range(out_of[0], out_of[0] + tiles):
                    dve.wait_ge(vprod, k + 1)
                    if k == KT - 1:
                        dve.wait_ge(vzero, 2)
                    n = KROWS[k]
                    dve.tensor_tensor(b.v[0:n, k, :].rearrange("p (h c) -> p h c", c=32)[:, :, 0:HD],
                                      b.bank[4 + k % 4][0:n, 0:D].rearrange("p (h c) -> p h c", c=HD),
                                      b.bv[0:n, l, :].rearrange("p (h c) -> p h c", c=HD),
                                      ALU.add).then_inc(vevac, 1)
                    if l == 0:
                        dve.tensor_tensor(ktok[0:n, k, :], b.bank[4 + k % 4][0:n, D:2 * D], bk_row[0:n, :],
                                          ALU.add).then_inc(vevac, 1)
                out_of[0] += tiles

            u = 0
            for m in range(DC):
                for at, width in KCOLS:
                    dve.wait_ge(prod, u + 1)
                    if l == 0:
                        ins = dve.tensor_scalar(kf[:, at:at + width], b.bank[u % 4][:, 0:width],
                                                b.bk[:, l, m:m + 1], None, ALU.add)
                    else:
                        ins = dve.scalar_tensor_tensor(out=kf[:, at:at + width], in0=b.bank[u % 4][:, 0:width],
                                                       scalar=b.bk[:, l, m:m + 1], in1=mask[:, at:at + width],
                                                       op0=ALU.add, op1=ALU.mult)
                    ins.then_inc(evac, 1)
                    u += 1
                dve.wait_ge(evac, u)
                if m >= 1:
                    values_out(4)
                    dve.wait_ge(stored, 16 * m)
                src = kf
                for r in range(3):
                    ins = dve.tensor_copy(parts[:, r, 0:SK], src[:, :])
                    if r == 2:
                        ins.then_inc(ready, 1)
                    else:
                        link(ins)
                        link(dve.tensor_tensor(rest[:, :], src[:, :], parts[:, r, 0:SK], ALU.subtract))
                        src = rest
                    if m >= 1:
                        values_out(2)
            values_out(KT - out_of[0])
            dve.wait_ge(vevac, NVE * KT)
            if l == 0:
                for m in range(DC):
                    dve.wait_ge(lin_made, m + 1)
                    w = H * 32 // DC
                    dve.tensor_tensor(b.lin[:, m * w:(m + 1) * w].rearrange("p (h c) -> p h c", c=32),
                                      b.bank[m][:, 0:w].rearrange("p (h c) -> p h c", c=32),
                                      own.rearrange("p (h a) -> p h a", a=1).to_broadcast([P, H // DC, 32]),
                                      ALU.mult).then_inc(lin_out, 1)
                dve.wait_ge(lin_out, DC)


def norm_stats(dve, b, c, s, src):
    for j in range(TC):
        dve.bn_stats(b.stats[:, j, :], src[:, bass.ds(c * TC + j, 1), :].rearrange("p a d -> p (a d)")
                     ).then_inc(s.stat, 1)
    dve.wait_ge(s.stat, c * STATS + TC)
    even, odd = b.stats[:, :, 0:3], b.stats[:, :, 3:6]
    dve.tensor_tensor(b.mv[:, :, 0], even[:, :, 1], odd[:, :, 1], ALU.add).then_inc(s.stat, 1)
    dve.tensor_tensor(b.mv[:, :, 1], even[:, :, 1], odd[:, :, 1], ALU.subtract).then_inc(s.stat, 1)
    dve.tensor_tensor(b.var[:, :], even[:, :, 2], odd[:, :, 2], ALU.add).then_inc(s.stat, 1)
    dve.wait_ge(s.stat, c * STATS + TC + 3)
    dve.tensor_scalar(b.mv[:, :, 0], b.mv[:, :, 0], 0.5, None, ALU.mult).then_inc(s.stat, 1)
    dve.scalar_tensor_tensor(out=b.mv[:, :, 1], in0=b.mv[:, :, 1], scalar=0.25, in1=b.mv[:, :, 1],
                             op0=ALU.mult, op1=ALU.mult).then_inc(s.stat, 1)
    dve.tensor_scalar(b.var[:, :], b.var[:, :], 1.0 / D, EPS, ALU.mult, ALU.add).then_inc(s.stat, 1)
    dve.wait_ge(s.stat, c * STATS + STATS)
    dve.tensor_tensor(b.var[:, :], b.var[:, :], b.mv[:, :, 1], ALU.add).then_inc(s.vare, 1)
    dve.wait_ge(s.root, 2 * c + 2)
    dve.tensor_tensor(b.newt[:, :], b.rstd[:, :], b.rstd[:, :], ALU.mult).then_inc(s.newton, 1)
    dve.wait_ge(s.newton, c * 4 + 1)
    dve.tensor_tensor(b.newt[:, :], b.newt[:, :], b.var[:, :], ALU.mult).then_inc(s.newton, 1)
    dve.wait_ge(s.newton, c * 4 + 2)
    dve.tensor_scalar(b.newt[:, :], b.newt[:, :], -0.5, 1.5, ALU.mult, ALU.add).then_inc(s.newton, 1)
    dve.wait_ge(s.newton, c * 4 + 3)
    dve.tensor_tensor(b.rstd[:, :], b.rstd[:, :], b.newt[:, :], ALU.mult).then_inc(s.newton, 1)
    dve.wait_ge(s.newton, c * 4 + 4)


def norm_vector(dve, b, c, s, xn, free=None):
    norm_stats(dve, b, c, s, b.x)
    if free:
        free()
    for j in range(TC):
        dve.tensor_scalar(xn(j), b.x[:, bass.ds(c * TC + j, 1), :].rearrange("p a d -> p (a d)"),
                          b.mv[:, j, 0:1], b.rstd[:, j:j + 1], ALU.subtract, ALU.mult).then_inc(s.normed, 1)


def norm_scalar(act, b, c, s):
    act.wait_ge(s.vare, c + 1)
    act.activation(b.rstd[:, :], b.var[:, :], ACT.Ln).then_inc(s.root, 1)
    act.wait_ge(s.root, 2 * c + 1)
    act.activation(b.rstd[:, :], b.rstd[:, :], ACT.Exp, scale=-0.5).then_inc(s.root, 1)


def norm_sems(b, n):
    s = Buffers()
    s.stat, s.vare, s.root, s.newton, s.normed = (b.sem(n + x) for x in (
        "stat", "vare", "root", "newton", "normed"))
    return s


def queries(nc, b, io, l):
    b.used = b.attn_at
    xn = b.carve([P, TC, D])
    qf = b.carve([P, DC, QC])
    rest = b.carve([P, QC])
    parts = b.carve([P, 3, DC, QC], bf16)
    n = f"q{l}_"
    s = norm_sems(b, n)
    turned, copied, prod, evac, chain, ready, stored = (b.sem(n + x) for x in (
        "turned", "copied", "prod", "evac", "chain", "ready", "stored"))
    NST = 16 * (4 - l)
    with nc.Block() as block:
        @block.sync
        def _(sp):
            with sp.Fori(0, NCH) as c:
                sp.wait_ge(ready, 2 * c + 2)
                for r in range(3):
                    sp.dma_start(b.qd[l][r, :, bass.ds(c * QC, QC)].rearrange("(m p) q -> p m q", p=P),
                                 parts[:, r]).then_inc(stored, 16)
                if l == 0:
                    sp.dma_start(b.q32[:, bass.ds(c * QC, QC)].rearrange("(m p) q -> p m q", p=P), qf
                                 ).then_inc(stored, 16)
            sp.wait_ge(stored, NST * NCH)

        @block.scalar
        def _(act):
            act.preload_act_table_set(LN_EXP)

            def copy_turned(c):
                for kk in range(DC):
                    act.wait_ge(turned, DC * c + kk + 1)
                    act.activation(b.xnT[:, kk, :], b.bank[kk][:, :], ACT.Copy).then_inc(copied, 1)

            norm_scalar(act, b, 0, s)
            with act.Fori(0, NCH - 1) as c:
                copy_turned(c)
                norm_scalar(act, b, c + 1, s)
            copy_turned(NCH - 1)

        @block.tensor
        def _(pe):
            with pe.Fori(0, NCH) as c:
                pe.wait_ge(s.normed, TC * c + TC)
                for kk in range(DC):
                    for j in range(TC):
                        mm = pe.transpose(b.bank[kk][:, j * P:(j + 1) * P], xn[:, j, kk * P:(kk + 1) * P],
                                          b.ident[:, :])
                    mm.then_inc(turned, 1)
                pe.wait_ge(copied, DC * c + DC)
                for m in range(DC):
                    for kk in range(DC):
                        mm = pe.matmul(b.bank[2 + m][:, :], b.wq[:, l, kk, m * P:(m + 1) * P],
                                       b.xnT[:, kk, :], start=(kk == 0), stop=(kk == DC - 1))
                    mm.then_inc(prod, 1)
                pe.wait_ge(evac, DC * c + DC)

        @block.vector
        def _(dve):
            def norm(c, free=None):
                norm_vector(dve, b, c, s, lambda j: xn[:, j, :], free=free)

            def norm_next(c):
                norm(c + 1, lambda: dve.wait_ge(turned, DC * c + DC))

            def split(c):
                k = 0
                for m in range(DC):
                    dve.wait_ge(prod, DC * c + m + 1)
                    dve.tensor_scalar(qf[:, m, :], b.bank[2 + m][:, :], b.bq[:, l, m:m + 1], HD ** -0.5,
                                      ALU.add, ALU.mult).then_inc(evac, 1)
                    dve.wait_ge(evac, DC * c + m + 1)
                    src = qf[:, m, :]
                    for r in range(3):
                        ins = dve.tensor_copy(parts[:, r, m, :], src)
                        if r == 2:
                            ins.then_inc(ready, 1)
                        else:
                            ins.then_inc(chain, 1)
                            k += 1
                            dve.wait_ge(chain, 8 * c + k)
                            dve.tensor_tensor(rest[:, :], src, parts[:, r, m, :],
                                              ALU.subtract).then_inc(chain, 1)
                            k += 1
                            dve.wait_ge(chain, 8 * c + k)
                            src = rest[:, :]
                    dve.wait_ge(ready, 2 * c + m + 1)
                assert k == 8

            norm(0)
            norm_next(0)
            split(0)
            with dve.Fori(1, NCH - 1) as c:
                norm_next(c)
                dve.wait_ge(stored, NST * c)
                split(c)
            dve.wait_ge(stored, NST * (NCH - 1))
            split(NCH - 1)


def load_queries(sp, b, l, q, c, g, loaded):
    for r in range(NB):
        sp.dma_start(q[r * HD:(r + 1) * HD, g * HG:(g + 1) * HG, :],
                     b.qd[l][QPART[r], g * HG * HD:(g + 1) * HG * HD, bass.ds(c * QC, QC)]
                     .rearrange("(h d) q -> d h q", d=HD)).then_inc(loaded[g], 16)


def key_tile(i):
    g, r = divmod(i, U)
    k, j = divmod(r, HG)
    return g, k, j


def value_product(pe, b, ring, nw, g, k, acc, done):
    for j in range(HG):
        h = g * HG + j
        i = (g * KT + k) * HG + j
        mm = pe.matmul(acc[32 * j:32 * j + 32, :], b.v[:, k, 32 * h:32 * h + 32],
                       ring[:, i % nw, :], start=(k == 0), stop=(k == KT - 1))
    mm.then_inc(done, 1)


def finish_sems(b, n):
    f = Buffers()
    f.acc_out, f.turned, f.recip, f.scaled, f.turned2, f.copied2, f.proj, f.added, f.resid = (
        b.sem(n + x) for x in ("acc_out", "turned", "recip", "scaled", "turned2", "copied2", "proj",
                               "added", "resid"))
    return f


class Finish:

    def __init__(self, b, l, f, accs):
        self.b, self.l, self.f, self.accs = b, l, f, accs
        self.rsum = [b.carve([P, H]) for _ in range(2)]
        self.att = [b.carve([P, D]) for _ in range(2)]
        self.attT = [b.carve([P, DC, P]) for _ in range(2)]
        self.out = [b.carve([P, D]) for _ in range(2)]

    def tensor(self, pe, step, c, t, o):
        b, f = self.b, self.f
        if step == 1:
            pe.wait_ge(f.acc_out, G * c + G)
            for g in range(G):
                mm = pe.transpose(o[:, g * P:(g + 1) * P], self.accs[:, g, t * P:(t + 1) * P], b.ident[:, :])
            mm.then_inc(f.turned, 1)
        elif step == 2:
            pe.wait_ge(f.scaled, TC * c + t + 1)
            for kk in range(DC):
                mm = pe.transpose(o[:, kk * P:(kk + 1) * P], self.att[t % 2][:, kk * P:(kk + 1) * P], b.ident[:, :])
            mm.then_inc(f.turned2, 1)
        else:
            pe.wait_ge(f.copied2, TC * c + t + 1)
            for kk in range(DC):
                mm = pe.matmul(o[:, 0:D], self.attT[t % 2][:, kk, :], b.wo[:, self.l, kk, :],
                               start=(kk == 0), stop=(kk == DC - 1))
            mm.then_inc(f.proj, 1)

    def vector(self, dve, step, c, t, o):
        b, f = self.b, self.f
        if step == 1:
            dve.wait_ge(f.turned, TC * c + t + 1)
            rows = o[:, 0:32 * H].rearrange("p (h c) -> p h c", c=32)
            dve.reciprocal(self.rsum[t % 2][:, :], rows[:, :, HD]).then_inc(f.recip, 1)
            dve.wait_ge(f.recip, TC * c + t + 1)
            dve.tensor_tensor(self.att[t % 2].rearrange("p (h c) -> p h c", c=HD), rows[:, :, 0:HD],
                              self.rsum[t % 2].rearrange("p (h a) -> p h a", a=1).to_broadcast([P, H, HD]),
                              ALU.mult).then_inc(f.scaled, 1)
        elif step == 3:
            dve.wait_ge(f.proj, TC * c + t + 1)
            dve.tensor_tensor(self.out[t % 2][:, :], o[:, 0:D], b.bo[:, self.l, :], ALU.add).then_inc(f.added, 1)
            dve.wait_ge(f.added, TC * c + t + 1)
            row = tile_of(b.x, c, t)
            dve.tensor_tensor(row, row, self.out[t % 2][:, :], ALU.add).then_inc(f.resid, 1)

    def scalar(self, act, step, c, t, o):
        if step == 2:
            act.wait_ge(self.f.turned2, TC * c + t + 1)
            act.activation(self.attT[t % 2].rearrange("p a q -> p (a q)"), o[:, 0:D], ACT.Copy
                           ).then_inc(self.f.copied2, 1)

    def turned_back(self, dve, step, c, t, o):
        if step == 2:
            dve.wait_ge(self.f.turned2, TC * c + t + 1)
            dve.tensor_copy(self.attT[t % 2].rearrange("p a q -> p (a q)"), o[:, 0:D]).then_inc(self.f.copied2, 1)

    def freed(self, step, c, t):
        return ((self.f.scaled, self.f.copied2, self.f.added)[step - 1], TC * c + t + 1)


FSTEPS = [(t, step) for two in range(0, TC, 2) for step in (1, 2, 3) for t in (two, two + 1)]


def attention0(nc, b, io):
    b.used = b.attn_at
    q = b.carve([P, H, QC], bf16)
    q32 = b.carve([P, DC, QC])
    NN, NE = 2, 4
    nring = b.carve([P, NN * HG, QC])
    ering = b.carve([P, NE * HG, QC])
    accs = b.carve([P, G, QC])
    n = "a0_"
    scored, clipped, logged, exped, valued_n, valued_e = (b.sem(n + x) for x in (
        "scored", "clipped", "logged", "exped", "valued_n", "valued_e"))
    loaded = [b.sem(f"{n}loaded{g}") for g in range(G)]
    loaded32 = [b.sem(f"{n}loaded32_{m}") for m in range(DC)]
    f = finish_sems(b, n)
    fin = Finish(b, 0, f, accs)
    NV = G * KT
    PG = U // 2
    NS = 2
    ACC, FIN = [b.bank[4], b.bank[5]], [b.bank[6], b.bank[7]]
    LAG_N, LAG_E = 1, 4
    OUT = 2 * LAG_E + 1
    AT = [OUT + 1 + 2 * n for n in range(len(FSTEPS))]
    assert AT[-1] < PG + OUT and PC2 % NS == 0 and NV % NN == 0 and NV % NE == 0

    def unit(x, v):
        return x.rearrange("p a q -> p (a q)")[:, v % (x.shape[1] // HG) * HG * QC:][:, 0:HG * QC]

    def pair(i):
        return b.psum[:, 2 * QC * (i % NS):2 * QC * (i % NS + 1)]

    zero = b.sem("a0_zero")
    zeros = b.xnT.rearrange("p a q -> p (a q)")

    with nc.Block() as block:
        @block.gpsimd
        def _(pool):
            pool.memset(zeros, 0.0).then_inc(zero, 1)

        @block.sync
        def _(sp):
            def clear_sorted():
                sp.wait_ge(zero, 1)
                n = 0
                for xs in b.xs:
                    flat = xs.rearrange("(p a) d -> p (a d)", p=P)
                    for at in range(0, xs.shape[0] // P * D, DC * QC):
                        sp.dma_start(flat[:, at:at + DC * QC], zeros).then_inc(b.cleared, 16)
                        n += 1
                return n

            def load32(c, m):
                sp.dma_start(q32[:, m, :], b.q32[m * P:(m + 1) * P, bass.ds(c * QC, QC)]
                             ).then_inc(loaded32[m], 16)

            for g in range(G):
                load_queries(sp, b, 0, q, 0, g, loaded)
                if g % 2 == 0:
                    load32(0, g // 2)
            stores = clear_sorted()
            with sp.Fori(1, NCH) as c:
                for g in range(G):
                    sp.wait_ge(scored, (c - 1) * PC2 + (g + 1) * PG)
                    load_queries(sp, b, 0, q, c, g, loaded)
                    if g % 2 == 1:
                        load32(c, g // 2)
            sp.wait_ge(b.cleared, 16 * stores)

        @block.tensor
        def _(pe):
            def times_values(ring, v, stop=False):
                g, k = divmod(v % NV, KT)
                for j in range(HG):
                    h = g * HG + j
                    mm = pe.matmul(ACC[g % 2][32 * j:32 * j + 32, :], b.v[:, k, 32 * h:32 * h + 32],
                                   unit(ring, v)[:, j * QC:(j + 1) * QC], start=False, stop=stop)
                return mm

            def values_n(c, v):
                first = isinstance(c, int) and c == 0
                g, k = divmod(v % NV, KT)
                if k == 0:
                    if not (first and g < 2):
                        pe.wait_ge(f.acc_out, G * (c + v // NV) + g - 1)
                    pe.wait_ge(loaded32[g // 2], 16 * (c + v // NV + 1))
                    for j in range(HG):
                        h = g * HG + j
                        pe.matmul(ACC[g % 2][32 * j:32 * j + 32, :], b.lin[:, 32 * h:32 * h + 32],
                                  q32[:, g // 2, :], start=True, stop=False)
                pe.wait_ge(clipped, c * PC2 + 2 * (v + 1))
                times_values(nring, v).then_inc(valued_n, 1)

            def values_e(c, v):
                pe.wait_ge(exped, c * NV + v + 1)
                times_values(ering, v, stop=v % KT == KT - 1).then_inc(valued_e, 1)

            def finish(c, t, step):
                n = FSTEPS.index((t, step))
                if n >= 2:
                    s, v = fin.freed(FSTEPS[n - 2][1], c, FSTEPS[n - 2][0])
                    pe.wait_ge(s, v)
                fin.tensor(pe, step, c, t, FIN[n % 2])

            def chunk(c, first):
                for i in range(PC2):
                    if i % PG == 0:
                        pe.wait_ge(loaded[i // PG], 16 * NB * (c + 1))
                    if i >= NS or not first:
                        pe.wait_ge(clipped, c * PC2 + i - NS + 1)
                    for u in (2 * i, 2 * i + 1):
                        g, k, j = key_tile(u)
                        mm = pe.matmul(pair(i)[:, QC * (u % 2):QC * (u % 2 + 1)],
                                       b.ks[0:ROW_MASK, g * HG + j, k * P:(k + 1) * P],
                                       q[0:ROW_MASK, g * HG + j, :], start=True, stop=True)
                    mm.then_inc(scored, 1)
                    if i % 2 == 1:
                        v = i // 2
                        if v >= LAG_N or not first:
                            values_n(c, v - LAG_N)
                        if v >= LAG_E or not first:
                            values_e(c, v - LAG_E)
                    if not first and i in AT:
                        t, step = FSTEPS[AT.index(i)]
                        finish(c - 1, t, step)

            chunk(0, True)
            with pe.Fori(1, NCH) as c:
                chunk(c, False)
            for v in range(NV - LAG_N, NV):
                values_n(NCH - 1, v)
            for v in range(NV - LAG_E, NV):
                values_e(NCH - 1, v)
            for t, step in FSTEPS:
                finish(NCH - 1, t, step)

        @block.vector
        def _(dve):
            def sums_out(c, g):
                dve.wait_ge(valued_e, c * NV + (g + 1) * KT)
                dve.tensor_copy(accs[:, g % G, :], ACC[g % 2]).then_inc(f.acc_out, 1)

            def chunk(c, first):
                for i in range(PC2):
                    v = i // 2
                    dve.wait_ge(scored, c * PC2 + i + 1)
                    if i % 2 == 0 and (v >= NN or not first):
                        dve.wait_ge(valued_n, c * NV + v - NN + 1)
                        dve.wait_ge(logged, c * NV + v - NN + 1)
                    dve.tensor_scalar(unit(nring, v)[:, 2 * QC * (i % 2):2 * QC * (i % 2 + 1)], pair(i), -1.0, 0.0,
                                      ALU.mult, ALU.max).then_inc(clipped, 1)
                    if i % PG == OUT and (i >= PG or not first):
                        if i // PG == 1 and not first:
                            dve.wait_ge(f.turned, TC * c)
                        sums_out(c, i // PG - 1)
                    if not first and i in AT:
                        t, step = FSTEPS[AT.index(i)]
                        fin.vector(dve, step, c - 1, t, FIN[FSTEPS.index((t, step)) % 2])
                        fin.turned_back(dve, step, c - 1, t, FIN[FSTEPS.index((t, step)) % 2])

            chunk(0, True)
            with dve.Fori(1, NCH) as c:
                chunk(c, False)
            sums_out(NCH - 1, G - 1)
            for t, step in FSTEPS:
                fin.vector(dve, step, NCH - 1, t, FIN[FSTEPS.index((t, step)) % 2])
                fin.turned_back(dve, step, NCH - 1, t, FIN[FSTEPS.index((t, step)) % 2])
            dve.wait_ge(f.resid, TC * NCH)

        @block.scalar
        def _(act):
            act.preload_act_table_set(LN_EXP)

            def log(c, v, first):
                act.wait_ge(clipped, c * PC2 + 2 * (v + 1))
                if v >= NE or not first:
                    act.wait_ge(valued_e, c * NV + v - NE + 1)
                act.activation(unit(ering, v), unit(nring, v), ACT.Ln, bias=1.0).then_inc(logged, 1)

            def exp(c, v):
                act.wait_ge(logged, c * NV + v + 1)
                act.activation(unit(ering, v), unit(ering, v), ACT.Exp, scale=-1.0).then_inc(exped, 1)

            def chunk(c, first):
                for v in range(NV):
                    log(c, v, first)
                    if v >= 1 or not first:
                        exp(c, v - 1)

            chunk(0, True)
            with act.Fori(1, NCH) as c:
                chunk(c, False)
            exp(NCH - 1, NV - 1)


AHEAD = 8
LAG_TURN = 3


def maximum_items(g, groups):
    items = [("half", g + 1, m) for m in range(AHEAD, 2 * HG * TC)]
    items += [("half", g + 2, m) for m in range(LAG_TURN)]
    items += [("turn", g + 1)]
    items += [("half", g + 2, m) for m in range(LAG_TURN, AHEAD)]
    return [x for x in items if x[1] < groups]


def slot_items(first, last):
    items, after = [], []
    for g in range(G):
        mine = maximum_items(g, G if last else 2 * G)
        if g == 0 and not first:
            for n, (t, s) in enumerate(FSTEPS):
                mine.insert(6 + 3 * n, ("finish", -1, t, s))
        span = U if mine and mine[-1][0] == "half" else U - 6
        items += mine
        after += [g * U + (span * (n + 1)) // len(mine) for n in range(len(mine))]
    if last:
        items += [("finish", 0, t, s) for t, s in FSTEPS]
        after += [UC] * len(FSTEPS)
    assert last or len(items) % 2 == 0
    return list(zip(items, after))


def attention1(nc, b, io):
    b.used = b.attn_at
    q = b.carve([P, H, QC], bf16)
    ring = b.carve([P, NW, QC])
    accs = b.carve([P, G, QC])
    mx2 = b.carve([P, HG * TC, 2])
    mx = b.carve([P, HG * TC])
    mparts = b.carve([P, P], bf16)
    mrows = b.carve([3 * HG * TC, P], bf16)
    n = "a1_"
    ones, zeroed, scored, exped, valued, mscored, mread, mchain, mcut, mturned, mcopied, placed = (
        b.sem(n + x) for x in ("ones", "zeroed", "scored", "exped", "valued", "mscored", "mread", "mchain",
                               "mcut", "mturned", "mcopied", "placed"))
    loaded = [b.sem(f"{n}loaded{g}") for g in range(G)]
    f = finish_sems(b, n)
    fin = Finish(b, 1, f, accs)
    NPV = G * KT
    MU = HG * TC
    MH = 2 * MU
    HALVES = [(0, SK // 2 + SK % 2 + 1), (SK // 2 + SK % 2 + 1, SK)]
    ACC = b.bank[7]
    slot = [b.psum[:, 512 * (NS1 + 2 * k):512 * (NS1 + 2 * k + 2)] for k in range(2)]
    slot_rows = [x[:, 0:P // 2].bitcast(bf16) for x in slot]
    BEFORE = maximum_items(-1, 2 * G)
    BEFORE = [("half", 0, m) for m in range(AHEAD)] + BEFORE
    assert len(BEFORE) % 2 == 1 and UC % NW == 0

    def chunks(engine, chunk):
        chunk(0, slot_items(True, False))
        with engine.Fori(1, NCH - 1) as c:
            chunk(c, slot_items(False, False))
        chunk(NCH - 1, slot_items(False, True))

    with nc.Block() as block:
        @block.gpsimd
        def _(pool):
            pool.memset(mparts[:, :], 0.0).then_inc(zeroed, 1)
            pool.wait_ge(zeroed, 1)
            pool.memset(q[ROW_MASK:P, :, :], 1.0).then_inc(ones, 1)

        @block.sync
        def _(sp):
            def place(c, d):
                sp.wait_ge(mcopied, c * G + d + 1)
                g = d % G
                for r in range(3):
                    sp.dma_start(q[ROW_MAX + r:ROW_MAX + r + 1, g * HG:(g + 1) * HG, :]
                                 .rearrange("a h (t q) -> a (h t) q", q=P),
                                 mrows[r * MU:(r + 1) * MU, :]).then_inc(placed, 16)

            sp.wait_ge(ones, 1)
            for g in range(G):
                load_queries(sp, b, 1, q, 0, g, loaded)
            place(0, 0)
            with sp.Fori(0, NCH - 1) as c:
                for g in range(G):
                    place(c, g + 1)
                    sp.wait_ge(scored, c * UC + (g + 1) * U)
                    load_queries(sp, b, 1, q, c + 1, g, loaded)
            for g in range(G - 1):
                place(NCH - 1, g + 1)

        @block.tensor
        def _(pe):
            pe.wait_ge(ones, 1)

            def slot_free(c, item):
                if item[0] == "half":
                    pe.wait_ge(mread, (c * G + item[1]) * MH + item[2] + 1)
                elif item[0] == "turn":
                    pe.wait_ge(mcopied, c * G + item[1] + 1)
                else:
                    s, v = fin.freed(item[3], c + item[1], item[2])
                    pe.wait_ge(s, v)

            def make(c, item, k):
                if item[0] == "half":
                    _, d, m = item
                    j, t = divmod(m // 2, TC)
                    h = d % G * HG + j
                    if m == 0:
                        pe.wait_ge(loaded[d % G], 16 * NB * (c + d // G + 1))
                    lo, hi = HALVES[m % 2]
                    for at in (lo, lo + 512):
                        to = min(at + 512, hi)
                        mm = pe.matmul(slot[k][:, at - lo:to - lo], q[0:ROW_MAX, h, t * P:(t + 1) * P],
                                       b.ks[0:ROW_MAX, h, at:to], start=True, stop=True)
                    mm.then_inc(mscored, 1)
                elif item[0] == "turn":
                    pe.wait_ge(mcut, c * G + item[1] + 1)
                    pe.transpose(slot_rows[k], mparts, b.identb[:, :]).then_inc(mturned, 1)
                else:
                    fin.tensor(pe, item[3], c + item[1], item[2], slot[k])

            def values(c, v):
                g, k = divmod(v % NPV, KT)
                pe.wait_ge(exped, c * UC + HG * (v + 1))
                if k == 0 and not (isinstance(c, int) and c == 0 and g == 0):
                    pe.wait_ge(f.acc_out, G * c + g)
                value_product(pe, b, ring, NW, g, k, ACC, valued)

            def chunk(c, items):
                todo = 0
                for i in range(UC):
                    g, k, j = key_tile(i)
                    h = g * HG + j
                    if i % U == 0:
                        pe.wait_ge(placed, 48 * (c * G + g + 1))
                    if i >= NS1:
                        pe.wait_ge(exped, c * UC + i - NS1 + 1)
                    elif not (isinstance(c, int) and c == 0):
                        pe.wait_ge(exped, c * UC)
                    pe.matmul(b.bank[i % NS1][:, :], b.ks[0:ROWS_ALL, h, k * P:(k + 1) * P],
                              q[0:ROWS_ALL, h, :], start=True, stop=True).then_inc(scored, 1)
                    while todo < len(items) and items[todo][1] <= i + 1:
                        slot_free(c, items[todo - 2][0] if todo >= 2 else ("half", 1, AHEAD - 2 + todo))
                        make(c, items[todo][0], todo % 2)
                        todo += 1
                    if i % HG == 2 and (i >= HG or not (isinstance(c, int) and c == 0)):
                        values(c, i // HG - 1)
                return todo

            for k, item in enumerate(BEFORE):
                if k >= 2:
                    slot_free(0, BEFORE[k - 2])
                make(0, item, (k + 1) % 2)
            chunk(0, slot_items(True, False))
            with pe.Fori(1, NCH - 1) as c:
                chunk(c, slot_items(False, False))
            items = slot_items(False, True)
            c = NCH - 1
            todo = chunk(c, [x for x in items if x[1] < UC])
            values(c, NPV - 1)
            for k in range(todo, len(items)):
                slot_free(c, items[k - 2][0])
                make(c, items[k][0], k % 2)

        @block.vector
        def _(dve):
            def use(c, item, k):
                if item[0] == "half":
                    _, d, m = item
                    group = c * G + d
                    dve.wait_ge(mscored, group * MH + m + 1)
                    lo, hi = HALVES[m % 2]
                    dve.tensor_reduce(mx2[:, m // 2, m % 2:m % 2 + 1], slot[k][:, 0:hi - lo], AX.X,
                                      ALU.max).then_inc(mread, 1)
                    if m == MH - 1:
                        cut(group)
                elif item[0] == "turn":
                    _, d = item
                    dve.wait_ge(mturned, c * G + d + 1)
                    if not (isinstance(c, int) and c * G + d == 0):
                        dve.wait_ge(placed, 48 * (c * G + d))
                    dve.tensor_copy(mrows[:, :], slot_rows[k][0:3 * MU, :]).then_inc(mcopied, 1)
                else:
                    fin.vector(dve, item[3], c + item[1], item[2], slot[k])

            def cut(group):
                dve.wait_ge(mread, (group + 1) * MH)
                dve.tensor_tensor(mx[:, :], mx2[:, :, 0], mx2[:, :, 1], ALU.max).then_inc(mchain, 1)
                dve.wait_ge(mchain, group * 5 + 1)
                for r in range(3):
                    ins = dve.tensor_copy(mparts[:, r * MU:(r + 1) * MU], mx[:, :])
                    if r == 2:
                        ins.then_inc(mcut, 1)
                        dve.wait_ge(mcut, group + 1)
                    else:
                        ins.then_inc(mchain, 1)
                        dve.wait_ge(mchain, group * 5 + 2 * r + 2)
                        dve.tensor_tensor(mx[:, :], mx[:, :], mparts[:, r * MU:(r + 1) * MU], ALU.subtract
                                          ).then_inc(mchain, 1)
                        dve.wait_ge(mchain, group * 5 + 2 * r + 3)

            dve.wait_ge(zeroed, 1)
            for k, item in enumerate(BEFORE):
                use(0, item, (k + 1) % 2)
            chunks(dve, lambda c, items: [use(c, item, k % 2) for k, (item, _) in enumerate(items)])
            dve.wait_ge(f.resid, TC * NCH)

        @block.scalar
        def _(act):
            act.preload_act_table_set(LN_EXP)

            def sums_out(c, g):
                act.wait_ge(valued, c * NPV + (g + 1) * KT)
                act.activation(accs[:, g % G, :], ACC, ACT.Copy).then_inc(f.acc_out, 1)

            def chunk(c, items):
                first = isinstance(c, int) and c == 0
                for i in range(UC):
                    act.wait_ge(scored, c * UC + i + 1)
                    if i >= NW or not first:
                        act.wait_ge(valued, c * NPV + (i - NW) // HG + 1)
                    act.activation(ring[:, i % NW, :], b.bank[i % NS1][:, :], ACT.Exp
                                   ).then_inc(exped, 1)
                    if i % U == OUT1 and (i >= U or not first):
                        if i // U == 1 and not first:
                            act.wait_ge(f.turned, TC * c)
                        sums_out(c, i // U - 1)
                    for k, (item, after) in enumerate(items):
                        if item[0] == "finish" and item[1] == -1 and after == i + 1:
                            fin.scalar(act, item[3], c - 1, item[2], slot[k % 2])

            chunks(act, chunk)
            c = NCH - 1
            sums_out(c, G - 1)
            for k, (item, after) in enumerate(slot_items(False, True)):
                if item[0] == "finish" and item[1] == 0:
                    fin.scalar(act, item[3], c, item[2], slot[k % 2])


def tile_of(x, c, j):
    return x[:, bass.ds(c * TC + j, 1), :].rearrange("p a d -> p (a d)")


def route(nc, b, io, l):
    top = l + 1
    NA, T = routing(top)
    b.used = 0
    b.shared = b.carve([P, NT, D])
    b.expert_at = b.used
    xn = b.carve([P, TC, D])
    xall = b.carve([P, NT, D])
    logits = b.carve([P, NT, E])
    logit_bias = b.carve([P, TC * E])
    gate_w = b.carve([P, DC, E])
    shared_w = b.carve([P, DC, D])
    shared_b = b.carve([P, D])
    best = b.carve([P, NT, E])
    best_at = b.carve([P, NT, E], u32)
    at_f = b.carve([P, top, NT])
    onehot = b.carve([P, NA, E])
    iota_e = b.carve([P, E])
    iota_rows = b.carve([P, NA])
    iota_t = b.carve([P, T])
    totals = b.carve([P, NA, E])
    upto = b.carve([P, E, NA])
    fills = b.carve([P, E, NA])
    tiles = b.carve([P, E])
    ends = b.carve([P, E])
    base = b.carve([P, E])
    place = b.carve([P, NA, E])
    place_f = b.carve([P, NA])
    owner = b.carve([P, T, E])
    owner_f = b.carve([P, T])
    expd = b.carve([P, NT, E])
    n = f"r{l}_"
    s = norm_sems(b, n)
    loaded, turned, copied, kept, prod, evac, chain, onehots, counted, shifted, exped, placed, sent, act_done = (
        b.sem(n + x) for x in ("loaded", "turned", "copied", "kept", "prod", "evac", "chain", "onehots",
                               "counted", "shifted", "exped", "placed", "sent", "act_done"))
    NL = 7 if l else 5
    with nc.Block() as block:
        @block.sync
        def _(sp):
            sp.dma_start(gate_w, io[f"gate{l}"].rearrange("(c p) e -> p c e", p=P)).then_inc(loaded, 16)
            sp.dma_start(iota_e, io["iota"][0:1, 0:E].to_broadcast([P, E])).then_inc(loaded, 16)
            sp.dma_start(iota_rows, io["iota"][1:2, 0:NA].to_broadcast([P, NA])).then_inc(loaded, 16)
            sp.dma_start(iota_t, io["iota"][0:1, 0:T].to_broadcast([P, T])).then_inc(loaded, 16)
            if l == 0:
                src = io["gate_bias"].rearrange("(a n) -> a n", a=1)
                for j in range(TC):
                    sp.dma_start(logit_bias[:, j * E:(j + 1) * E], src.to_broadcast([P, E])).then_inc(loaded, 16)
            else:
                sp.dma_start(shared_w, io["shared_w"].rearrange("(c p) n -> p c n", p=P)).then_inc(loaded, 16)
                sp.dma_start(shared_b, io["shared_b"].rearrange("(a n) -> a n", a=1).to_broadcast([P, D])
                             ).then_inc(loaded, 16)
            sp.wait_ge(loaded, 16 * (4 + (TC if l == 0 else 2)))

        NLOAD = 16 * (4 + (TC if l == 0 else 2))

        @block.scalar
        def _(act):
            act.preload_act_table_set(LN_EXP)

            def copy_turned(c):
                for kk in range(DC):
                    act.wait_ge(turned, DC * c + kk + 1)
                    act.activation(b.xnT[:, kk, :], b.bank[kk][:, :], ACT.Copy).then_inc(copied, 1)

            norm_scalar(act, b, 0, s)
            with act.Fori(0, NCH - 1) as c:
                copy_turned(c)
                norm_scalar(act, b, c + 1, s)
            copy_turned(NCH - 1)
            act.wait_ge(shifted, 1)
            if l == 0:
                act.activation(expd[:, :, :], expd[:, :, :], ACT.Exp).then_inc(exped, 1)
            else:
                act.activation(expd[:, :, 0], expd[:, :, 0], ACT.Exp).then_inc(exped, 1)
                act.wait_ge(evac, NCH * (1 + TC))
                act.activation(b.shared[:, :, :], b.shared[:, :, :], ACT.Gelu).then_inc(act_done, 1)

        @block.tensor
        def _(pe):
            pe.wait_ge(loaded, NLOAD)
            with pe.Fori(0, NCH) as c:
                pe.wait_ge(s.normed, TC * c + TC)
                for kk in range(DC):
                    for j in range(TC):
                        mm = pe.transpose(b.bank[kk][:, j * P:(j + 1) * P], xn[:, j, kk * P:(kk + 1) * P],
                                          b.ident[:, :])
                    mm.then_inc(turned, 1)
                pe.wait_ge(copied, DC * c + DC)
                for j in range(TC):
                    for kk in range(DC):
                        mm = pe.matmul(b.bank[2][:, j * E:(j + 1) * E], b.xnT[:, kk, j * P:(j + 1) * P],
                                       gate_w[:, kk, :], start=(kk == 0), stop=(kk == DC - 1))
                mm.then_inc(prod, 1)
                if l == 1:
                    for j in range(TC):
                        for kk in range(DC):
                            mm = pe.matmul(b.bank[3 + j][:, 0:D], b.xnT[:, kk, j * P:(j + 1) * P],
                                           shared_w[:, kk, :], start=(kk == 0), stop=(kk == DC - 1))
                        mm.then_inc(prod, 1)
                pe.wait_ge(evac, (1 + TC * l) * (c + 1))
            pe.wait_ge(onehots, 1)
            flat = onehot.rearrange("p a e -> p (a e)")
            pe.matmul(b.bank[0][:, 0:NA * E], b.tri[:, :], flat, start=True, stop=True)
            pe.matmul(b.bank[1][:, 0:NA * E], b.ones[:, :], flat, start=True, stop=True).then_inc(counted, 1)

        @block.gpsimd
        def _(pool):
            with pool.Fori(0, NCH) as c:
                pool.wait_ge(s.normed, TC * c + TC)
                pool.tensor_copy(xall[:, bass.ds(c * TC, TC), :], xn[:, :, :]).then_inc(kept, 1)
            pool.wait_ge(kept, NCH)
            pool.wait_ge(placed, 1)
            for a in range(NA):
                pool.indirect_dma_start(b.xs[l][:, :], bass.IndirectOffsetOnAxis(ap=b.slot[:, a:a + 1], axis=0),
                                        xall[:, a % NT, :], None).then_inc(sent, 16)
            pool.wait_ge(sent, 16 * NA)

        @block.vector
        def _(dve):
            dve.wait_ge(loaded, NLOAD)
            flat = logits.rearrange("p t e -> p (t e)")
            def norm(c, free=None):
                norm_vector(dve, b, c, s, lambda j: xn[:, j, :], free=free)

            def logits_out(c):
                per = 1 + TC * l
                dve.wait_ge(prod, per * c + 1)
                out = flat[:, bass.ds(c * TC * E, TC * E)]
                if l == 0:
                    dve.tensor_tensor(out, b.bank[2][:, 0:TC * E], logit_bias[:, :], ALU.add).then_inc(evac, 1)
                else:
                    dve.tensor_copy(out, b.bank[2][:, 0:TC * E]).then_inc(evac, 1)
                    for j in range(TC):
                        dve.wait_ge(prod, per * c + 2 + j)
                        dve.tensor_tensor(tile_of(b.shared, c, j), b.bank[3 + j][:, 0:D], shared_b[:, :],
                                          ALU.add).then_inc(evac, 1)

            def xn_free(c):
                dve.wait_ge(turned, DC * c + DC)
                dve.wait_ge(kept, c + 1)

            norm(0)
            with dve.Fori(0, NCH - 1) as c:
                norm(c + 1, lambda: xn_free(c))
                logits_out(c)
            logits_out(NCH - 1)
            dve.wait_ge(evac, NCH * (1 + TC * l))
            count = [0]

            def link(ins):
                count[0] += 1
                ins.then_inc(chain, 1)
                dve.wait_ge(chain, count[0])

            for t in range(NT):
                ins = dve.max(best[:, t, :], logits[:, t, :])
                ins.then_inc(chain, 1)
            count[0] += NT
            dve.wait_ge(chain, count[0])
            for t in range(NT):
                dve.max_index(best_at[:, t, :], best[:, t, :], logits[:, t, :]).then_inc(chain, 1)
            count[0] += NT
            dve.wait_ge(chain, count[0])
            if l == 0:
                dve.tensor_tensor(expd[:, :, :], logits[:, :, :], best[:, :, 0:1].to_broadcast([P, NT, E]),
                                  ALU.subtract).then_inc(shifted, 1)
            else:
                dve.tensor_tensor(expd[:, :, 0], best[:, :, 1], best[:, :, 0], ALU.subtract).then_inc(shifted, 1)
            link(dve.tensor_copy(at_f[:, :, :], best_at[:, :, 0:top].rearrange("p t r -> p r t")))
            dve.tensor_tensor(onehot[:, :, :],
                              at_f.rearrange("p r (t a) -> p (r t) a", a=1).to_broadcast([P, NA, E]),
                              iota_e.rearrange("p (a e) -> p a e", a=1).to_broadcast([P, NA, E]),
                              ALU.is_equal).then_inc(onehots, 1)
            dve.wait_ge(exped, 1)
            if l == 0:
                link(dve.tensor_reduce(b.gate[:, 1, :], expd[:, :, :], AX.X, ALU.add))
                link(dve.reciprocal(b.gate[:, 0, :], b.gate[:, 1, :]))
            else:
                link(dve.tensor_scalar(b.gate[:, 1, :], expd[:, :, 0], 1.0, None, ALU.add))
                link(dve.reciprocal(b.gate[:, 0, :], b.gate[:, 1, :]))
                link(dve.tensor_tensor(b.gate[:, 1, :], expd[:, :, 0], b.gate[:, 0, :], ALU.mult))
            dve.wait_ge(counted, 1)
            link(dve.tensor_copy(totals.rearrange("p a e -> p (a e)"), b.bank[1][:, 0:NA * E]))
            for e in range(E):
                dve.tensor_tensor_scan(upto[:, e, :], b.ones[:, 0:NA], totals[:, :, e], 0.0,
                                       ALU.mult, ALU.add).then_inc(chain, 1)
            count[0] += E
            dve.wait_ge(chain, count[0])
            link(dve.tensor_tensor(fills[:, :, :], upto[:, :, NA - 1:NA].to_broadcast([P, E, NA]),
                                   iota_rows.rearrange("p (a n) -> p a n", a=1).to_broadcast([P, E, NA]),
                                   ALU.is_gt))
            link(dve.tensor_reduce(tiles[:, :], fills[:, :, :], AX.X, ALU.add))
            link(dve.tensor_tensor_scan(ends[:, :], b.ones[:, 0:E], tiles[:, :], 0.0, ALU.mult, ALU.add))
            link(dve.tensor_tensor(base[:, :], ends[:, :], tiles[:, :], ALU.subtract))
            link(dve.tensor_scalar(base[:, :], base[:, :], float(P), None, ALU.mult))
            link(dve.tensor_tensor(place.rearrange("p a e -> p (a e)"), b.bank[0][:, 0:NA * E],
                                   totals.rearrange("p a e -> p (a e)"), ALU.subtract))
            link(dve.tensor_tensor(place[:, :, :], place[:, :, :], upto.rearrange("p e a -> p a e"), ALU.add))
            link(dve.tensor_tensor(place[:, :, :], place[:, :, :],
                                   base.rearrange("p (a e) -> p a e", a=1).to_broadcast([P, NA, E]), ALU.add))
            link(dve.tensor_tensor(place[:, :, :], place[:, :, :], onehot[:, :, :], ALU.mult))
            link(dve.tensor_reduce(place_f[:, :], place[:, :, :], AX.X, ALU.add))
            dve.tensor_copy(b.slot[:, 0:NA], place_f[:, :]).then_inc(placed, 1)
            link(dve.tensor_tensor(owner[:, :, :],
                                   ends.rearrange("p (a e) -> p a e", a=1).to_broadcast([P, T, E]),
                                   iota_t.rearrange("p (t a) -> p t a", a=1).to_broadcast([P, T, E]),
                                   ALU.is_le))
            link(dve.tensor_reduce(owner_f[:, :], owner[:, :, :], AX.X, ALU.add))
            link(dve.tensor_scalar(b.texp[:, 0:T], owner_f[:, :], float(E - 1), None, ALU.min))
            dve.wait_ge(placed, 1)
            if l == 1:
                dve.wait_ge(act_done, 1)


def experts(nc, b, io, l):
    _, T = routing(l + 1)
    W = HID * (2 - l)
    NOW = 4
    assert T % NOW == 0
    b.used = b.expert_at
    w1 = [b.carve([P, DC, W]) for _ in range(2)]
    w2 = [b.carve([P, MC, D]) for _ in range(2)]
    b1 = [b.carve([P, MC]) for _ in range(2)]
    b2 = [b.carve([1, D]) for _ in range(2)]
    xt = [b.carve([P, D]) for _ in range(2)]
    xT = [b.carve([P, DC, P]) for _ in range(2)]
    gated = [b.carve([P, HID]) for _ in range(2)]
    h = [b.carve([P, MC, P]) for _ in range(2)]
    y = [b.carve([P, D]) for _ in range(2)]
    now = b.carve([1, NOW], u32)
    n = f"e{l}_"
    named, turned, turned_out, up, active, hidden, down, y_out = (
        b.sem(n + x) for x in ("named", "turned", "turned_out", "up", "active", "hidden", "down", "y_out"))
    rows_in, up_in, down_in, stored = (
        [b.sem(f"{n}{x}{k}") for k in range(2)] for x in ("rows_in", "up_in", "down_in", "stored"))
    ND = 1 + 2 * l
    NH = 2
    TURN = b.bank[7]

    with nc.Block() as block:
        @block.gpsimd
        def _(pool):
            def name(t, k):
                pool.tensor_copy(now[0:1, k:k + 1], b.texp[0:1, bass.ds(t, 1)]).then_inc(named, 1)

            def name_next(t, k):
                pool.wait_ge(up, NH * (t - 1))
                name(t, k)

            for k in range(2):
                name(k, k)
            for k in range(2, NOW):
                name_next(k, k)
            with pool.Fori(1, T // NOW) as p:
                for k in range(NOW):
                    name_next(NOW * p + k, k)

        @block.sync
        def _(sp):
            def expert(k):
                return sp.value_load(now[0:1, k % NOW:k % NOW + 1], min_val=0, max_val=E - 1)

            def load_up(t, k):
                sp.wait_ge(named, t + 1)
                sp.dma_start(xt[k % 2], b.xs[l][bass.ds(t * P, P), :]).then_inc(rows_in[k % 2], 16)
                sp.dma_start(w1[k % 2], io[f"w1_{l}"][bass.ds(expert(k), 1)].rearrange("a (c p) n -> p (a c) n", p=P)
                             ).then_inc(up_in[k % 2], 16)

            def load_down(k):
                e = expert(k)
                if l == 1:
                    sp.dma_start(b1[k % 2], io["b1"][bass.ds(e, 1)].rearrange("a p c -> p (a c)")
                                 ).then_inc(down_in[k % 2], 16)
                    sp.dma_start(b2[k % 2], io["b2"][bass.ds(e, 1), :]).then_inc(down_in[k % 2], 16)
                sp.dma_start(w2[k % 2], io[f"w2_{l}"][bass.ds(e, 1)].rearrange("a (c p) n -> p (a c) n", p=P)
                             ).then_inc(down_in[k % 2], 16)

            def store(t, k):
                sp.wait_ge(y_out, t + 1)
                sp.dma_start(b.ys[l][bass.ds(t * P, P), :], y[k % 2]).then_inc(stored[k % 2], 16)

            def advance(t, k):
                load_up(t, k)
                store(t - 3, k - 3)
                load_down(k - 1)

            for k in range(2):
                load_up(k, k)
                load_down(k)
            load_up(2, 2)
            advance(3, 3)
            with sp.Fori(1, T // NOW) as p:
                for k in range(NOW):
                    advance(NOW * p + k, k)
            store(T - 3, T - 3)
            load_down(T - 1)
            for k in range(2):
                store(T - 2 + k, k)
            for k in range(2):
                sp.wait_ge(stored[k], 16 * (T // 2))

        @block.tensor
        def _(pe):
            def turn(t, k, p):
                pe.wait_ge(rows_in[k], 16 * (p + 1))
                if not (isinstance(t, int) and t < 1):
                    pe.wait_ge(turned_out, t)
                for kk in range(DC):
                    mm = pe.transpose(TURN[:, kk * P:(kk + 1) * P], xt[k][:, kk * P:(kk + 1) * P], b.ident[:, :])
                mm.then_inc(turned, 1)

            def up_half(t, k, half):
                for part in range(2 - l):
                    bank = b.bank[half + 2 * part] if l == 0 else b.bank[2 * k + half]
                    for m in range(MC // 2):
                        for kk in range(DC):
                            at = part * HID + (half * MC // 2 + m) * P
                            mm = pe.matmul(bank[:, m * P:(m + 1) * P], w1[k][:, kk, at:at + P], xT[k][:, kk, :],
                                           start=(kk == 0), stop=(kk == DC - 1))
                mm.then_inc(up, 1)

            def rise(t, k, p):
                pe.wait_ge(up_in[k], 16 * (p + 1))
                pe.wait_ge(turned_out, t + 1)
                for half in range(NH):
                    before = 1 if l == 0 else 2
                    if not (isinstance(t, int) and t < before):
                        pe.wait_ge(hidden, NH * (t - before + 1))
                    up_half(t, k, half)

            def fall(t, k, p):
                pe.wait_ge(down_in[k], 16 * ND * (p + 1))
                pe.wait_ge(hidden, NH * (t + 1))
                if not (isinstance(t, int) and t < 2):
                    pe.wait_ge(y_out, t - 1)
                out = b.bank[4 + k]
                for m in range(MC):
                    mm = pe.matmul(out[:, 0:D], h[k][:, m, :], w2[k][:, m, :], start=(m == 0),
                                   stop=(l == 0 and m == MC - 1))
                if l == 1:
                    mm = pe.matmul(out[:, 0:D], b.ones[0:1, :], b2[k], start=False, stop=True)
                mm.then_inc(down, 1)

            def pair(p):
                rise(2 * p + 1, 1, p)
                turn(2 * p + 2, 0, p + 1)
                fall(2 * p, 0, p)
                rise(2 * p + 2, 0, p + 1)
                turn(2 * p + 3, 1, p + 1)
                fall(2 * p + 1, 1, p)

            turn(0, 0, 0)
            rise(0, 0, 0)
            turn(1, 1, 0)
            pair(0)
            with pe.Fori(1, T // 2 - 1) as p:
                pair(p)
            rise(T - 1, 1, T // 2 - 1)
            fall(T - 2, 0, T // 2 - 1)
            fall(T - 1, 1, T // 2 - 1)

        @block.scalar
        def _(act):
            def tile(p, k):
                t = 2 * p + k
                first = isinstance(p, int) and p == 0
                for half in range(NH):
                    act.wait_ge(up, NH * t + half + 1)
                    if l == 0:
                        if not first:
                            act.wait_ge(hidden, NH * (t - 1))
                        act.activation(gated[k][:, half * 512:(half + 1) * 512], b.bank[half][:, :],
                                       ACT.Silu).then_inc(active, 1)
                    else:
                        if not first:
                            act.wait_ge(down, t - 1)
                        act.wait_ge(down_in[k], 16 * ND * (p + 1))
                        for m in range(MC // 2):
                            at = half * MC // 2 + m
                            ins = act.activation(h[k][:, at, :], b.bank[2 * k + half][:, m * P:(m + 1) * P],
                                                 ACT.Gelu, bias=b1[k][:, at:at + 1])
                        ins.then_inc(hidden, 1)

            for k in range(2):
                tile(0, k)
            with act.Fori(1, T // 2) as p:
                for k in range(2):
                    tile(p, k)

        @block.vector
        def _(dve):
            def turn_out(t, k):
                dve.wait_ge(turned, t + 1)
                dve.tensor_copy(xT[k].rearrange("p a q -> p (a q)"), TURN[:, 0:D]).then_inc(turned_out, 1)

            def gate(t, k):
                for half in range(NH):
                    dve.wait_ge(active, NH * t + half + 1)
                    dve.tensor_tensor(h[k].rearrange("p a q -> p (a q)")[:, half * 512:(half + 1) * 512],
                                      gated[k][:, half * 512:(half + 1) * 512], b.bank[2 + half][:, :],
                                      ALU.mult).then_inc(hidden, 1)

            def out(t, k, p):
                dve.wait_ge(down, t + 1)
                dve.wait_ge(stored[k], 16 * p)
                dve.tensor_copy(y[k], b.bank[4 + k][:, 0:D]).then_inc(y_out, 1)

            def step(t, k, turned_next=True):
                if l == 0:
                    gate(t, k)
                if turned_next:
                    turn_out(t + 1, 1 - k)

            turn_out(0, 0)
            step(0, 0)
            step(1, 1)
            out(0, 0, 0)
            step(2, 0)
            out(1, 1, 0)
            with dve.Fori(1, T // 2 - 1) as p:
                step(2 * p + 1, 1)
                out(2 * p, 0, p)
                step(2 * p + 2, 0)
                out(2 * p + 1, 1, p)
            step(T - 1, 1, turned_next=False)
            out(T - 2, 0, T // 2 - 1)
            out(T - 1, 1, T // 2 - 1)


def combine(nc, b, io, l):
    top = l + 1
    NA, _ = routing(top)
    b.used = b.expert_at
    got = b.carve([P, NA, D])
    mixed = b.carve([P, NT, D])
    gamma = b.carve([P, D])
    beta = b.carve([P, D])
    xn = b.carve([P, TC, D])
    n = f"c{l}_"
    s = norm_sems(b, n)
    halved, mixes, loaded, shifted, final, written = (b.sem(n + x) for x in (
        "halved", "mixes", "loaded", "shifted", "final", "written"))
    gathered = [b.sem(f"{n}gathered{c}") for c in range(NCH)]
    with nc.Block() as block:
        @block.gpsimd
        def _(pool):
            for c in range(NCH):
                for t in range(c * TC, (c + 1) * TC):
                    for a in range(t, NA, NT):
                        pool.indirect_dma_start(got[:, a, :], None, b.ys[l][:, :],
                                                bass.IndirectOffsetOnAxis(ap=b.slot[:, a:a + 1], axis=0)
                                                ).then_inc(gathered[c], 16)

        if l == 0:
            @block.vector
            def _(dve):
                for c in range(NCH):
                    dve.wait_ge(gathered[c], 16 * TC * top)
                    for t in range(c * TC, (c + 1) * TC):
                        dve.scalar_tensor_tensor(out=b.x[:, t, :], in0=got[:, t, :], scalar=b.gate[:, 0, t:t + 1],
                                                 in1=b.x[:, t, :], op0=ALU.mult, op1=ALU.add).then_inc(mixes, 1)
                dve.wait_ge(mixes, NT)
            return

        @block.sync
        def _(sp):
            sp.dma_start(gamma, io["gamma"].rearrange("(a n) -> a n", a=1).to_broadcast([P, D])).then_inc(loaded, 16)
            sp.dma_start(beta, io["beta"].rearrange("(a n) -> a n", a=1).to_broadcast([P, D])).then_inc(loaded, 16)
            out = io["out"].rearrange("(t p) d -> p t d", p=P)
            for c in range(NCH):
                sp.wait_ge(final, TC * (c + 1))
                sp.dma_start(out[:, c * TC:(c + 1) * TC, :], b.x[:, c * TC:(c + 1) * TC, :]).then_inc(written, 16)
            sp.wait_ge(written, 16 * NCH)

        @block.scalar
        def _(act):
            act.preload_act_table_set(LN_EXP)
            with act.Fori(0, NCH) as c:
                norm_scalar(act, b, c, s)

        @block.vector
        def _(dve):
            dve.tensor_scalar(b.shared[:, :, :], b.shared[:, :, :], 0.5, None, ALU.mult).then_inc(halved, 1)
            dve.wait_ge(loaded, 32)
            dve.tensor_tensor(b.x[:, :, :], b.x[:, :, :],
                              beta.rearrange("p (a d) -> p a d", a=1).to_broadcast([P, NT, D]), ALU.add
                              ).then_inc(halved, 1)
            dve.wait_ge(halved, 2)
            for c in range(NCH):
                tiles = range(c * TC, (c + 1) * TC)
                dve.wait_ge(gathered[c], 16 * TC * top)
                for r, other in enumerate((b.shared, mixed)):
                    for j, t in enumerate(tiles):
                        if r == 1:
                            dve.wait_ge(mixes, 2 * TC * c + j + 1)
                        dve.scalar_tensor_tensor(out=mixed[:, t, :], in0=got[:, r * NT + t, :],
                                                 scalar=b.gate[:, r, t:t + 1], in1=other[:, t, :], op0=ALU.mult,
                                                 op1=ALU.add).then_inc(mixes, 1)
                dve.wait_ge(mixes, 2 * TC * (c + 1))
                norm_stats(dve, b, c, s, mixed)
                if c >= 1:
                    dve.wait_ge(final, TC * c)
                for j, t in enumerate(tiles):
                    dve.scalar_tensor_tensor(out=xn[:, j, :], in0=mixed[:, t, :], scalar=b.mv[:, j, 0:1],
                                             in1=gamma[:, :], op0=ALU.subtract, op1=ALU.mult).then_inc(shifted, 1)
                for j, t in enumerate(tiles):
                    dve.wait_ge(shifted, TC * c + j + 1)
                    dve.scalar_tensor_tensor(out=b.x[:, t, :], in0=xn[:, j, :], scalar=b.rstd[:, j:j + 1],
                                             in1=b.x[:, t, :], op0=ALU.mult, op1=ALU.add).then_inc(final, 1)


def kernel(**inputs):
    import numpy as _np
    import concourse.bacc as _bacc
    from concourse import mybir as _mybir
    from concourse.bass_utils import run_bass_kernel_spmd as _run

    a = {k: _np.asarray(v) for k, v in inputs.items()}
    arrays = {"x": a["x"][0], "ctxT": a["ctx_1024"][0].T, "mask": a["mask_BxS2_bf1"].view(_np.uint8)}
    for l in range(2):
        for n in "qkvo":
            arrays[f"w{n}T{l}"] = a[f"L{l}_xattn_W{n}"].T
        for n in "qk":
            arrays[f"b{n}{l}"] = a[f"L{l}_xattn_b{n}"].reshape(DC, P).T
        for n in "vo":
            arrays[f"b{n}{l}"] = a[f"L{l}_xattn_b{n}"]
    arrays |= {"gate0": a["L0_ffn_router_w"], "gate_bias": a["L0_ffn_router_b"], "w1_0": a["L0_ffn_w1"],
               "w2_0": a["L0_ffn_w2"], "gate1": a["L1_ffn_gate_W"], "w1_1": a["L1_ffn_W1"],
               "w2_1": a["L1_ffn_W2"], "b1": a["L1_ffn_b1"].reshape(E, MC, P).transpose(0, 2, 1),
               "b2": a["L1_ffn_b2"], "shared_w": a["L1_ffn_shared_W"], "shared_b": a["L1_ffn_shared_b"],
               "gamma": a["L1_ffn_gamma"], "beta": a["L1_ffn_beta"]}
    arrays["iota"] = _np.stack([_np.arange(64), P * _np.arange(64)]).astype(_np.float32)
    arrays["tri"] = _np.triu(_np.ones((P, P), _np.float32), 1)
    kconst = _np.zeros((P, 2), _np.float32)
    rest = _np.float32(FILL)
    for r in range(3):
        part = (_np.array([rest]).view(_np.uint32) & _np.uint32(0xFFFF0000)).view(_np.float32)[0]
        rest = rest - part
        kconst[ROW_MASK + r] = (-part, part)
        kconst[ROW_MAX + r] = (0.0, -1.0)
    arrays["kconst"] = kconst
    arrays["own"] = _np.kron(_np.eye(P // HD), _np.ones((HD, 1))).astype(_np.float32)
    arrays["bk_row"] = a["L0_xattn_bk"].reshape(1, D)
    arrays = {k: _np.ascontiguousarray(v) for k, v in arrays.items()}

    nc = _bacc.Bacc("TRN2", target_bir_lowering=False, num_devices=1)
    io = {k: nc.dram_tensor(f"in_{k}", v.shape, _mybir.dt.from_np(v.dtype), kind="ExternalInput").ap()
          for k, v in arrays.items()}
    io["out"] = nc.dram_tensor("out_x", (S, D), fp32, kind="ExternalOutput").ap()
    build(nc, io)
    r = _run(nc, [{f"in_{k}": v for k, v in arrays.items()}], core_ids=[0])
    return r.results[0]["out_x"].reshape(1, S, D)
```
